# Optimizing a Trainium2 kernel written in Bass

```python
import numpy as np
import jax
import jax.numpy as jnp

def _softmax(x, axis=-1):
    return jax.nn.softmax(x, axis=axis)

def _gelu(x):
    return jax.nn.gelu(x, approximate=True)

def _silu(x):
    return jax.nn.silu(x)

def _sigmoid(x):
    return jax.nn.sigmoid(x)

def _layernorm(x, axis=-1, eps=1e-05):
    m = jnp.mean(x, axis=axis, keepdims=True)
    v = jnp.var(x, axis=axis, keepdims=True)
    return (x - m) / jnp.sqrt(v + eps)

def _scatter_add(tgt, idx, src, axis=0):
    return tgt.at[idx].add(src)

def _segment_sum(src, seg, n):
    return jax.ops.segment_sum(src, seg, n)
kernel_name = 'mk_gnn_preln_d4_gnn_r64_77956e'

def setup_inputs(seed: int=0):
    np.random.seed(seed)
    _w = jnp.asarray

    def _rec_inputs():
        import jax
        import jax.numpy as jnp
        _gk = jax.random.key(seed)
        x = -0.0005121 + 1.001 * jax.random.normal(jax.random.fold_in(_gk, 1), (100000, 32), jnp.float32)
        src = jax.random.randint(jax.random.fold_in(_gk, 2), (25000,), 0, 100000, jnp.int32)
        dst = jax.random.randint(jax.random.fold_in(_gk, 3), (25000,), 0, 100000, jnp.int32)
        _o = jnp.argsort(dst, stable=True)
        src = src[_o]
        dst = dst[_o]
        edge_attr_16 = -0.00019784 + 0.999804 * jax.random.normal(jax.random.fold_in(_gk, 12), (25000, 16), jnp.float32)
        edge_weight = jax.random.uniform(jax.random.fold_in(_gk, 15), (25000,), jnp.float32, 0.0, 1)
        return (x, src, dst, edge_attr_16, edge_weight)
    x, src, dst, edge_attr_16, edge_weight = _rec_inputs()

    def _L0_gnn_setup():
        import jax, jax.numpy as jnp
        import numpy as np
        N_ATOMS = 100000
        N_EDGES = 6250
        ATOM_DIM = 32
        BOND_DIM = 16
        key = jax.random.key(seed)
        k1, k2, k3, k4 = jax.random.split(key, 4)
        atom_features = jax.random.normal(k1, (N_ATOMS, ATOM_DIM), dtype=jnp.float32)
        bond_features = jax.random.normal(k2, (N_EDGES, BOND_DIM), dtype=jnp.float32)
        pair_indices = jax.random.randint(k3, (N_EDGES, 2), 0, N_ATOMS, dtype=jnp.int64)
        limit = np.sqrt(6.0 / (BOND_DIM + ATOM_DIM * ATOM_DIM)).astype(np.float32)
        kernel = jax.random.uniform(k4, (BOND_DIM, ATOM_DIM * ATOM_DIM), dtype=jnp.float32, minval=-limit, maxval=limit)
        bias = jnp.zeros((ATOM_DIM * ATOM_DIM,), dtype=jnp.float32)
        return {'atom_features': atom_features, 'bond_features': bond_features, 'pair_indices': pair_indices, 'kernel': kernel, 'bias': bias}
    _L0_gnn_all = _L0_gnn_setup()
    _L0_gnn_in = {k: v for k, v in _L0_gnn_all.items() if k in ('kernel', 'bias')}
    del _L0_gnn_all

    def _L1_gnn_setup():
        import jax, jax.numpy as jnp
        import numpy as np
        N_NODES = 50000
        N_EDGES = 12500
        C_IN = 32
        C_OUT = 32
        BN_EPS = 1e-05

        def batch_norm(h, gamma, beta):
            mean = jnp.mean(h, axis=0)
            var = jnp.mean((h - mean) ** 2, axis=0)
            return (h - mean) * jax.lax.rsqrt(var + BN_EPS) * gamma + beta
        key = jax.random.key(seed)
        ks = jax.random.split(key, 8)
        x = jax.random.normal(ks[0], (N_NODES, C_IN), dtype=jnp.float32)
        edge_index = jax.random.randint(ks[1], (2, N_EDGES), 0, N_NODES, dtype=jnp.int64)
        s1 = 1.0 / np.sqrt(2 * C_IN)
        s2 = 1.0 / np.sqrt(C_OUT)
        W1 = jax.random.uniform(ks[2], (2 * C_IN, C_OUT), jnp.float32, -s1, s1)
        b1 = jax.random.uniform(ks[3], (C_OUT,), jnp.float32, -s1, s1)
        W2 = jax.random.uniform(ks[4], (C_OUT, C_OUT), jnp.float32, -s2, s2)
        b2 = jax.random.uniform(ks[5], (C_OUT,), jnp.float32, -s2, s2)
        gamma1 = jnp.ones((C_OUT,), jnp.float32)
        beta1 = jnp.zeros((C_OUT,), jnp.float32)
        gamma2 = jnp.ones((C_OUT,), jnp.float32)
        beta2 = jnp.zeros((C_OUT,), jnp.float32)
        return {'x': x, 'W1': W1, 'b1': b1, 'gamma1': gamma1, 'beta1': beta1, 'W2': W2, 'b2': b2, 'gamma2': gamma2, 'beta2': beta2, 'edge_index': edge_index}
    _L1_gnn_all = _L1_gnn_setup()
    _L1_gnn_in = {k: v for k, v in _L1_gnn_all.items() if k in ('W1', 'b1', 'gamma1', 'beta1', 'W2', 'b2', 'gamma2', 'beta2')}
    del _L1_gnn_all

    def _L2_gnn_setup():
        import jax, jax.numpy as jnp
        import numpy as np
        N_NODES = 100000
        N_EDGES = 25000
        EMB_DIM = 32
        NUM_LAYERS = 3
        key = jax.random.key(seed)
        k_emb, k_w, k_row, k_col = jax.random.split(key, 4)
        emb = jax.random.normal(k_emb, (N_NODES, EMB_DIM), dtype=jnp.float32)
        edge_weight = jax.random.uniform(k_w, (N_EDGES,), dtype=jnp.float32)
        row = jax.random.randint(k_row, (N_EDGES,), 0, N_NODES, dtype=jnp.int32)
        col = jax.random.randint(k_col, (N_EDGES,), 0, N_NODES, dtype=jnp.int32)
        return {'emb': emb, 'edge_weight': edge_weight, 'row': row, 'col': col, 'num_layers': NUM_LAYERS}
    _L2_gnn_all = _L2_gnn_setup()
    _L2_gnn_in = {k: v for k, v in _L2_gnn_all.items() if k in ()}
    del _L2_gnn_all

    def _L3_gnn_setup():
        import jax, jax.numpy as jnp
        import numpy as np
        N_NODES = 100000
        N_EDGES = 25000
        D = 32
        H = 2 * D
        EPS = 1e-07

        def _edge_softmax(logits, dst, num_nodes):
            m = jax.ops.segment_max(logits, dst, num_segments=num_nodes)
            e = jnp.exp(logits - m[dst])
            s = jax.ops.segment_sum(e, dst, num_segments=num_nodes)
            return e / s[dst]
        key = jax.random.key(seed)
        ks = jax.random.split(key, 6)
        x = jax.random.normal(ks[0], (N_NODES, D), dtype=jnp.float32)
        edge_index = jax.random.randint(ks[1], (2, N_EDGES), 0, N_NODES, dtype=jnp.int64)
        beta = jnp.ones((1,), dtype=jnp.float32)
        W1 = jax.random.normal(ks[2], (D, H), dtype=jnp.float32) * (1.0 / np.sqrt(D))
        b1 = jnp.zeros((H,), dtype=jnp.float32)
        W2 = jax.random.normal(ks[3], (H, D), dtype=jnp.float32) * (1.0 / np.sqrt(H))
        b2 = jnp.zeros((D,), dtype=jnp.float32)
        return {'x': x, 'edge_index': edge_index, 'beta': beta, 'W1': W1, 'b1': b1, 'W2': W2, 'b2': b2}
    _L3_gnn_all = _L3_gnn_setup()
    _L3_gnn_in = {k: v for k, v in _L3_gnn_all.items() if k in ('beta', 'W1', 'b1', 'W2', 'b2')}
    del _L3_gnn_all
    return {'x': x, 'src': src, 'dst': dst, 'edge_attr_16': edge_attr_16, 'edge_weight': edge_weight, 'L0_gnn_kernel': _L0_gnn_in['kernel'], 'L0_gnn_bias': _L0_gnn_in['bias'], 'L1_gnn_W1': _L1_gnn_in['W1'], 'L1_gnn_b1': _L1_gnn_in['b1'], 'L1_gnn_gamma1': _L1_gnn_in['gamma1'], 'L1_gnn_beta1': _L1_gnn_in['beta1'], 'L1_gnn_W2': _L1_gnn_in['W2'], 'L1_gnn_b2': _L1_gnn_in['b2'], 'L1_gnn_gamma2': _L1_gnn_in['gamma2'], 'L1_gnn_beta2': _L1_gnn_in['beta2'], 'L3_gnn_beta': _L3_gnn_in['beta'], 'L3_gnn_W1': _L3_gnn_in['W1'], 'L3_gnn_b1': _L3_gnn_in['b1'], 'L3_gnn_W2': _L3_gnn_in['W2'], 'L3_gnn_b2': _L3_gnn_in['b2']}

def reference(x, src, dst, edge_attr_16, edge_weight, L0_gnn_kernel, L0_gnn_bias, L1_gnn_W1, L1_gnn_b1, L1_gnn_gamma1, L1_gnn_beta1, L1_gnn_W2, L1_gnn_b2, L1_gnn_gamma2, L1_gnn_beta2, L3_gnn_beta, L3_gnn_W1, L3_gnn_b1, L3_gnn_W2, L3_gnn_b2):
    import jax
    import jax.numpy as jnp

    def _L0_gnn_ref(atom_features, bond_features, pair_indices, kernel, bias):
        import jax, jax.numpy as jnp
        import numpy as np
        N_ATOMS = 100000
        N_EDGES = 6250
        ATOM_DIM = 32
        BOND_DIM = 16
        n_atoms, d = atom_features.shape
        e = bond_features.shape[0]
        edge_mats = (bond_features @ kernel + bias).reshape(e, d, d)
        neighbors = atom_features[pair_indices[:, 1]]
        transformed = jnp.einsum('eij,ej->ei', edge_mats, neighbors)
        return jax.ops.segment_sum(transformed, pair_indices[:, 0], num_segments=n_atoms)

    def _L1_gnn_ref(x, W1, b1, gamma1, beta1, W2, b2, gamma2, beta2, edge_index):
        import jax, jax.numpy as jnp
        import numpy as np
        N_NODES = 50000
        N_EDGES = 12500
        C_IN = 32
        C_OUT = 32
        BN_EPS = 1e-05

        def batch_norm(h, gamma, beta):
            mean = jnp.mean(h, axis=0)
            var = jnp.mean((h - mean) ** 2, axis=0)
            return (h - mean) * jax.lax.rsqrt(var + BN_EPS) * gamma + beta
        row, col = (edge_index[0], edge_index[1])
        ef = jnp.concatenate([x[row], x[col]], axis=-1)
        h = jax.nn.relu(batch_norm(ef @ W1 + b1, gamma1, beta1))
        h = jax.nn.relu(batch_norm(h @ W2 + b2, gamma2, beta2))
        out = jax.ops.segment_sum(h, row, num_segments=x.shape[0])
        return out

    def _L2_gnn_ref(emb, edge_weight, row, col, num_layers):
        import jax, jax.numpy as jnp
        import numpy as np
        N_NODES = 100000
        N_EDGES = 25000
        EMB_DIM = 32
        NUM_LAYERS = 3
        n = emb.shape[0]
        w = edge_weight[:, None]
        X = emb
        for _ in range(num_layers):
            msgs = w * X[col]
            X = jax.ops.segment_sum(msgs, row, num_segments=n)
        return X

    def _L3_gnn_ref(x, edge_index, beta, W1, b1, W2, b2):
        import jax, jax.numpy as jnp
        import numpy as np
        N_NODES = 100000
        N_EDGES = 25000
        D = 32
        H = 2 * D
        EPS = 1e-07

        def _edge_softmax(logits, dst, num_nodes):
            m = jax.ops.segment_max(logits, dst, num_segments=num_nodes)
            e = jnp.exp(logits - m[dst])
            s = jax.ops.segment_sum(e, dst, num_segments=num_nodes)
            return e / s[dst]
        n = x.shape[0]
        dst = edge_index[0]
        src = edge_index[1]
        edge_msg = jax.nn.relu(x[src]) + EPS
        alpha = _edge_softmax(beta * edge_msg, dst, n)
        h = jax.ops.segment_sum(edge_msg * alpha, dst, num_segments=n)
        h = jax.nn.relu(h @ W1 + b1) @ W2 + b2
        return h
    edge_index = jnp.stack([src, dst])
    edge_index_t = jnp.stack([src, dst], axis=1)
    h = jnp.maximum(_layernorm(x, axis=-1), 0.0)
    x = x + _L0_gnn_ref(h, edge_attr_16, edge_index_t, L0_gnn_kernel, L0_gnn_bias)
    h = jnp.maximum(_layernorm(x, axis=-1), 0.0)
    x = x + _L1_gnn_ref(h, L1_gnn_W1, L1_gnn_b1, L1_gnn_gamma1, L1_gnn_beta1, L1_gnn_W2, L1_gnn_b2, L1_gnn_gamma2, L1_gnn_beta2, edge_index)
    h = jnp.maximum(_layernorm(x, axis=-1), 0.0)
    x = x + _L2_gnn_ref(h, edge_weight, src, dst, 3)
    h = jnp.maximum(_layernorm(x, axis=-1), 0.0)
    x = x + _L3_gnn_ref(h, edge_index, L3_gnn_beta, L3_gnn_W1, L3_gnn_b1, L3_gnn_W2, L3_gnn_b2)
    return x

_drawn_inputs = setup_inputs


def setup_inputs(seed=0):
    import zlib

    import numpy as np

    out = dict(_drawn_inputs(seed))
    spreads = {'L0_gnn_bias': (0.0, 0.1),
     'L1_gnn_gamma1': (1.0, 0.2),
     'L1_gnn_beta1': (0.0, 0.279),
     'L1_gnn_gamma2': (1.0, 0.2),
     'L1_gnn_beta2': (0.0, 0.1),
     'L3_gnn_b1': (0.0, 0.33),
     'L3_gnn_b2': (0.0, 0.1)}
    factors = {'edge_weight': 5.184, 'L1_gnn_b1': 64.0, 'L1_gnn_b2': 64.0}
    for name, (base, spread) in spreads.items():
        noise = np.random.default_rng([zlib.crc32(name.encode()), seed]).standard_normal(out[name].shape)
        drawn = base * np.exp(spread * noise) if base else spread * noise
        out[name] = jnp.asarray(drawn.astype(out[name].dtype))
    for name, factor in factors.items():
        out[name] = (out[name] * factor).astype(out[name].dtype)
    return out
```

```python
import concourse.bass as bass
from concourse import mybir
from contextlib import ExitStack

FP32 = mybir.dt.float32
I32 = mybir.dt.int32
ALU = mybir.AluOpType
ACT = mybir.ActivationFunctionType
AX = mybir.AxisListType

P = 128
D = 32
BOND = 16
H2 = 2 * D
LN_EPS = 1e-05
BN_EPS = 1e-05
MSG_EPS = 1e-07
BIG = 1e38
NOWHERE = 1 << 20


def gnn(nc, x, src, dst, attr, weight, bond_k, bond_b, w1a, b1a, g1a, be1a, w1b, b1b, g1b, be1b,
        beta3, w3a, b3a, w3b, b3b, out):
    NODES = x.shape[0]
    EDGES = src.shape[0]
    TILES = -(-EDGES // (P * 4)) * 4
    SLOTS = P * TILES
    QUADS = TILES // 4
    FULL_P = EDGES // TILES
    REST = EDGES - FULL_P * TILES
    assert FULL_P == P - 1 and 0 < REST < TILES
    SORT_C = 256
    SORT_N = P * SORT_C
    ID_BITS = SORT_N.bit_length() - 1
    HALF = NODES // 2
    LIFT = 1 << (23 - ID_BITS)
    CH = 4
    CT = TILES // CH
    ROW = 20
    LAST_N = -(-NODES // P) * P
    XROWS = 71
    XCH = (NODES // P) // XROWS
    assert XCH * XROWS == NODES // P
    XLEFT = NODES - P * XCH * XROWS
    LOOP = 8
    LOOPS = QUADS // LOOP
    assert LOOPS * LOOP == QUADS - 1

    ctx = ExitStack()
    with ctx:
        def sb(name, shape, dt=FP32):
            return ctx.enter_context(nc.sbuf_tensor(name, shape, dt))

        def pb(name, shape, dt=FP32):
            return ctx.enter_context(nc.psum_tensor(name, shape, dt))

        def sem(name):
            return ctx.enter_context(nc.semaphore(name))

        def dram(name, shape, dt=FP32):
            return nc.dram_tensor(name, shape, dt, kind="Internal").ap()

        sorted_keys = dram("sorted_keys", (SORT_N + 2,))
        edge_rows = dram("edge_rows", (SLOTS, ROW))
        last_slot = dram("last_slot", (LAST_N, 1), I32)
        tables = [dram(f"table{n}", (SLOTS, D)) for n in range(5)]

        x_src = sb("x_src", [P, TILES, D])
        x_dst = sb("x_dst", [P, TILES, D])
        buf_a = sb("buf_a", [P, TILES, D])
        buf_b = sb("buf_b", [P, TILES, D])
        buf_c = sb("buf_c", [P, TILES, D])
        rows = sb("rows", [P, TILES, ROW])
        rows_i = rows[:, :, :].bitcast(I32)
        packed = buf_a[:, :, :].rearrange("p t d -> p (t d)")[:, 0:TILES * ROW].rearrange(
            "p (t r) -> p t r", r=ROW)
        packed_i = packed.bitcast(I32)
        attr_in = buf_b[:, :, 0:BOND]

        key_a = sb("key_a", [P, SORT_C])
        key_b = sb("key_b", [P, SORT_C])
        key_i = sb("key_i", [P, SORT_C], I32)
        key_t = sb("key_t", [P, SORT_C], I32)
        edge_id = sb("edge_id", [P, SORT_C], I32)
        col_i = sb("col_i", [P, SORT_C], I32)
        part_i = sb("part_i", [P, 1], I32)
        part_t = sb("part_t", [P, 1], I32)
        COL_LEVELS = SORT_C.bit_length() - 2
        PART_LEVELS = ID_BITS - COL_LEVELS - 1
        PART_TURNS = P.bit_length() - 1
        sign_col = sb("sign_col", [P, COL_LEVELS, SORT_C])
        sign_part = sb("sign_part", [P, PART_LEVELS])
        zero1 = sb("zero1", [1, 1])

        key_here = sb("key_here", [P, TILES])
        key_prev = sb("key_prev", [P, TILES])
        key_next = sb("key_next", [P, TILES])
        row_index = sb("row_index", [P, TILES], I32)
        src_index = sb("src_index", [P, TILES], I32)
        dst_index = sb("dst_index", [P, TILES], I32)
        tail_index = sb("tail_index", [P, TILES], I32)
        slot_id = sb("slot_id", [P, TILES], I32)
        dst_last = sb("dst_last", [P, TILES], I32)
        weight_s = sb("weight_s", [P, TILES])
        goes_on = sb("goes_on", [P, TILES])
        goes_on_neg = sb("goes_on_neg", [P, TILES])
        not_tail = sb("not_tail", [P, TILES])
        is_tail = sb("is_tail", [P, TILES])
        from_prev = sb("from_prev", [P, TILES])
        from_prev_neg = sb("from_prev_neg", [P, TILES])
        from_next = sb("from_next", [P, TILES])
        whole = sb("whole", [D, P])
        whole_neg = sb("whole_neg", [D, P])
        whole_next = sb("whole_next", [D, P])
        wide = sb("wide", [P, D])
        carry_t = sb("carry_t", [D, P + 1])
        carry = sb("carry", [P, D])
        mean = sb("mean", [P, TILES])
        var = sb("var", [P, TILES])
        eps_c = sb("eps_c", [P, 1])

        ident = sb("ident", [P, P])
        ones = sb("ones", [P, P])
        ones_full = sb("ones_full", [P, P])
        bond_w = sb("bond_w", [P, BOND * D])
        bond_bd = sb("bond_bd", [P, P])
        w1s_bd = sb("w1s_bd", [P, P])
        w1d_bd = sb("w1d_bd", [P, P])
        w2_bd = sb("w2_bd", [P, P])
        b1_row = sb("b1_row", [1, P])
        b2_row = sb("b2_row", [1, P])
        bn_par = sb("bn_par", [P, 4, D])
        beta_c = sb("beta_c", [P, 1])
        w3a_bd = sb("w3a_bd", [P, P])
        w3b_bd = sb("w3b_bd", [P, H2])
        b3a_c = sb("b3a_c", [P, 1])
        b3b_row = sb("b3b_row", [1, P])
        rb3a = sb("rb3a", [H2, 1])
        rb3a_w = sb("rb3a_w", [H2, P])
        idle_row = sb("idle_row", [P, D])
        sums = sb("sums", [P, 2, D])
        bn_mean = sb("bn_mean", [P, D])
        bn_scale = sb("bn_scale", [P, D])
        w_t = [sb(f"w_t{n}", [P, 2, P]) for n in range(2)]
        r_t = [sb(f"r_t{n}", [P, 2, P]) for n in range(2)]
        prod = sb("prod", [P, 2, BOND * D])
        x_ring = [sb(f"x_ring{n}", [P, XROWS * D]) for n in range(2)]

        ps_t = [pb(f"ps_t{n}", [P, 4, P]) for n in range(2)]
        ps_u = [pb(f"ps_u{n}", [P, 2, BOND * D]) for n in range(2)]
        ps_o = [pb(f"ps_o{n}", [P, 4, P]) for n in range(2)]
        ps_key = ps_t[0][:, 0:2, :].rearrange("p a b -> p (a b)")
        ps_small = ps_t[1][:, 0, :]

        key_pair = (key_a, key_b)
        moves, key_turned = 0, []
        for level in range(1, ID_BITS + 1):
            moves += level < ID_BITS
            crossing = max(0, level - (SORT_C.bit_length() - 1))
            if crossing:
                key_turned += [key_pair[moves % 2], key_pair[(moves + 1 + crossing) % 2]]
                moves += 2
            moves += level + (level < ID_BITS)
        key_sorted = key_pair[moves % 2]

        weight_loads = [(bn_par[:, n, :], p.partition_broadcast(P)) for n, p in enumerate((g1a, be1a, g1b, be1b))]
        weight_loads.append((beta_c[:, :], beta3.partition_broadcast(P)))
        for t in range(4):
            r = slice(32 * t, 32 * t + 32)
            weight_loads += [
                (bond_w[r, :], bond_k), (bond_bd[r, r], bond_b), (w1s_bd[r, r], w1a[0:D, :]),
                (w1d_bd[r, r], w1a[D:2 * D, :]), (w2_bd[r, r], w1b), (b1_row[0:1, r], b1a.unsqueeze(0)),
                (b2_row[0:1, r], b1b.unsqueeze(0)), (b3b_row[0:1, r], b3b.unsqueeze(0)),
                (w3a_bd[r, H2 * (t % 2):H2 * (t % 2) + H2], w3a)]
        for t in range(2):
            r = slice(H2 * t, H2 * t + H2)
            weight_loads += [(w3b_bd[r, D * t:D * t + D], w3b), (b3a_c[r, :], b3a.unsqueeze(1))]

        iotas = sem("iotas")
        ident_made = sem("ident_made")
        keys_blank = sem("keys_blank")
        src_in = sem("src_in")
        edges_blank = sem("edges_blank")
        edges_in = sem("edges_in")
        packed_done = sem("packed_done")
        rows_stored = sem("rows_stored")
        weights_in = sem("weights_in")
        blocks_blank = sem("blocks_blank")
        dve_step = sem("dve_step")
        bond_step = sem("bond_step")
        to_pe = sem("to_pe")
        from_pe = sem("from_pe")
        sorted_done = sem("sorted_done")
        sorted_stored = sem("sorted_stored")
        keys_back = sem("keys_back")
        src_known = sem("src_known")
        last_blank = sem("last_blank")
        last_filled = sem("last_filled")
        x_blank = sem("x_blank")
        got_rows = sem("got_rows")
        dst_known = sem("dst_known")
        got_dst = [sem(f"got_dst{c}") for c in range(CH)]
        got_xs = sem("got_xs")
        last_written = sem("last_written")
        got_last = sem("got_last")
        state_made = sem("state_made")
        state_stored = sem("state_stored")
        centred = sem("centred")
        squared = sem("squared")
        root_ready = sem("root_ready")
        rooted = sem("rooted")
        input_ready = sem("input_ready")
        turned = sem("turned")
        copied = sem("copied")
        bond_mm = sem("bond_mm")
        lin_mm = sem("lin_mm")
        lin_used = sem("lin_used")
        hid_mm = sem("hid_mm")
        hid_done = sem("hid_done")
        exp_ready = sem("exp_ready")
        exp_done = sem("exp_done")
        x_loaded = [sem(f"x_loaded{n}") for n in range(2)]
        x_added = sem("x_added")
        x_stored = [sem(f"x_stored{n}") for n in range(2)]
        out_rows = sem("out_rows")
        final_made = sem("final_made")

        block = ctx.enter_context(nc.Block())

        STEPS = 5
        STATES = 5

        def first_then_second(eng, first, second):
            if eng is None:
                for q in range(QUADS + 1):
                    if q < QUADS:
                        first(q, q % 2)
                    if q and (q % LOOP or q == QUADS):
                        second(q - 1, (q - 1) % 2)
                    elif q:
                        second(q - 1, (q - 1) % 2)
                return
            with eng.Fori(0, LOOPS) as i:
                for j in range(LOOP + 1):
                    if j < LOOP:
                        first(i * LOOP + j, j % 2)
                    if j:
                        second(i * LOOP + j - 1, (j - 1) % 2)
            first(QUADS - 1, (QUADS - 1) % 2)
            second(QUADS - 1, (QUADS - 1) % 2)

        def quad(buf, q):
            return buf[:, bass.ds(q * 4, 4), :].rearrange("p t d -> p (t d)")

        def chunk(buf, c):
            return buf[:, c * CT:(c + 1) * CT]

        def bcast(a, n):
            return a.unsqueeze(len(a.shape)).to_broadcast(list(a.shape) + [n])

        NORMS = [(buf_a, buf_b, var[:, :], D), (buf_a, buf_c, var[:, :], D), (buf_b, buf_c, var[:, :], D),
                 (buf_c, buf_b, bn_scale[:, :], EDGES), (buf_c, buf_b, bn_scale[:, :], EDGES),
                 (buf_a, buf_b, var[:, :], D), (buf_a, buf_b, var[:, :], D)]

        @block.sync
        def _(sp):
            def by_edge(to, of):
                full = FULL_P * TILES
                yield sp.dma_start(to[0:FULL_P, 0:TILES], of[0:full].rearrange("(p t) k -> p t k", t=TILES))
                yield sp.dma_start(to[FULL_P:P, 0:REST], of[full:EDGES].unsqueeze(0))

            sp.wait_ge(keys_blank, 1)
            for load in by_edge(key_i[:, :].unsqueeze(2), src.unsqueeze(1)):
                load.then_inc(src_in, 16)
            sp.wait_ge(edges_blank, 1)
            for to, of in ((attr_in, attr), (key_prev[:, :].unsqueeze(2), weight.unsqueeze(1)),
                           (dst_index[:, :].unsqueeze(2), dst.unsqueeze(1))):
                for load in by_edge(to, of):
                    load.then_inc(edges_in, 16)
            sp.wait_ge(last_blank, 1)
            sp.dma_start(last_slot[:, 0].rearrange("(p t) -> p t", p=P),
                         buf_c[:, :, :].bitcast(I32).rearrange("p t d -> p (t d)")[:, 0:LAST_N // P])\
                .then_inc(last_filled, 16)
            sp.wait_ge(packed_done, 1)
            sp.dma_start(edge_rows.rearrange("(p t) r -> p t r", p=P), packed).then_inc(rows_stored, 16)
            sp.dma_start(sorted_keys[0:1].unsqueeze(0), zero1[:, :]).then_inc(sorted_stored, 16)
            sp.wait_ge(sorted_done, 1)
            sp.dma_start(sorted_keys[1:1 + SORT_N].rearrange("(p t) -> p t", p=P), key_sorted[:, :])\
                .then_inc(sorted_stored, 16)
            sp.wait_ge(sorted_stored, 32)
            for to, off in ((key_here, 1), (key_prev, 0), (key_next, 2)):
                sp.dma_start(to[:, :], sorted_keys[off:off + SLOTS].rearrange("(p t) -> p t", p=P))\
                    .then_inc(keys_back, 16)
            for n, buf in enumerate((x_src, x_src, buf_c, buf_c, x_src)):
                sp.wait_ge(state_made, n + 1)
                sp.dma_start(tables[n].rearrange("(p t) d -> p t d", p=P), buf[:, :, :])\
                    .then_inc(state_stored, 16)
            sp.wait_ge(state_stored, 16 * STATES)

        @block.scalar
        def _(act):
            act.wait_ge(blocks_blank, 1)
            for to, of in weight_loads:
                act.dma_start(to, of).then_inc(weights_in, 16)

            def x_rows(t, c):
                return t[0:P * XCH * XROWS, :].rearrange("(p c r) d -> c p (r d)", c=XCH, r=XROWS)[c]

            def load(c):
                if c >= 2:
                    act.wait_ge(x_stored[c % 2], 16 * (c // 2))
                act.dma_start(x_ring[c % 2][:, :], x_rows(x, c)).then_inc(x_loaded[c % 2], 16)

            load(0)
            for c in range(XCH):
                if c + 1 < XCH:
                    load(c + 1)
                act.wait_ge(x_added, c + 1)
                act.dma_start(x_rows(out, c), x_ring[c % 2][:, :]).then_inc(x_stored[c % 2], 16)
            left = x_ring[XCH % 2][0:XLEFT, 0:D]
            act.wait_ge(x_stored[XCH % 2], 16 * (XCH // 2))
            act.dma_start(left, x[P * XCH * XROWS:NODES, :]).then_inc(x_loaded[XCH % 2], 16)
            act.wait_ge(x_added, XCH + 1)
            act.dma_start(out[P * XCH * XROWS:NODES, :], left).then_inc(x_stored[XCH % 2], 16)

            def norm(k):
                of, to, root, count = NORMS[k]
                for c in range(CH):
                    act.wait_ge(centred, k * CH + c + 1)
                    act.activation(chunk(to, c), chunk(of, c), ACT.Square).then_inc(squared, 1)
                act.wait_ge(root_ready, k + 1)
                act.activation(root, root, ACT.Sqrt, bias=eps_c[:, :], scale=1.0 / count).then_inc(rooted, 1)

            def copy_turned(stage, blocks):
                def copy(q, s):
                    act.wait_ge(turned, stage * QUADS + q + 1)
                    act.wait_ge(lin_mm, stage * QUADS + q + 1)
                    act.activation(w_t[s][:, 0:blocks, :], ps_t[s][:, 0:blocks, :], ACT.Copy)\
                        .then_inc(copied, 1)
                return copy

            def take(stage):
                def move(q, s):
                    act.wait_ge(lin_mm, stage * QUADS + q + 3)
                    act.activation(quad(buf_c, q), ps_o[s][:, 0, :], ACT.Copy).then_inc(lin_used, 1)
                return move

            def hidden(q, s):
                act.wait_ge(hid_mm, q + 1)
                act.wait_ge(lin_mm, 3 * QUADS + q + 1)
                act.activation(r_t[s][:, :, :], ps_u[s][:, :, 0:P], ACT.Relu, bias=b3a_c[:, :])\
                    .then_inc(hid_done, 1)

            act.sem_inc(copied, 2)
            act.sem_inc(hid_done, 2)
            norm(0)
            first_then_second(act, copy_turned(0, 1), lambda q, s: None)
            norm(1)
            norm(2)
            first_then_second(act, copy_turned(1, 2), take(1))
            norm(3)
            first_then_second(act, copy_turned(2, 1), take(2))
            norm(4)
            norm(5)
            norm(6)
            act.wait_ge(exp_ready, 1)
            act.activation(buf_b[:, :, :], buf_b[:, :, :], ACT.Exp).then_inc(exp_done, 1)
            first_then_second(act, copy_turned(3, 1), hidden)

        @block.gpsimd
        def _(gp):
            gp.iota(edge_id[:, 0:TILES], pattern=[[1, TILES]], base=0, channel_multiplier=TILES)\
                .then_inc(iotas, 1)
            gp.iota(edge_id[:, TILES:SORT_C], pattern=[[1, SORT_C - TILES]], base=SLOTS,
                    channel_multiplier=SORT_C - TILES).then_inc(iotas, 1)
            gp.iota(slot_id[:, :], pattern=[[1, TILES]], base=0, channel_multiplier=TILES).then_inc(iotas, 1)
            gp.iota(col_i[:, :], pattern=[[1, SORT_C]], base=0, channel_multiplier=0).then_inc(iotas, 1)
            gp.iota(part_i[:, :], pattern=[[1, 1]], base=0, channel_multiplier=1).then_inc(iotas, 1)
            gp.memset(ident[:, :], 0.0).then_inc(ident_made, 1)
            gp.memset(ones_full[:, :], 1.0).then_inc(ident_made, 1)
            gp.wait_ge(ident_made, 2)
            gp.affine_select(out=ident[:, :], in_=ident[:, :], compare_op=ALU.not_equal, fill=1.0, base=0,
                             pattern=[[-1, P]], channel_multiplier=1).then_inc(ident_made, 1)
            gp.affine_select(out=ones_full[:, :], in_=ones_full[:, :], compare_op=ALU.is_gt, fill=0.0,
                             base=FULL_P, pattern=[[0, P]], channel_multiplier=-1).then_inc(ident_made, 1)

            def gather(to, table, index, t, signal):
                gp.indirect_dma_start(out=to, out_offset=None, in_=table,
                                      in_offset=bass.IndirectOffsetOnAxis(ap=index[:, t:t + 1], axis=0),
                                      bounds_check=min(table.shape[0], NODES) - 1,
                                      oob_is_err=False).then_inc(signal, 16)

            def scatter(table, index, of, t, signal):
                gp.indirect_dma_start(out=table, in_=of, in_offset=None,
                                      out_offset=bass.IndirectOffsetOnAxis(ap=index[:, t:t + 1], axis=0),
                                      bounds_check=NODES - 1, oob_is_err=False).then_inc(signal, 16)

            gp.wait_ge(rows_stored, 16)
            gp.wait_ge(src_known, 1)
            for t in range(TILES):
                gather(rows[:, t, :], edge_rows, row_index, t, got_rows)
            gp.wait_ge(dst_known, 1)
            for t in range(TILES):
                gather(x_dst[:, t, :], x, dst_index, t, got_dst[t // CT])
            gp.wait_ge(x_blank, 1)
            for t in range(TILES):
                gather(x_src[:, t, :], x, src_index, t, got_xs)
            gp.wait_ge(last_filled, 16)
            for t in range(TILES):
                scatter(last_slot, tail_index, slot_id[:, t:t + 1], t, last_written)
            gp.wait_ge(last_written, 16 * TILES)
            for t in range(TILES):
                gather(dst_last[:, t:t + 1], last_slot, dst_index, t, got_last)
            gp.wait_ge(got_last, 16 * TILES)
            for n, buf in enumerate((x_dst, x_dst, buf_b, buf_b, x_dst)):
                gp.wait_ge(state_stored, 16 * (n + 1))
                for t in range(TILES):
                    gather(buf[:, t, :], tables[n], dst_last, t, got_dst[t // CT])
            gp.wait_ge(x_stored[0], 16 * (XCH // 2 + (XCH % 2)  + (1 - XCH % 2)))
            gp.wait_ge(x_stored[1], 16 * (XCH // 2 + XCH % 2))
            gp.wait_ge(final_made, 1)
            for t in range(TILES):
                scatter(out, tail_index, x_src[:, t, :], t, out_rows)
            gp.wait_ge(out_rows, 16 * TILES)

        @block.vector
        def _(v):
            steps = [0]

            def step(ins):
                steps[0] += 1
                ins.then_inc(dve_step, 1)

            def settle():
                v.wait_ge(dve_step, steps[0])

            def link(ins):
                step(ins)
                settle()

            small = [0]

            def pe_does():
                small[0] += 1
                v.sem_inc(to_pe, 1)
                v.wait_ge(from_pe, small[0])

            def over_t(a, n):
                return a.unsqueeze(1).to_broadcast([P, n, D])

            link(v.memset(key_i[:, :], NODES))
            v.sem_inc(keys_blank, 1)
            step(v.memset(attr_in, 0.0))
            step(v.memset(key_prev[:, :], 0.0))
            step(v.memset(dst_index[:, :], 0))
            step(v.memset(packed, 0.0))
            settle()
            v.sem_inc(edges_blank, 1)
            step(v.memset(buf_c[:, :, :].bitcast(I32), NOWHERE))
            step(v.memset(zero1[:, :], 0.0))
            step(v.memset(ones[:, :], 1.0))
            step(v.memset(eps_c[:, :], LN_EPS))
            step(v.memset(x_src[:, :, :], 0.0))
            for t in (bond_bd, w1s_bd, w1d_bd, w2_bd, w3a_bd, w3b_bd):
                step(v.memset(t[:, :], 0.0))
            settle()
            v.sem_inc(last_blank, 1)
            v.sem_inc(x_blank, 1)
            v.sem_inc(blocks_blank, 1)
            v.sem_inc(bond_step, STEPS)
            v.sem_inc(lin_used, 2)

            v.wait_ge(iotas, 5)
            v.wait_ge(src_in, 32)
            link(v.tensor_copy(key_a[:, :], key_i[:, :]))
            link(v.tensor_scalar(key_b[:, :], key_a[:, :], float(HALF), None, ALU.is_ge))
            link(v.tensor_scalar(key_t[:, :], key_a[:, :], float(HALF), None, ALU.is_lt))
            link(v.scalar_tensor_tensor(key_a[:, :], key_b[:, :], -float(HALF), key_a[:, :], ALU.mult, ALU.add))
            link(v.tensor_scalar(key_i[:, :], key_a[:, :], float(LIFT), None, ALU.add))
            link(v.tensor_scalar(key_i[:, :], key_i[:, :], ID_BITS, None, ALU.logical_shift_left))
            link(v.tensor_scalar(key_t[:, :], key_t[:, :], 31, None, ALU.logical_shift_left))
            link(v.tensor_tensor(key_i[:, :], key_i[:, :], edge_id[:, :], ALU.bitwise_or))
            link(v.tensor_tensor(key_a[:, :].bitcast(I32), key_i[:, :], key_t[:, :], ALU.bitwise_or))
            for n in range(COL_LEVELS):
                link(v.tensor_scalar(key_t[:, :], col_i[:, :], 2 << n, None, ALU.bitwise_and))
                link(v.tensor_scalar(sign_col[:, n, :], key_t[:, :], -1.0 / (1 << n), 1.0, ALU.mult, ALU.add))
            for n in range(PART_LEVELS):
                link(v.tensor_scalar(part_t[:, :], part_i[:, :], 1 << n, None, ALU.bitwise_and))
                link(v.tensor_scalar(sign_part[:, n:n + 1], part_t[:, :], -2.0 / (1 << n), 1.0,
                                     ALU.mult, ALU.add))

            v.wait_ge(edges_in, 16 * 6)
            step(v.tensor_copy(packed[:, :, 0:BOND], attr_in))
            step(v.tensor_copy(packed[:, :, BOND], key_prev[:, :]))
            step(v.tensor_copy(packed_i[:, :, BOND + 1], dst_index[:, :]))
            settle()
            v.sem_inc(packed_done, 1)

            pair = [key_a, key_b]

            def flip(level):
                a, b = pair
                if level <= COL_LEVELS:
                    link(v.tensor_tensor(b[:, :], a[:, :], sign_col[:, level - 1, :], ALU.mult))
                else:
                    n = level - COL_LEVELS - 1
                    link(v.tensor_scalar(b[:, :], a[:, :], sign_part[:, n:n + 1], None, ALU.mult))
                pair.reverse()

            def exchange(distance):
                a, b = (k[:, :].rearrange("p (b h d) -> p b h d", h=2, d=distance) for k in pair)
                step(v.tensor_tensor(b[:, :, 0], a[:, :, 0], a[:, :, 1], ALU.min))
                link(v.tensor_tensor(b[:, :, 1], a[:, :, 0], a[:, :, 1], ALU.max))
                pair.reverse()

            def turn_keys():
                pe_does()
                link(v.tensor_copy(pair[1][:, :], ps_key))
                pair.reverse()

            for level in range(1, ID_BITS + 1):
                if level < ID_BITS:
                    flip(level)
                distance = 1 << (level - 1)
                if distance >= SORT_C:
                    turn_keys()
                    while distance >= SORT_C:
                        exchange(distance // SORT_C)
                        distance //= 2
                    turn_keys()
                while distance:
                    exchange(distance)
                    distance //= 2
                if level < ID_BITS:
                    flip(level)
            assert pair[0] is key_sorted
            v.sem_inc(sorted_done, 1)

            v.wait_ge(keys_back, 16 * 3)
            here, prev, nxt = (k[:, :].bitcast(I32) for k in (key_here, key_prev, key_next))
            link(v.tensor_scalar(row_index[:, :], here, SORT_N - 1, None, ALU.bitwise_and))
            for k in (here, prev, nxt):
                step(v.tensor_scalar(k, k, ID_BITS, None, ALU.logical_shift_right))
            settle()
            step(v.tensor_tensor(goes_on[:, :], here, prev, ALU.is_equal))
            step(v.tensor_tensor(not_tail[:, :], here, nxt, ALU.is_equal))
            settle()
            half_bit = 31 - ID_BITS
            step(v.tensor_scalar(prev, here, half_bit, None, ALU.logical_shift_right))
            step(v.tensor_scalar(nxt, here, (1 << half_bit) - 1, None, ALU.bitwise_and))
            settle()
            link(v.tensor_scalar(src_index[:, :], prev, float(-HALF), float(HALF - LIFT), ALU.mult, ALU.add))
            link(v.tensor_tensor(src_index[:, :], src_index[:, :], nxt, ALU.add))
            v.sem_inc(src_known, 1)
            step(v.scalar_tensor_tensor(tail_index[:, :], not_tail[:, :], float(NOWHERE), src_index[:, :],
                                        ALU.mult, ALU.add))
            step(v.tensor_scalar(is_tail[:, :], not_tail[:, :], -1.0, 1.0, ALU.mult, ALU.add))
            step(v.tensor_scalar(goes_on_neg[:, :], goes_on[:, :], 1.0, BIG, ALU.subtract, ALU.mult))
            step(v.tensor_tensor_scan(from_prev[:, :], goes_on[:, :], goes_on[:, :], 1.0,
                                      op0=ALU.mult, op1=ALU.mult))
            step(v.tensor_tensor_scan(from_next[:, ::-1], not_tail[:, ::-1], not_tail[:, ::-1], 1.0,
                                      op0=ALU.mult, op1=ALU.mult))
            settle()
            link(v.tensor_scalar(from_prev_neg[:, :], from_prev[:, :], 1.0, BIG, ALU.subtract, ALU.mult))
            link(v.tensor_copy(wide[:, :], from_prev[:, TILES - 1:TILES].to_broadcast([P, D])))
            pe_does()
            link(v.tensor_copy(whole[:, :], ps_small[0:D, :]))
            link(v.tensor_scalar(whole_neg[:, :], whole[:, :], 1.0, BIG, ALU.subtract, ALU.mult))
            link(v.tensor_copy(wide[:, :], from_next[:, 0:1].to_broadcast([P, D])))
            pe_does()
            link(v.tensor_copy(whole_next[:, :], ps_small[0:D, :]))

            v.wait_ge(weights_in, 16 * len(weight_loads))
            link(v.tensor_scalar(rb3a[:, :], b3a_c[0:H2, :], 0.0, None, ALU.max))
            link(v.tensor_copy(rb3a_w[:, :], rb3a[:, :].to_broadcast([H2, P])))
            pe_does()
            link(v.tensor_copy(idle_row[:, :], ps_small[:, 0:D]))
            for c in range(XCH):
                v.wait_ge(x_loaded[c % 2], 16 * (c // 2 + 1))
                ring = x_ring[c % 2][:, :].rearrange("p (r d) -> p r d", d=D)
                link(v.tensor_tensor(ring, ring, over_t(idle_row[:, :], XROWS), ALU.add))
                v.sem_inc(x_added, 1)
            v.wait_ge(x_loaded[XCH % 2], 16 * (XCH // 2 + 1))
            left = x_ring[XCH % 2][0:XLEFT, 0:D]
            link(v.tensor_tensor(left, left, idle_row[0:XLEFT, :], ALU.add))
            v.sem_inc(x_added, 1)

            v.wait_ge(got_rows, 16 * TILES)
            step(v.tensor_copy(dst_index[:, :], rows_i[:, :, BOND + 1]))
            step(v.tensor_copy(weight_s[:, :], rows[:, :, BOND]))
            settle()
            v.sem_inc(dst_known, 1)

            def layer_norm(k, of, passes=None):
                to, sq, _, _ = NORMS[k]
                for c in range(CH):
                    if passes:
                        v.wait_ge(got_dst[c], 16 * CT * passes)
                    part = chunk(mean, c)
                    link(v.tensor_reduce(out=part, in_=chunk(of, c), op=ALU.add, axis=AX.X))
                    link(v.tensor_scalar(part, part, 1.0 / D, None, ALU.mult))
                    link(v.tensor_tensor(chunk(to, c), chunk(of, c), bcast(part, D), ALU.subtract))
                    v.sem_inc(centred, 1)
                for c in range(CH):
                    v.wait_ge(squared, k * CH + c + 1)
                    step(v.tensor_reduce(out=chunk(var, c), in_=chunk(sq, c), op=ALU.add, axis=AX.X))
                settle()
                v.sem_inc(root_ready, 1)
                v.wait_ge(rooted, k + 1)
                link(v.reciprocal(var[:, :], var[:, :]))
                link(v.scalar_tensor_tensor(to[:, :, :], to[:, :, :], 0.0, bcast(var[:, :], D),
                                            ALU.max, ALU.mult))

            def over_edges(buf):
                by_channel = buf[:, :, :].rearrange("p t d -> p d t")
                step(v.tensor_reduce(out=sums[:, 0, :], in_=by_channel[:, :, 0:REST], op=ALU.add, axis=AX.X))
                step(v.tensor_reduce(out=sums[:, 1, :], in_=by_channel[:, :, REST:TILES], op=ALU.add, axis=AX.X))
                settle()
                pe_does()

            def batch_norm(k, n, to):
                of, sq, _, _ = NORMS[k]
                over_edges(of)
                link(v.tensor_scalar(bn_mean[:, :], ps_small[:, 0:D], 1.0 / EDGES, None, ALU.mult))
                for c in range(CH):
                    link(v.tensor_tensor(chunk(of, c), chunk(of, c), over_t(bn_mean[:, :], CT), ALU.subtract))
                    v.sem_inc(centred, 1)
                v.wait_ge(squared, (k + 1) * CH)
                over_edges(sq)
                link(v.tensor_copy(bn_scale[:, :], ps_small[:, 0:D]))
                v.sem_inc(root_ready, 1)
                v.wait_ge(rooted, k + 1)
                link(v.reciprocal(bn_scale[:, :], bn_scale[:, :]))
                link(v.tensor_tensor(bn_scale[:, :], bn_scale[:, :], bn_par[:, 2 * n, :], ALU.mult))
                link(v.tensor_tensor(of[:, :, :], of[:, :, :], over_t(bn_scale[:, :], TILES), ALU.mult))
                link(v.tensor_tensor(of[:, :, :], of[:, :, :], over_t(bn_par[:, 2 * n + 1, :], TILES), ALU.add))
                link(v.tensor_scalar(to[:, :, :], of[:, :, :], 0.0, None, ALU.max))

            def group_prefix(buf, largest=False):
                on, inside, came, start, ops = (
                    (goes_on_neg, whole_neg, from_prev_neg, -BIG, (ALU.add, ALU.max)) if largest else
                    (goes_on, whole, from_prev, 0.0, (ALU.mult, ALU.add)))
                for d in range(D):
                    step(v.tensor_tensor_scan(buf[:, :, d], on[:, :], buf[:, :, d], start,
                                              op0=ops[0], op1=ops[1]))
                step(v.memset(carry_t[:, 0:1], start))
                settle()
                pe_does()
                link(v.tensor_tensor_scan(carry_t[:, 1:P + 1], inside[:, :], ps_small[0:D, :], start,
                                          op0=ops[0], op1=ops[1]))
                pe_does()
                link(v.tensor_copy(carry[:, :], ps_small[:, 0:D]))
                for d in range(D):
                    step(v.scalar_tensor_tensor(buf[:, :, d], came[:, :], carry[:, d:d + 1], buf[:, :, d],
                                                ops[0], ops[1]))
                settle()

            def tails_back(to, of):
                link(v.tensor_tensor(to[:, :, :], of[:, :, :], bcast(is_tail[:, :], D), ALU.mult))
                for d in range(D):
                    step(v.tensor_tensor_scan(to[:, ::-1, d], not_tail[:, ::-1], to[:, ::-1, d], 0.0,
                                              op0=ALU.mult, op1=ALU.add))
                step(v.memset(carry_t[:, P:P + 1], 0.0))
                settle()
                pe_does()
                link(v.tensor_tensor_scan(carry_t[:, 0:P][:, ::-1], whole_next[:, ::-1],
                                          ps_small[0:D, ::-1], 0.0, op0=ALU.mult, op1=ALU.add))
                pe_does()
                link(v.tensor_copy(carry[:, :], ps_small[:, 0:D]))
                for d in range(D):
                    step(v.scalar_tensor_tensor(to[:, :, d], from_next[:, :], carry[:, d:d + 1], to[:, :, d],
                                                ALU.mult, ALU.add))
                settle()

            layer_norm(0, x_dst, 1)
            v.wait_ge(last_filled, 16)
            v.sem_inc(input_ready, 1)

            def bond_quad(q, s):
                for h in range(2):
                    t = q * 4 + 2 * h
                    done = STEPS * q + STEPS + 2 * h
                    v.wait_ge(bond_mm, q * 2 + h + 1)
                    v.tensor_tensor(prod[:, :, :].rearrange("p t (k i) -> p t k i", k=BOND),
                                    ps_u[h][:, :, :].rearrange("p t (k i) -> p t k i", k=BOND),
                                    bcast(rows[:, bass.ds(t, 2), 0:BOND], D), ALU.mult).then_inc(bond_step, 1)
                    v.wait_ge(bond_step, done + 1)
                    v.tensor_reduce(out=buf_c[:, bass.ds(t, 2), :],
                                    in_=prod[:, :, :].rearrange("p t (k i) -> p t i k", k=BOND),
                                    op=ALU.add, axis=AX.X).then_inc(bond_step, 1)
                    v.wait_ge(bond_step, done + 2)
                v.wait_ge(lin_mm, q + 3)
                v.tensor_tensor(quad(buf_c, q), quad(buf_c, q), ps_o[s][:, 0, :], ALU.add)\
                    .then_inc(bond_step, 1)
                v.wait_ge(bond_step, STEPS * q + 2 * STEPS)

            first_then_second(v, bond_quad, lambda q, s: None)
            v.sem_inc(lin_used, QUADS)
            group_prefix(buf_c)
            tails_back(buf_b, buf_c)
            v.wait_ge(got_xs, 16 * TILES)
            link(v.tensor_tensor(x_src[:, :, :], x_src[:, :, :], buf_b[:, :, :], ALU.add))
            v.sem_inc(state_made, 1)

            layer_norm(1, x_src)
            layer_norm(2, x_dst, 2)
            v.sem_inc(input_ready, 1)
            v.wait_ge(lin_used, 2 * QUADS + 2)
            batch_norm(3, 0, buf_a)
            v.sem_inc(input_ready, 1)
            v.wait_ge(lin_used, 3 * QUADS + 2)
            batch_norm(4, 1, buf_c)
            group_prefix(buf_c)
            v.wait_ge(state_stored, 16)
            link(v.tensor_tensor(x_src[:, :, :], x_src[:, :, :], buf_c[:, :, :], ALU.add))
            v.sem_inc(state_made, 1)

            layer_norm(5, x_dst, 3)
            of = buf_a
            for turn in range(3):
                if turn:
                    for c in range(CH):
                        v.wait_ge(got_dst[c], 16 * CT * (3 + turn))
                    v.wait_ge(state_stored, 16 * (2 + turn))
                link(v.tensor_tensor(buf_c[:, :, :], of[:, :, :], bcast(weight_s[:, :], D), ALU.mult))
                if turn < 2:
                    link(v.memset(buf_b[:, :, :], 0.0))
                group_prefix(buf_c)
                if turn < 2:
                    v.sem_inc(state_made, 1)
                of = buf_b
            v.wait_ge(state_stored, 16 * 2)
            link(v.tensor_tensor(x_src[:, :, :], x_src[:, :, :], buf_c[:, :, :], ALU.add))
            v.sem_inc(state_made, 1)

            layer_norm(6, x_dst, 6)
            link(v.tensor_scalar(buf_a[:, :, :], buf_a[:, :, :], 0.0, MSG_EPS, ALU.max, ALU.add))
            link(v.tensor_scalar(buf_b[:, :, :], buf_a[:, :, :], beta_c[:, :], None, ALU.mult))
            link(v.tensor_copy(buf_c[:, :, :], buf_b[:, :, :]))
            group_prefix(buf_c, largest=True)
            tails_back(x_dst, buf_c)
            link(v.tensor_tensor(buf_b[:, :, :], buf_b[:, :, :], x_dst[:, :, :], ALU.subtract))
            v.sem_inc(exp_ready, 1)
            v.wait_ge(exp_done, 1)
            link(v.tensor_tensor(buf_a[:, :, :], buf_a[:, :, :], buf_b[:, :, :], ALU.mult))
            group_prefix(buf_a)
            group_prefix(buf_b)
            link(v.tensor_scalar(buf_b[:, :, :], buf_b[:, :, :], 1e-30, None, ALU.max))
            link(v.reciprocal(buf_b[:, :, :], buf_b[:, :, :]))
            link(v.tensor_tensor(buf_a[:, :, :], buf_a[:, :, :], buf_b[:, :, :], ALU.mult))
            v.sem_inc(input_ready, 1)
            v.wait_ge(state_stored, 16 * STATES)

            def add_quad(q, s):
                v.wait_ge(lin_mm, 3 * QUADS + q + 3)
                v.tensor_tensor(quad(x_src, q), quad(x_src, q), ps_o[s][:, 0, :], ALU.add).then_inc(lin_used, 1)

            first_then_second(v, add_quad, lambda q, s: None)
            v.wait_ge(lin_used, 4 * QUADS + 2)
            v.sem_inc(final_made, 1)

        @block.tensor
        def _(pe):
            small = [0]

            def asked():
                small[0] += 1
                pe.wait_ge(to_pe, small[0])

            def turn_keys(keys):
                asked()
                pe.transpose(ps_t[0][:, 0, :], keys[:, 0:P], ident[:, :])
                pe.transpose(ps_t[0][:, 1, :], keys[:, P:2 * P], ident[:, :]).then_inc(from_pe, 1)

            def turn_wide(a):
                asked()
                pe.transpose(ps_small[0:D, :], a, ident[:, :]).then_inc(from_pe, 1)

            def turn_back(a):
                asked()
                pe.transpose(ps_small[:, 0:D], a, ident[0:D, 0:D]).then_inc(from_pe, 1)

            def group_carry(buf):
                turn_wide(buf[:, TILES - 1, :])
                turn_back(carry_t[:, 0:P])

            def tail_carry(buf):
                turn_wide(buf[:, 0, :])
                turn_back(carry_t[:, 1:P + 1])

            def over_edges():
                asked()
                pe.matmul(ps_small[:, 0:D], ones[:, :], sums[:, 0, :], start=True, stop=False)
                pe.matmul(ps_small[:, 0:D], ones_full[:, :], sums[:, 1, :], start=False, stop=True)\
                    .then_inc(from_pe, 1)

            def turn(stage, *bufs):
                def one(q, s):
                    pe.wait_ge(copied, stage * QUADS + q + 1)
                    for n, buf in enumerate(bufs):
                        last = pe.transpose(ps_t[s][:, n, :], quad(buf, q), ident[:, :])
                    last.then_inc(turned, 1)
                return one

            def ready(stage, q):
                pe.wait_ge(copied, stage * QUADS + q + 3)
                if stage:
                    pe.wait_ge(lin_used, stage * QUADS + q + 1)

            def bond_products(q, s):
                ready(0, q)
                for h in range(2):
                    pe.wait_ge(bond_step, STEPS * q + 1 + 2 * h)
                    for t in range(2):
                        r = slice(32 * (2 * h + t), 32 * (2 * h + t) + 32)
                        last = pe.matmul(ps_u[h][:, t, :], w_t[s][r, 0, :], bond_w[r, :], start=True, stop=True)
                    last.then_inc(bond_mm, 1)
                pe.wait_ge(bond_step, STEPS * q)
                pe.matmul(ps_o[s][:, 0, :], w_t[s][:, 0, :], bond_bd[:, :], start=True, stop=True)\
                    .then_inc(lin_mm, 1)

            def pair_products(q, s):
                ready(1, q)
                pe.matmul(ps_o[s][:, 0, :], ones[0:1, :], b1_row[:, :], start=True, stop=False)
                pe.matmul(ps_o[s][:, 0, :], w_t[s][:, 0, :], w1s_bd[:, :], start=False, stop=False)
                pe.matmul(ps_o[s][:, 0, :], w_t[s][:, 1, :], w1d_bd[:, :], start=False, stop=True)\
                    .then_inc(lin_mm, 1)

            def second_products(q, s):
                ready(2, q)
                pe.matmul(ps_o[s][:, 0, :], ones[0:1, :], b2_row[:, :], start=True, stop=False)
                pe.matmul(ps_o[s][:, 0, :], w_t[s][:, 0, :], w2_bd[:, :], start=False, stop=True)\
                    .then_inc(lin_mm, 1)

            def mlp_products(q, s):
                ready(3, q)
                pe.wait_ge(hid_done, q + 1)
                for u in range(2):
                    r = slice(64 * u, 64 * u + 64)
                    last = pe.matmul(ps_u[s][:, u, 0:P], w3a_bd[r, :], w_t[s][r, 0, :], start=True, stop=True)
                last.then_inc(hid_mm, 1)
                pe.wait_ge(hid_done, q + 3)
                pe.matmul(ps_o[s][:, 0, :], ones[0:1, :], b3b_row[:, :], start=True, stop=False)
                for u in range(2):
                    last = pe.matmul(ps_o[s][:, 0, H2 * u:H2 * u + H2], r_t[s][:, u, :], w3b_bd[:, :],
                                     start=False, stop=u == 1)
                last.then_inc(lin_mm, 1)

            pe.sem_inc(lin_mm, 2)
            pe.wait_ge(ident_made, 4)
            for n in range(2 * PART_TURNS):
                turn_keys(key_turned[n])
            turn_wide(wide[:, :])
            turn_wide(wide[:, :])
            pe.wait_ge(weights_in, 16 * len(weight_loads))
            asked()
            pe.matmul(ps_small[:, 0:D], rb3a_w[:, :], w3b_bd[0:H2, 0:D], start=True, stop=False)
            pe.matmul(ps_small[:, 0:D], ones[0:1, :], b3b_row[:, 0:D], start=False, stop=True).then_inc(from_pe, 1)
            pe.wait_ge(input_ready, 1)
            first_then_second(None, turn(0, buf_a), bond_products)
            group_carry(buf_c)
            tail_carry(buf_b)
            pe.wait_ge(input_ready, 2)
            first_then_second(None, turn(1, buf_a, buf_b), pair_products)
            over_edges()
            over_edges()
            pe.wait_ge(input_ready, 3)
            first_then_second(None, turn(2, buf_a), second_products)
            over_edges()
            over_edges()
            group_carry(buf_c)
            for _ in range(3):
                group_carry(buf_c)
            group_carry(buf_c)
            tail_carry(x_dst)
            group_carry(buf_a)
            group_carry(buf_b)
            pe.wait_ge(input_ready, 4)
            first_then_second(None, turn(3, buf_a), mlp_products)


def kernel(**inputs):
    import numpy as np
    import concourse.bacc as bacc
    from concourse import mybir as mb
    from concourse.bass_utils import run_bass_kernel_spmd as run

    a = {k: np.ascontiguousarray(v) for k, v in inputs.items()}
    a["L0_gnn_kernel"] = np.ascontiguousarray(a["L0_gnn_kernel"].reshape(16, 32, 32).transpose(2, 0, 1)
                                              .reshape(32, 512))
    a["L0_gnn_bias"] = np.ascontiguousarray(a["L0_gnn_bias"].reshape(32, 32).T)
    names = ["x", "src", "dst", "edge_attr_16", "edge_weight", "L0_gnn_kernel", "L0_gnn_bias",
             "L1_gnn_W1", "L1_gnn_b1", "L1_gnn_gamma1", "L1_gnn_beta1", "L1_gnn_W2", "L1_gnn_b2",
             "L1_gnn_gamma2", "L1_gnn_beta2", "L3_gnn_beta", "L3_gnn_W1", "L3_gnn_b1", "L3_gnn_W2", "L3_gnn_b2"]
    nc = bacc.Bacc("TRN2", target_bir_lowering=False, num_devices=1)
    arrays, args = {}, []
    for name in names:
        arrays[f"in_{name}"] = a[name]
        args.append(nc.dram_tensor(f"in_{name}", a[name].shape, mb.dt.from_np(a[name].dtype),
                                   kind="ExternalInput").ap())
    args.append(nc.dram_tensor("out_x", a["x"].shape, mb.dt.float32, kind="ExternalOutput").ap())
    gnn(nc, *args)
    return run(nc, [arrays], core_ids=[0]).results[0]["out_x"]
```

```python
import concourse.bass as bass
from concourse import mybir
from contextlib import ExitStack

FP32 = mybir.dt.float32
I32 = mybir.dt.int32
F16 = mybir.dt.float16
BF16 = mybir.dt.bfloat16
ALU = mybir.AluOpType
ACT = mybir.ActivationFunctionType
AX = mybir.AxisListType

P = 128
D = 32
BOND = 16
H2 = 2 * D
LN_EPS = 1e-05
BN_EPS = 1e-05
MSG_EPS = 1e-07
BIG = 1e38
NOWHERE = 1 << 20


def gnn(nc, x, src, dst, attr, weight, bond_k, bond_b, w1a, b1a, g1a, be1a, w1b, b1b, g1b, be1b,
        beta3, w3a, b3a, w3b, b3b, out):
    NODES = x.shape[0]
    EDGES = src.shape[0]
    TILES = -(-EDGES // (P * 4)) * 4
    SLOTS = P * TILES
    QUADS = TILES // 4
    FULL_P = EDGES // TILES
    REST = EDGES - FULL_P * TILES
    assert FULL_P == P - 1 and 0 < REST < TILES
    SORT_C = 256
    SORT_N = P * SORT_C
    ID_BITS = SORT_N.bit_length() - 1
    HALF = NODES // 2
    LIFT = 1 << (23 - ID_BITS)
    NARROW = 64
    W_AT, DST_AT, X_AT = BOND, BOND + 1, BOND + 2
    ROW = X_AT + D
    XROW = D + 1
    LOS = -(-NODES // P)
    LO_H = LOS // 2
    LAST_N = LOS * P
    XROWS = 71
    XCH = (NODES // P) // XROWS
    assert XCH * XROWS == NODES // P
    XLEFT = NODES - P * XCH * XROWS
    HOT = 4
    HOT_LOOP = 28
    LOOP = 8
    CHUNK = 28
    NC = TILES // CHUNK
    QUADS_C = CHUNK // 4
    assert NC * CHUNK == TILES
    PARTS = 3
    KP = PARTS * D
    LOOPS = QUADS // LOOP
    ZEROS = TILES * D // 4
    assert LOOPS * LOOP == QUADS - 1

    ctx = ExitStack()
    with ctx:
        def sb(name, shape, dt=FP32):
            return ctx.enter_context(nc.sbuf_tensor(name, shape, dt))

        def pb(name, shape, dt=FP32):
            return ctx.enter_context(nc.psum_tensor(name, shape, dt))

        def sem(name):
            return ctx.enter_context(nc.semaphore(name))

        def dram(name, shape, dt=FP32):
            return nc.dram_tensor(name, shape, dt, kind="Internal").ap()

        sorted_keys = dram("sorted_keys", (SORT_N + 2,))
        edge_rows = dram("edge_rows", (SLOTS, ROW))
        node_last = dram("node_last", (LAST_N,))
        nodes_x = dram("nodes_x", (NODES, XROW))
        x1_table, x2_table, y1_table = (dram(n, (SLOTS, D)) for n in ("x1_table", "x2_table", "y1_table"))
        y2_table, y3_table = (dram(n, (SLOTS, D)) for n in ("y2_table", "y3_table"))
        h_table = dram("h_table", (SLOTS, D))

        rows = sb("rows", [P, TILES, ROW])
        x_src = rows[:, :, X_AT:ROW]
        x_dst_rows = sb("x_dst_rows", [P, TILES, XROW])
        x_dst = x_dst_rows[:, :, 0:D]
        buf_ab = sb("buf_ab", [P, 2, TILES + 2, D])
        wide_a, wide_b, wide_c = buf_ab[:, 0], buf_ab[:, 1], sb("wide_c", [P, TILES + 2, D])
        buf_a, buf_b, buf_c = (w[:, 0:TILES, :] for w in (wide_a, wide_b, wide_c))
        x_state = rows[:, :, :].rearrange("p t r -> p (t r)")[:, 0:TILES * D].rearrange("p (t d) -> p t d", d=D)
        spare = x_dst_rows[:, :, :].rearrange("p t k -> p (t k)")
        buf_d = spare[:, 0:TILES * D].rearrange("p (t d) -> p t d", d=D)
        x_live = spare[:, 0:(TILES + 2) * D].rearrange("p (t d) -> p t d", d=D)
        packed = buf_ab[:, :, :, :].rearrange("p a t d -> p (a t d)")[:, 0:TILES * ROW].rearrange(
            "p (t r) -> p t r", r=ROW)
        early = wide_c[:, :, :].rearrange("p t d -> p (t d)")
        PAD = XROWS * XROW
        x_pad = [early[:, n * PAD:(n + 1) * PAD].rearrange("p (r k) -> p r k", k=XROW) for n in range(2)]
        early2 = x_dst_rows[:, :, :].rearrange("p t k -> p (t k)")
        cnt, tot, run, turned_last = (early2[:, n * 896:n * 896 + w] for n, w in
                                      enumerate((LOS, LOS, LOS, 7 * P)))
        ones_wide = early2[:, 4 * 896:4 * 896 + LOS]
        attr_in = rows[:, :, :].rearrange("p t r -> p (t r)")[:, 0:TILES * BOND].rearrange(
            "p (t k) -> p t k", k=BOND)

        key_a = sb("key_a", [P, SORT_C])
        key_b = sb("key_b", [P, SORT_C])
        key_i = sb("key_i", [P, SORT_C], I32)
        key_t = sb("key_t", [P, SORT_C], I32)
        edge_id = sb("edge_id", [P, SORT_C], I32)
        col_i = sb("col_i", [P, SORT_C], I32)
        part_i = sb("part_i", [P, 1], I32)
        part_t = sb("part_t", [P, 1], I32)
        COL_LEVELS = SORT_C.bit_length() - 2
        PART_LEVELS = ID_BITS - COL_LEVELS - 1
        PART_TURNS = P.bit_length() - 1
        sign_col = sb("sign_col", [P, COL_LEVELS, SORT_C], F16)
        sign_part = sb("sign_part", [P, PART_LEVELS])
        zero1 = sb("zero1", [1, 1])

        key_here = sb("key_here", [P, TILES])
        key_prev = sb("key_prev", [P, TILES])
        key_next = sb("key_next", [P, TILES])
        row_index = sb("row_index", [P, TILES], I32)
        src_index = sb("src_index", [P, TILES], I32)
        dst_index = sb("dst_index", [P, TILES], I32)
        tail_index = sb("tail_index", [P, TILES], I32)
        dst_last = sb("dst_last", [P, TILES], I32)
        src_raw = dst_last
        last_sb = sb("last_sb", [P, NODES // P])
        last_left = sb("last_left", [XLEFT, 1])
        src_hi = sb("src_hi", [P, TILES])
        src_lo = sb("src_lo", [P, TILES])
        lo_iota = sb("lo_iota", [P, LOS], F16)
        hot = sb("hot", [P, HOT * (LOS + P)], F16)
        hot_lo = [hot[:, n * (LOS + P):n * (LOS + P) + LOS] for n in range(HOT)]
        hot_hi = [hot[:, n * (LOS + P) + LOS:(n + 1) * (LOS + P)] for n in range(HOT)]
        weights_early = sb("weights_early", [KP, (BOND + 1) * D])
        VE_MAX = TILES + 2
        live_parts = hot[:, :].bitcast(FP32)
        (live_w, live_ids, live_goes, live_from, live_y, live_slot, live_last, live_empty, live_t) = (
            live_parts[:, n * VE_MAX:(n + 1) * VE_MAX] for n in range(9))
        live_y, live_slot, live_last = (a.bitcast(I32) for a in (live_y, live_slot, live_last))
        slot_id = sb("slot_id", [P, TILES], I32)
        own_tail = sb("own_tail", [P, TILES])
        live = sb("live", [P, TILES])
        count_i = sb("count_i", [D, 1], I32)
        row_base = sb("row_base", [P, 1])
        live_whole = sb("live_whole", [D, P])
        upper = sb("upper", [P, P])
        weight_s = sb("weight_s", [P, TILES])
        goes_on = sb("goes_on", [P, TILES])
        goes_on_neg = sb("goes_on_neg", [P, TILES])
        not_tail = sb("not_tail", [P, TILES])
        is_tail = sb("is_tail", [P, TILES])
        from_prev = sb("from_prev", [P, TILES])
        from_prev_neg = sb("from_prev_neg", [P, TILES])
        from_next = sb("from_next", [P, TILES])
        whole = sb("whole", [D, P])
        whole_neg = sb("whole_neg", [D, P])
        whole_next = sb("whole_next", [D, P])
        wide = sb("wide", [P, D])
        carry_t = sb("carry_t", [D, P + 1])
        carry = sb("carry", [P, D])
        mean = sb("mean", [P, TILES])
        var = sb("var", [P, TILES])
        eps_c = sb("eps_c", [P, 1])

        ident = sb("ident", [P, P])
        ones = sb("ones", [P, P])
        ones_full = sb("ones_full", [P, P])
        ident_half = sb("ident_half", [P, P], BF16)
        bond_parts = sb("bond_parts", [KP, PARTS, BOND * D], BF16)
        bias_parts = sb("bias_parts", [KP, PARTS, D], BF16)
        w1s_bd = sb("w1s_bd", [P, P])
        w1d_bd = sb("w1d_bd", [P, P])
        w2_bd = sb("w2_bd", [P, P])
        b1_row = sb("b1_row", [1, P])
        b2_row = sb("b2_row", [1, P])
        bn_par = sb("bn_par", [P, 4, D])
        beta_c = sb("beta_c", [P, 1])
        w3a_bd = sb("w3a_bd", [P, P])
        w3b_bd = sb("w3b_bd", [P, H2])
        b3a_c = sb("b3a_c", [P, 1])
        b3b_row = sb("b3b_row", [1, P])
        rb3a = sb("rb3a", [H2, 1])
        rb3a_w = sb("rb3a_w", [H2, P])
        idle_row = sb("idle_row", [P, D])
        sums = sb("sums", [P, 2, D])
        bn_mean = sb("bn_mean", [P, D])
        bn_scale = sb("bn_scale", [P, D])
        w_t = [sb(f"w_t{n}", [P, 2, P]) for n in range(2)]
        r_t = [sb(f"r_t{n}", [P, 2, P]) for n in range(2)]
        x_ring = [sb("x_ring0", [P, XROWS * D]),
                  buf_ab[:, :, :, :].rearrange("p a t d -> p (a t d)")[:, TILES * ROW:TILES * ROW + XROWS * D]]

        ps_t = [pb(f"ps_t{n}", [P, 4, P]) for n in range(2)]
        ps_u = [pb(f"ps_u{n}", [P, 2, BOND * D]) for n in range(2)]
        ps_o = [pb(f"ps_o{n}", [P, 4, P]) for n in range(2)]
        prod = x_ring[0][:, 0:2 * BOND * D].rearrange("p (t f) -> p t f", t=2)
        PART_W = CHUNK * KP // 2
        norm_parts = [wide_b.rearrange("p t d -> p (t d)")[:, n * PART_W:(n + 1) * PART_W].bitcast(BF16)
                      .rearrange("p (t n j) -> p t n j", n=PARTS, j=D) for n in range(2)]
        parts_t = [w_t[n][:, :, :].rearrange("p a b -> p (a b)").bitcast(BF16)[0:KP, :] for n in range(2)]
        ps_parts = [ps_t[n][:, 0:2, :].rearrange("p a b -> p (a b)").bitcast(BF16)[0:KP, :] for n in range(2)]
        ps_key = ps_t[0][:, 0:2, :].rearrange("p a b -> p (a b)")
        ps_small = ps_t[1][:, 0, :]

        key_pair = (key_a, key_b)
        moves, key_turned = 0, []
        for level in range(1, ID_BITS + 1):
            moves += level < ID_BITS
            crossing = max(0, level - (SORT_C.bit_length() - 1))
            if crossing:
                key_turned += [key_pair[moves % 2], key_pair[(moves + 1 + crossing) % 2]]
                moves += 2
            moves += level + (level < ID_BITS)
        key_sorted = key_pair[moves % 2]

        bond_in = weights_early[0:KP, 0:BOND * D]
        bias_in = weights_early[0:KP, BOND * D:BOND * D + D]
        weight_loads = [(bn_par[:, n, :], p.partition_broadcast(P)) for n, p in enumerate((g1a, be1a, g1b, be1b))]
        weight_loads.append((beta_c[:, :], beta3.partition_broadcast(P)))
        for t in range(4):
            r = slice(32 * t, 32 * t + 32)
            weight_loads += [
                (w1s_bd[r, r], w1a[0:D, :]),
                (w1d_bd[r, r], w1a[D:2 * D, :]), (w2_bd[r, r], w1b), (b1_row[0:1, r], b1a.unsqueeze(0)),
                (b2_row[0:1, r], b1b.unsqueeze(0)), (b3b_row[0:1, r], b3b.unsqueeze(0)),
                (w3a_bd[r, H2 * (t % 2):H2 * (t % 2) + H2], w3a)]
        for n in range(PARTS):
            r = slice(D * n, D * n + D)
            weight_loads += [(bond_in[r, :], bond_k), (bias_in[r, :], bond_b)]
        for t in range(2):
            r = slice(H2 * t, H2 * t + H2)
            weight_loads += [(w3b_bd[r, D * t:D * t + D], w3b), (b3a_c[r, :], b3a.unsqueeze(1))]

        iotas = sem("iotas")
        ident_made = sem("ident_made")
        keys_blank = sem("keys_blank")
        src_in = sem("src_in")
        edges_blank = sem("edges_blank")
        edges_in = sem("edges_in")
        packed_done = sem("packed_done")
        rows_stored = sem("rows_stored")
        weights_in = sem("weights_in")
        blocks_blank = sem("blocks_blank")
        dve_step = sem("dve_step")
        bond_step = sem("bond_step")
        to_pe = sem("to_pe")
        from_pe = sem("from_pe")
        sorted_done = sem("sorted_done")
        sorted_stored = sem("sorted_stored")
        keys_back = sem("keys_back")
        src_known = sem("src_known")
        hot_made = sem("hot_made")
        hot_used = sem("hot_used")
        counted = sem("counted")
        last_made = sem("last_made")
        last_stored = sem("last_stored")
        last_back = sem("last_back")
        x_padded = sem("x_padded")
        padded_stored = [sem(f"padded_stored{n}") for n in range(2)]
        got_rows = sem("got_rows")
        dst_known = sem("dst_known")
        last_known = sem("last_known")
        got_dst = [sem(f"got_dst{c}") for c in range(NC)]
        got_xs = sem("got_xs")
        state_made = sem("state_made")
        state_stored = sem("state_stored")
        state_spread = sem("state_spread")
        state_kept = sem("state_kept")
        zeros_made = sem("zeros_made")
        zeros_stored = sem("zeros_stored")
        h_stored = sem("h_stored")
        count_known = sem("count_known")
        last_listed = sem("last_listed")
        slot_listed = sem("slot_listed")
        y_listed = sem("y_listed")
        got_live = sem("got_live")
        h_made = sem("h_made")
        h_put = sem("h_put")
        h_back = sem("h_back")
        y_made = sem("y_made")
        y_put = sem("y_put")
        y3_back = sem("y3_back")
        centred = sem("centred")
        squared = sem("squared")
        root_ready = sem("root_ready")
        rooted = sem("rooted")
        input_ready = sem("input_ready")
        turned = sem("turned")
        copied = sem("copied")
        bond_mm = sem("bond_mm")
        parts_first = sem("parts_first")
        rest_made = sem("rest_made")
        parts_second = sem("parts_second")
        parts_made = sem("parts_made")
        lin_mm = sem("lin_mm")
        lin_used = sem("lin_used")
        hid_mm = sem("hid_mm")
        hid_done = sem("hid_done")
        exp_ready = sem("exp_ready")
        exp_done = sem("exp_done")
        x_loaded = [sem(f"x_loaded{n}") for n in range(2)]
        x_added = sem("x_added")
        x_stored = [sem(f"x_stored{n}") for n in range(2)]
        out_rows = sem("out_rows")
        final_made = sem("final_made")

        block = ctx.enter_context(nc.Block())

        CHUNKS = [(t, t + CHUNK) for t in range(0, TILES, CHUNK)]
        STEPS = 5

        def first_then_second(eng, first, second):
            if eng is None:
                for q in range(QUADS + 1):
                    if q < QUADS:
                        first(q, q % 2)
                    if q:
                        second(q - 1, (q - 1) % 2)
                return
            with eng.Fori(0, LOOPS) as i:
                for j in range(LOOP + 1):
                    if j < LOOP:
                        first(i * LOOP + j, j % 2)
                    if j:
                        second(i * LOOP + j - 1, (j - 1) % 2)
            first(QUADS - 1, (QUADS - 1) % 2)
            second(QUADS - 1, (QUADS - 1) % 2)

        def narrow_or_wide(eng, layers):
            count = eng.value_load(count_i[0:1, 0:1], min_val=0, max_val=TILES)
            with eng.If(count < NARROW + 1):
                layers(NARROW)
            with eng.Else():
                layers(TILES)

        def quad(buf, q):
            return buf[:, bass.ds(q * 4, 4), :].rearrange("p t d -> p (t d)")

        def slots_norm(of, to, sq):
            return [(of[:, a:b], to[:, a:b], sq[:, a:b], mean[:, a:b], var[:, a:b]) for a, b in CHUNKS]

        def live_norm(vw):
            cols = slice(1, 1 + vw)
            return [(x_live[:, cols], wide_b[:, cols], wide_c[:, cols], live_t[:, cols], live_empty[:, cols])]

        NORM0 = slots_norm(x_dst, buf_a, buf_c)

        def bcast(a, n):
            return a.unsqueeze(len(a.shape)).to_broadcast(list(a.shape) + [n])

        @block.sync
        def _(sp):
            def by_edge(to, of):
                full = FULL_P * TILES
                yield sp.dma_start(to[0:FULL_P, 0:TILES], of[0:full].rearrange("(p t) k -> p t k", t=TILES))
                yield sp.dma_start(to[FULL_P:P, 0:REST], of[full:EDGES].unsqueeze(0))

            sp.wait_ge(keys_blank, 1)
            for to in (src_raw, key_i):
                for load in by_edge(to[:, :].unsqueeze(2), src.unsqueeze(1)):
                    load.then_inc(src_in, 16)
            sp.wait_ge(edges_blank, 1)
            for to, of in ((attr_in, attr), (key_prev[:, :].unsqueeze(2), weight.unsqueeze(1)),
                           (dst_index[:, :].unsqueeze(2), dst.unsqueeze(1))):
                for load in by_edge(to, of):
                    load.then_inc(edges_in, 16)
            sp.wait_ge(sorted_done, 1)
            sp.dma_start(sorted_keys[0:1].unsqueeze(0), zero1[:, :]).then_inc(sorted_stored, 16)
            sp.dma_start(sorted_keys[1:1 + SORT_N].rearrange("(p t) -> p t", p=P), key_sorted[:, :])\
                .then_inc(sorted_stored, 16)
            sp.wait_ge(sorted_stored, 32)
            for to, off in ((key_here, 1), (key_prev, 0), (key_next, 2)):
                sp.dma_start(to[:, :], sorted_keys[off:off + SLOTS].rearrange("(p t) -> p t", p=P))\
                    .then_inc(keys_back, 16)
            sp.wait_ge(last_made, 1)
            by_lo = node_last.rearrange("(l h) -> l h", h=P)
            whole_blocks = LOS // P
            tl = turned_last.rearrange("p (b h) -> p b h", h=P)
            sp.dma_start(by_lo[0:whole_blocks * P].rearrange("(b l) h -> l b h", l=P), tl[:, 0:whole_blocks])\
                .then_inc(last_stored, 16)
            sp.dma_start(by_lo[whole_blocks * P:LOS], tl[0:LOS - whole_blocks * P, whole_blocks])\
                .then_inc(last_stored, 16)
            sp.wait_ge(last_stored, 32)
            full = P * XCH * XROWS
            sp.dma_start(last_sb[:, :], node_last[0:full].rearrange("(p r) -> p r", p=P)).then_inc(last_back, 16)
            sp.dma_start(last_left[:, :], node_last[full:NODES].unsqueeze(1)).then_inc(last_back, 16)
            sp.wait_ge(packed_done, 1)
            sp.wait_ge(got_xs, 16 * TILES)
            sp.dma_start(edge_rows.rearrange("(p t) r -> p t r", p=P), packed).then_inc(rows_stored, 16)
            def by_slot(table):
                return table.rearrange("(p t) d -> p t d", p=P)

            sp.wait_ge(zeros_made, 1)
            for table in (y2_table, y3_table):
                for n in range(4):
                    sp.dma_start(table.rearrange("(p t) d -> p (t d)", p=P)[:, n * ZEROS:(n + 1) * ZEROS],
                                 x_ring[0][:, 0:ZEROS]).then_inc(zeros_stored, 16)
            sp.wait_ge(input_ready, NC)
            sp.dma_start(by_slot(h_table), buf_a).then_inc(h_stored, 16)
            sp.wait_ge(state_made, 1)
            sp.dma_start(by_slot(x1_table), buf_a).then_inc(state_stored, 16)
            sp.wait_ge(count_known, 1)

            def layers(vw):
                sp.wait_ge(h_put, 16 * vw)
                sp.dma_start(buf_b, by_slot(h_table)).then_inc(h_back, 16)
                sp.wait_ge(state_made, 2)
                sp.dma_start(by_slot(x2_table), x_state).then_inc(state_stored, 16)
                sp.wait_ge(h_put, 16 * vw * 2)
                sp.dma_start(buf_a, by_slot(h_table)).then_inc(h_back, 16)
                sp.wait_ge(state_made, 3)
                sp.dma_start(by_slot(y1_table), buf_c).then_inc(state_stored, 16)
                sp.wait_ge(y_put, 16 * (vw + 2) * 2)
                sp.wait_ge(h_put, 16 * vw * 3)
                sp.dma_start(buf_a, by_slot(h_table)).then_inc(h_back, 16)
                sp.dma_start(buf_c, by_slot(y3_table)).then_inc(y3_back, 16)
                sp.wait_ge(y3_back, 16)
                sp.wait_ge(state_stored, 16 * 3)

            narrow_or_wide(sp, layers)

        @block.scalar
        def _(act):
            act.wait_ge(blocks_blank, 1)
            for to, of in weight_loads:
                act.dma_start(to, of).then_inc(weights_in, 16)

            def x_rows(t, c):
                return t[0:P * XCH * XROWS, :].rearrange("(p c r) d -> c p (r d)", c=XCH, r=XROWS)[c]

            def load(c):
                if c >= 2:
                    act.wait_ge(x_stored[c % 2], 16 * (c // 2))
                act.dma_start(x_ring[c % 2][:, :], x_rows(x, c)).then_inc(x_loaded[c % 2], 16)

            def pad(c, ring, tail, padded, to):
                act.wait_ge(x_loaded[c % 2], 16 * (c // 2 + 1))
                if c >= 2:
                    act.wait_ge(padded_stored[c % 2], 16 * (c // 2))
                act.activation(padded[:, :, D], tail, ACT.Copy).then_inc(x_padded, 1)
                act.activation(padded[:, :, 0:D], ring, ACT.Copy).then_inc(x_padded, 1)
                act.wait_ge(x_padded, 2 * c + 2)
                act.dma_start(to, padded).then_inc(padded_stored[c % 2], 16)

            full = P * XCH * XROWS
            padded_rows = nodes_x[0:full].rearrange("(p c r) k -> c p r k", c=XCH, r=XROWS)
            left = x_ring[XCH % 2][0:XLEFT, 0:D]
            load(0)
            act.wait_ge(last_back, 32)
            for c in range(XCH):
                if c + 1 < XCH:
                    load(c + 1)
                pad(c, x_ring[c % 2][:, :].rearrange("p (r d) -> p r d", d=D),
                    last_sb[:, c * XROWS:(c + 1) * XROWS], x_pad[c % 2], padded_rows[c])
                act.wait_ge(x_added, c + 1)
                act.dma_start(x_rows(out, c), x_ring[c % 2][:, :]).then_inc(x_stored[c % 2], 16)
            act.wait_ge(x_stored[XCH % 2], 16 * (XCH // 2))
            act.dma_start(left, x[full:NODES, :]).then_inc(x_loaded[XCH % 2], 16)
            pad(XCH, left.unsqueeze(1), last_left[:, :], x_pad[XCH % 2][0:XLEFT, 0:1],
                nodes_x[full:NODES].unsqueeze(1))
            act.wait_ge(x_added, XCH + 1)
            act.dma_start(out[full:NODES, :], left).then_inc(x_stored[XCH % 2], 16)

            normed = [0]

            def square(part):
                act.wait_ge(centred, normed[0] + part + 1)
                of = act_parts[part]
                act.activation(of[2], of[1], ACT.Square).then_inc(squared, 1)

            def root(part):
                act.wait_ge(root_ready, normed[0] + part + 1)
                v = act_parts[part][4]
                act.activation(v, v, ACT.Sqrt, bias=eps_c[:, :], scale=1.0 / D).then_inc(rooted, 1)

            def norm(parts):
                act_parts[:] = parts
                for n in range(len(parts) + 1):
                    if n < len(parts):
                        square(n)
                    if n:
                        root(n - 1)
                normed[0] += len(parts)

            act_parts = []

            def edge_norm():
                for n, (a, b) in enumerate(CHUNKS):
                    act.wait_ge(centred, normed[0] + n + 1)
                    act.activation(buf_b[:, a:b], buf_c[:, a:b], ACT.Square).then_inc(squared, 1)
                act.wait_ge(root_ready, normed[0] + NC)
                act.activation(bn_scale[:, :], bn_scale[:, :], ACT.Sqrt, bias=eps_c[:, :], scale=1.0 / EDGES)\
                    .then_inc(rooted, NC)
                normed[0] += NC

            def copy_turned(stage, blocks):
                def copy(q, s):
                    act.wait_ge(turned, stage * QUADS + q + 1)
                    act.wait_ge(lin_mm, stage * QUADS + q + 1)
                    act.activation(w_t[s][:, 0:blocks, :], ps_t[s][:, 0:blocks, :], ACT.Copy)\
                        .then_inc(copied, 1)
                return copy

            def take(stage):
                def move(q, s):
                    act.wait_ge(lin_mm, stage * QUADS + q + 3)
                    act.activation(quad(buf_c, q), ps_o[s][:, 0, :], ACT.Copy).then_inc(lin_used, 1)
                return move

            def hidden(q, s):
                act.wait_ge(hid_mm, q + 1)
                act.wait_ge(lin_mm, 3 * QUADS + q + 1)
                act.activation(r_t[s][:, :, :], ps_u[s][:, :, 0:P], ACT.Relu, bias=b3a_c[:, :])\
                    .then_inc(hid_done, 1)

            for n in range(2):
                act.wait_ge(x_stored[n], 16 * ((XCH + 2 - n) // 2))
            act.sem_inc(copied, 2)
            act.sem_inc(hid_done, 2)
            act_parts[:] = NORM0

            def first_parts(n):
                a, b = CHUNKS[n]
                act.wait_ge(input_ready, n + 1)
                if n >= 2:
                    act.wait_ge(turned, QUADS_C * (n - 1))
                act.activation(norm_parts[n % 2][:, :, 0], buf_a[:, a:b], ACT.Copy).then_inc(parts_first, 1)

            def second_parts(n):
                a, b = CHUNKS[n]
                act.wait_ge(rest_made, n + 1)
                act.activation(norm_parts[n % 2][:, :, 1], buf_c[:, a:b], ACT.Copy).then_inc(parts_second, 1)

            def copy_parts(q, s):
                act.wait_ge(turned, q + 1)
                act.wait_ge(lin_mm, q + 1)
                act.activation(parts_t[s], ps_parts[s], ACT.Copy).then_inc(copied, 1)

            for n in range(NC + 1):
                stages = [square, root, first_parts, second_parts] if n < NC else [None] * 4
                for stage, ahead in zip(stages + [None], ((), (1, 2), (3,), (4,), (5, 6, 7))):
                    for j in ahead:
                        q = QUADS_C * (n - 1) + j
                        if 0 <= q < QUADS and (n or j == QUADS_C):
                            copy_parts(q, q % 2)
                    if stage:
                        stage(n)
            normed[0] += NC
            act.wait_ge(state_spread, 1)
            act.activation(x_state, buf_b, ACT.Copy).then_inc(state_kept, 1)
            act.wait_ge(count_known, 1)

            def layers(vw):
                norm(slots_norm(x_state, buf_a, buf_c))
                norm(live_norm(vw))
                first_then_second(act, copy_turned(1, 2), take(1))
                edge_norm()
                first_then_second(act, copy_turned(2, 1), take(2))
                edge_norm()
                norm(live_norm(vw))
                norm(live_norm(vw))
                act.wait_ge(exp_ready, 1)
                act.activation(buf_b, buf_b, ACT.Exp).then_inc(exp_done, 1)
                first_then_second(act, copy_turned(3, 1), hidden)
                normed[0] = NC

            narrow_or_wide(act, layers)

        @block.gpsimd
        def _(gp):
            gp.iota(edge_id[:, 0:TILES], pattern=[[1, TILES]], base=0, channel_multiplier=TILES)\
                .then_inc(iotas, 1)
            gp.iota(edge_id[:, TILES:SORT_C], pattern=[[1, SORT_C - TILES]], base=SLOTS,
                    channel_multiplier=SORT_C - TILES).then_inc(iotas, 1)
            gp.iota(slot_id[:, :], pattern=[[1, TILES]], base=0, channel_multiplier=TILES).then_inc(iotas, 1)
            gp.iota(lo_iota[:, :], pattern=[[1, LOS]], base=0, channel_multiplier=0,
                    allow_small_or_imprecise_dtypes=True).then_inc(iotas, 1)
            gp.iota(col_i[:, :], pattern=[[1, SORT_C]], base=0, channel_multiplier=0).then_inc(iotas, 1)
            gp.iota(part_i[:, :], pattern=[[1, 1]], base=0, channel_multiplier=1).then_inc(iotas, 1)
            gp.memset(ident[:, :], 0.0).then_inc(ident_made, 1)
            gp.memset(ones_full[:, :], 1.0).then_inc(ident_made, 1)
            gp.memset(upper[:, :], 1.0).then_inc(ident_made, 1)
            gp.memset(ident_half[:, :], 0.0).then_inc(ident_made, 1)
            gp.wait_ge(ident_made, 4)
            gp.affine_select(out=ident_half[:, :], in_=ident_half[:, :], compare_op=ALU.not_equal, fill=1.0,
                             base=0, pattern=[[-1, P]], channel_multiplier=1).then_inc(ident_made, 1)
            gp.affine_select(out=upper[:, :], in_=upper[:, :], compare_op=ALU.is_ge, fill=0.0, base=0,
                             pattern=[[1, P]], channel_multiplier=-1).then_inc(ident_made, 1)
            gp.affine_select(out=ident[:, :], in_=ident[:, :], compare_op=ALU.not_equal, fill=1.0, base=0,
                             pattern=[[-1, P]], channel_multiplier=1).then_inc(ident_made, 1)
            gp.affine_select(out=ones_full[:, :], in_=ones_full[:, :], compare_op=ALU.is_gt, fill=0.0,
                             base=FULL_P, pattern=[[0, P]], channel_multiplier=-1).then_inc(ident_made, 1)

            def gather(to, table, index, t, signal):
                gp.indirect_dma_start(out=to, out_offset=None, in_=table,
                                      in_offset=bass.IndirectOffsetOnAxis(ap=index[:, t:t + 1], axis=0),
                                      bounds_check=table.shape[0] - 1,
                                      oob_is_err=False).then_inc(signal, 16)

            def scatter(table, index, of, t, signal):
                gp.indirect_dma_start(out=table, in_=of, in_offset=None,
                                      out_offset=bass.IndirectOffsetOnAxis(ap=index[:, t:t + 1], axis=0),
                                      bounds_check=table.shape[0] - 1, oob_is_err=False).then_inc(signal, 16)

            gp.wait_ge(edges_blank, 1)
            gp.wait_ge(src_in, 16 * 4)
            for t in range(TILES):
                gather(packed[:, t, X_AT:ROW], x, src_raw, t, got_xs)
            gp.wait_ge(rows_stored, 16)
            gp.wait_ge(src_known, 1)
            for t in range(TILES):
                gather(rows[:, t, :], edge_rows, row_index, t, got_rows)
            gp.wait_ge(dst_known, 1)
            for n in range(2):
                gp.wait_ge(padded_stored[n], 16 * ((XCH + 2 - n) // 2))
            for t in range(TILES):
                gather(x_dst_rows[:, t, :], nodes_x, dst_index, t, got_dst[t // CHUNK])
            gp.wait_ge(h_stored, 16)
            gp.wait_ge(zeros_stored, 16 * 8)
            gp.wait_ge(state_stored, 16)
            gp.wait_ge(count_known, 1)

            def layers(vw):
                gathers, puts_h, puts_y = [0], [0], [0]

                def at_live(buf, table):
                    for j in range(1, 1 + vw):
                        gather(buf[:, j, :], table, live_last, j, got_live)

                def put_h():
                    puts_h[0] += 1
                    gp.wait_ge(h_made, puts_h[0])
                    for j in range(1, 1 + vw):
                        scatter(h_table, live_slot, wide_b[:, j, :], j, h_put)
                    gp.wait_ge(h_put, 16 * vw * puts_h[0])

                def put_y(table):
                    puts_y[0] += 1
                    gp.wait_ge(y_made, puts_y[0])
                    for j in range(vw + 2):
                        scatter(table, live_y, wide_b[:, j, :], j, y_put)
                    gp.wait_ge(y_put, 16 * (vw + 2) * puts_y[0])

                gp.wait_ge(last_listed, 1)
                at_live(x_live, x1_table)
                gp.wait_ge(slot_listed, 1)
                put_h()
                gp.wait_ge(state_stored, 16 * 2)
                at_live(x_live, x2_table)
                put_h()
                gp.wait_ge(state_stored, 16 * 3)
                at_live(wide_b, y1_table)
                gp.wait_ge(y_listed, 1)
                put_y(y2_table)
                at_live(wide_b, y2_table)
                put_y(y3_table)
                at_live(wide_b, y3_table)
                put_h()
                for n in range(2):
                    gp.wait_ge(x_stored[n], 16 * ((XCH + 2 - n) // 2))
                for t in range(TILES):
                    if t % 4 == 0:
                        gp.wait_ge(lin_used, 3 * QUADS + t // 4 + 3)
                    scatter(out, tail_index, x_state[:, t, :], t, out_rows)
                gp.wait_ge(out_rows, 16 * TILES)

            narrow_or_wide(gp, layers)

        @block.vector
        def _(v):
            steps = [0]

            def step(ins):
                steps[0] += 1
                ins.then_inc(dve_step, 1)

            def settle():
                v.wait_ge(dve_step, steps[0])

            def link(ins):
                step(ins)
                settle()

            small = [0]

            def pe_does():
                small[0] += 1
                v.sem_inc(to_pe, 1)
                v.wait_ge(from_pe, small[0])

            def over_t(a, n):
                return a.unsqueeze(1).to_broadcast([P, n, D])

            step(v.memset(key_i[:, :], NODES))
            step(v.memset(src_raw[:, :], NODES))
            settle()
            v.sem_inc(keys_blank, 1)
            step(v.memset(attr_in, 0.0))
            step(v.memset(key_prev[:, :], 0.0))
            step(v.memset(dst_index[:, :], 0))
            step(v.memset(packed, 0.0))
            settle()
            v.sem_inc(edges_blank, 1)
            step(v.memset(zero1[:, :], 0.0))
            step(v.memset(ones[:, :], 1.0))
            step(v.memset(eps_c[:, :], LN_EPS))
            step(v.memset(ones_wide, 1.0))
            for t in (w1s_bd, w1d_bd, w2_bd, w3a_bd, w3b_bd):
                step(v.memset(t[:, :], 0.0))
            settle()
            v.sem_inc(blocks_blank, 1)
            v.sem_inc(bond_step, STEPS)
            v.sem_inc(lin_used, 2)

            v.wait_ge(iotas, 6)
            v.wait_ge(src_in, 16 * 4)
            link(v.tensor_copy(key_a[:, :], key_i[:, :]))
            step(v.tensor_scalar(key_b[:, :], key_a[:, :], -1.0, float(HALF - 1), ALU.mult, ALU.add))
            step(v.tensor_scalar(key_t[:, :], key_a[:, :], float(HALF), None, ALU.is_lt))
            step(v.tensor_scalar(tail_index[:, :], key_i[:, 0:TILES], P - 1, None, ALU.bitwise_and))
            step(v.tensor_scalar(row_index[:, :], key_i[:, 0:TILES], P.bit_length() - 1, None,
                                 ALU.logical_shift_right))
            settle()
            step(v.tensor_copy(src_hi[:, :], tail_index[:, :]))
            step(v.tensor_copy(src_lo[:, :], row_index[:, :]))
            link(v.scalar_tensor_tensor(key_a[:, :], key_a[:, :], -float(HALF), key_b[:, :], ALU.add, ALU.max))
            link(v.tensor_scalar(key_i[:, :], key_a[:, :], float(LIFT), None, ALU.add))
            link(v.tensor_scalar(key_i[:, :], key_i[:, :], ID_BITS, None, ALU.logical_shift_left))
            link(v.tensor_scalar(key_t[:, :], key_t[:, :], 31, None, ALU.logical_shift_left))
            link(v.tensor_tensor(key_i[:, :], key_i[:, :], edge_id[:, :], ALU.bitwise_or))
            link(v.tensor_tensor(key_a[:, :].bitcast(I32), key_i[:, :], key_t[:, :], ALU.bitwise_or))
            for n in range(COL_LEVELS):
                link(v.tensor_scalar(key_t[:, :], col_i[:, :], 2 << n, None, ALU.bitwise_and))
                link(v.tensor_scalar(sign_col[:, n, :], key_t[:, :], -1.0 / (1 << n), 1.0, ALU.mult, ALU.add))
            for n in range(PART_LEVELS):
                link(v.tensor_scalar(part_t[:, :], part_i[:, :], 1 << n, None, ALU.bitwise_and))
                link(v.tensor_scalar(sign_part[:, n:n + 1], part_t[:, :], -2.0 / (1 << n), 1.0,
                                     ALU.mult, ALU.add))

            v.wait_ge(edges_in, 16 * 6)
            step(v.tensor_copy(packed[:, :, 0:BOND], attr_in))
            step(v.tensor_copy(packed[:, :, W_AT], key_prev[:, :]))
            step(v.tensor_copy(packed[:, :, DST_AT], dst_index[:, :]))
            settle()
            v.sem_inc(packed_done, 1)

            pair = [key_a, key_b]

            def flip(level):
                a, b = pair
                if level <= COL_LEVELS:
                    link(v.tensor_tensor(b[:, :], a[:, :], sign_col[:, level - 1, :], ALU.mult))
                else:
                    n = level - COL_LEVELS - 1
                    link(v.tensor_scalar(b[:, :], a[:, :], sign_part[:, n:n + 1], None, ALU.mult))
                pair.reverse()

            def exchange(distance):
                a, b = (k[:, :].rearrange("p (b h d) -> p b h d", h=2, d=distance) for k in pair)
                step(v.tensor_tensor(b[:, :, 0], a[:, :, 0], a[:, :, 1], ALU.min))
                link(v.tensor_tensor(b[:, :, 1], a[:, :, 0], a[:, :, 1], ALU.max))
                pair.reverse()

            def turn_keys():
                pe_does()
                link(v.tensor_copy(pair[1][:, :], ps_key))
                pair.reverse()

            for level in range(1, ID_BITS + 1):
                if level < ID_BITS:
                    flip(level)
                distance = 1 << (level - 1)
                if distance >= SORT_C:
                    turn_keys()
                    while distance >= SORT_C:
                        exchange(distance // SORT_C)
                        distance //= 2
                    turn_keys()
                while distance:
                    exchange(distance)
                    distance //= 2
                if level < ID_BITS:
                    flip(level)
            assert pair[0] is key_sorted
            v.sem_inc(sorted_done, 1)

            v.wait_ge(keys_back, 16 * 3)
            here, prev, nxt = (k[:, :].bitcast(I32) for k in (key_here, key_prev, key_next))
            link(v.tensor_scalar(row_index[:, :], here, SORT_N - 1, None, ALU.bitwise_and))
            for k in (here, prev, nxt):
                step(v.tensor_scalar(k, k, ID_BITS, None, ALU.logical_shift_right))
            settle()
            step(v.tensor_tensor(goes_on[:, :], here, prev, ALU.is_equal))
            step(v.tensor_tensor(not_tail[:, :], here, nxt, ALU.is_equal))
            settle()
            half_bit = 31 - ID_BITS
            step(v.tensor_scalar(prev, here, half_bit, None, ALU.logical_shift_right))
            step(v.tensor_scalar(nxt, here, (1 << half_bit) - 1, None, ALU.bitwise_and))
            settle()
            link(v.tensor_scalar(mean[:, :], prev, -2.0, 1.0, ALU.mult, ALU.add))
            link(v.scalar_tensor_tensor(mean[:, :], nxt, -float(LIFT), mean[:, :], ALU.add, ALU.mult))
            link(v.scalar_tensor_tensor(mean[:, :], prev, -1.0, mean[:, :], ALU.mult, ALU.add))
            link(v.tensor_scalar(src_index[:, :], mean[:, :], float(HALF), None, ALU.add))
            v.sem_inc(src_known, 1)
            step(v.scalar_tensor_tensor(tail_index[:, :], not_tail[:, :], float(NOWHERE), src_index[:, :],
                                        ALU.mult, ALU.add))
            step(v.tensor_scalar(is_tail[:, :], not_tail[:, :], -1.0, 1.0, ALU.mult, ALU.add))
            step(v.tensor_scalar(goes_on_neg[:, :], goes_on[:, :], 1.0, BIG, ALU.subtract, ALU.mult))
            step(v.tensor_tensor_scan(from_prev[:, :], goes_on[:, :], goes_on[:, :], 1.0,
                                      op0=ALU.mult, op1=ALU.mult))
            step(v.tensor_tensor_scan(from_next[:, ::-1], not_tail[:, ::-1], not_tail[:, ::-1], 1.0,
                                      op0=ALU.mult, op1=ALU.mult))
            settle()
            link(v.tensor_scalar(from_prev_neg[:, :], from_prev[:, :], 1.0, BIG, ALU.subtract, ALU.mult))
            link(v.tensor_copy(wide[:, :], from_prev[:, TILES - 1:TILES].to_broadcast([P, D])))
            pe_does()
            link(v.tensor_copy(whole[:, :], ps_small[0:D, :]))
            link(v.tensor_scalar(whole_neg[:, :], whole[:, :], 1.0, BIG, ALU.subtract, ALU.mult))
            link(v.tensor_copy(wide[:, :], from_next[:, 0:1].to_broadcast([P, D])))
            pe_does()
            link(v.tensor_copy(whole_next[:, :], ps_small[0:D, :]))

            def hot(t, s):
                v.wait_ge(hot_used, t + 1)
                v.tensor_scalar(hot_lo[s][:, :], lo_iota[:, :], src_lo[:, bass.ds(t, 1)], None, ALU.is_equal)\
                    .then_inc(hot_made, 1)
                v.tensor_scalar(hot_hi[s][:, :], lo_iota[:, 0:P], src_hi[:, bass.ds(t, 1)], None, ALU.is_equal)\
                    .then_inc(hot_made, 1)

            with v.Fori(0, TILES // HOT_LOOP) as i:
                for j in range(HOT_LOOP):
                    hot(i * HOT_LOOP + j, j % HOT)
            v.wait_ge(counted, 1)
            for h in range(2):
                step(v.tensor_copy(cnt[:, h * LO_H:(h + 1) * LO_H], ps_o[h][:, :, :].rearrange(
                    "p a b -> p (a b)")[:, 0:LO_H]))
            settle()
            pe_does()
            for h in range(2):
                part = slice(h * LO_H, (h + 1) * LO_H)
                step(v.tensor_copy(tot[:, part], ps_u[1][:, h, 0:LO_H]))
            settle()
            link(v.tensor_tensor_scan(run, ones_wide, tot, -1.0, op0=ALU.mult, op1=ALU.add))
            link(v.tensor_tensor(run, run, tot, ALU.subtract))
            for h in range(2):
                part = slice(h * LO_H, (h + 1) * LO_H)
                step(v.tensor_tensor(run[:, part], run[:, part], ps_u[0][:, h, 0:LO_H], ALU.add))
            step(v.tensor_scalar(cnt, cnt, 0.0, float(NOWHERE), ALU.is_equal, ALU.mult))
            settle()
            link(v.tensor_tensor(run, run, cnt, ALU.add))
            pe_does()
            for b in range(-(-LOS // P)):
                w = min(P, LOS - b * P)
                step(v.tensor_copy(turned_last[0:w, b * P:(b + 1) * P], ps_t[b // 4][0:w, b % 4, :]))
            settle()
            v.sem_inc(last_made, 1)

            v.wait_ge(weights_in, 16 * len(weight_loads))
            link(v.tensor_scalar(rb3a[:, :], b3a_c[0:H2, :], 0.0, None, ALU.max))
            link(v.tensor_copy(rb3a_w[:, :], rb3a[:, :].to_broadcast([H2, P])))
            pe_does()
            link(v.tensor_copy(idle_row[:, :], ps_small[:, 0:D]))
            for c in range(XCH):
                v.wait_ge(x_padded, 2 * c + 2)
                ring = x_ring[c % 2][:, :].rearrange("p (r d) -> p r d", d=D)
                link(v.tensor_tensor(ring, ring, over_t(idle_row[:, :], XROWS), ALU.add))
                v.sem_inc(x_added, 1)
            v.wait_ge(x_padded, 2 * XCH + 2)
            left = x_ring[XCH % 2][0:XLEFT, 0:D]
            link(v.tensor_tensor(left, left, idle_row[0:XLEFT, :], ALU.add))
            v.sem_inc(x_added, 1)

            for n in range(2):
                v.wait_ge(x_stored[n], 16 * ((XCH + 2 - n) // 2))
            link(v.memset(x_ring[0][:, 0:ZEROS], 0.0))
            v.sem_inc(zeros_made, 1)

            v.wait_ge(got_rows, 16 * TILES)
            step(v.tensor_copy(dst_index[:, :], rows[:, :, DST_AT]))
            step(v.tensor_copy(weight_s[:, :], rows[:, :, W_AT]))
            settle()
            v.sem_inc(dst_known, 1)

            normed = [0]

            def centre(parts, n):
                of, to, _, m, _ = parts[n]
                link(v.tensor_reduce(out=m, in_=of, op=ALU.add, axis=AX.X))
                link(v.tensor_scalar(m, m, 1.0 / D, None, ALU.mult))
                link(v.tensor_tensor(to, of, bcast(m, D), ALU.subtract))
                v.sem_inc(centred, 1)

            def spread(parts, n):
                v.wait_ge(squared, normed[0] + n + 1)
                link(v.tensor_reduce(out=parts[n][4], in_=parts[n][2], op=ALU.add, axis=AX.X))
                v.sem_inc(root_ready, 1)

            def scale(parts, n):
                _, to, _, _, var_n = parts[n]
                v.wait_ge(rooted, normed[0] + n + 1)
                link(v.reciprocal(var_n, var_n))
                link(v.scalar_tensor_tensor(to, to, 0.0, bcast(var_n, D), ALU.max, ALU.mult))

            def layer_norm(parts):
                for n in range(len(parts) + 2):
                    if n < len(parts):
                        centre(parts, n)
                    if 1 <= n <= len(parts):
                        spread(parts, n - 1)
                    if n >= 2:
                        scale(parts, n - 2)
                normed[0] += len(parts)

            def over_edges(buf):
                by_channel = buf[:, :, :].rearrange("p t d -> p d t")
                step(v.tensor_reduce(out=sums[:, 0, :], in_=by_channel[:, :, 0:REST], op=ALU.add, axis=AX.X))
                step(v.tensor_reduce(out=sums[:, 1, :], in_=by_channel[:, :, REST:TILES], op=ALU.add, axis=AX.X))
                settle()
                pe_does()

            def batch_norm(n, to):
                over_edges(buf_c)
                link(v.tensor_scalar(bn_mean[:, :], ps_small[:, 0:D], 1.0 / EDGES, None, ALU.mult))
                for a, b in CHUNKS:
                    link(v.tensor_tensor(buf_c[:, a:b], buf_c[:, a:b], over_t(bn_mean[:, :], b - a), ALU.subtract))
                    v.sem_inc(centred, 1)
                v.wait_ge(squared, normed[0] + NC)
                over_edges(buf_b)
                link(v.tensor_copy(bn_scale[:, :], ps_small[:, 0:D]))
                v.sem_inc(root_ready, NC)
                v.wait_ge(rooted, normed[0] + NC)
                normed[0] += NC
                link(v.reciprocal(bn_scale[:, :], bn_scale[:, :]))
                link(v.tensor_tensor(bn_scale[:, :], bn_scale[:, :], bn_par[:, 2 * n, :], ALU.mult))
                link(v.tensor_tensor(buf_c, buf_c, over_t(bn_scale[:, :], TILES), ALU.mult))
                link(v.tensor_tensor(buf_c, buf_c, over_t(bn_par[:, 2 * n + 1, :], TILES), ALU.add))
                link(v.tensor_scalar(to, buf_c, 0.0, None, ALU.max))

            def group_prefix(buf, largest=False, live_sums=False):
                on, inside, came, start, ops = (
                    (goes_on_neg, whole_neg, from_prev_neg, -BIG, (ALU.add, ALU.max)) if largest else
                    (goes_on, whole, from_prev, 0.0, (ALU.mult, ALU.add)))
                if live_sums:
                    on, inside, came = live_goes[:, 0:buf.shape[1]], live_whole, live_from[:, 0:buf.shape[1]]
                else:
                    on, came = on[:, :], came[:, :]
                for d in range(D):
                    step(v.tensor_tensor_scan(buf[:, :, d], on, buf[:, :, d], start,
                                              op0=ops[0], op1=ops[1]))
                step(v.memset(carry_t[:, 0:1], start))
                settle()
                pe_does()
                link(v.tensor_tensor_scan(carry_t[:, 1:P + 1], inside[:, :], ps_small[0:D, :], start,
                                          op0=ops[0], op1=ops[1]))
                pe_does()
                link(v.tensor_copy(carry[:, :], ps_small[:, 0:D]))
                for d in range(D):
                    step(v.scalar_tensor_tensor(buf[:, :, d], came, carry[:, d:d + 1], buf[:, :, d],
                                                ops[0], ops[1]))
                settle()

            def carry_back():
                link(v.memset(carry_t[:, P:P + 1], 0.0))
                pe_does()
                link(v.tensor_tensor_scan(carry_t[:, 0:P][:, ::-1], whole_next[:, ::-1],
                                          ps_small[0:D, ::-1], 0.0, op0=ALU.mult, op1=ALU.add))
                pe_does()
                link(v.tensor_copy(carry[:, :], ps_small[:, 0:D]))

            def tails_back(to, of):
                link(v.tensor_tensor(to[:, :, :], of[:, :, :], bcast(is_tail[:, :], D), ALU.mult))
                for d in range(D):
                    step(v.tensor_tensor_scan(to[:, ::-1, d], not_tail[:, ::-1], to[:, ::-1, d], 0.0,
                                              op0=ALU.mult, op1=ALU.add))
                settle()
                carry_back()
                for d in range(D):
                    step(v.scalar_tensor_tensor(to[:, :, d], from_next[:, :], carry[:, d:d + 1], to[:, :, d],
                                                ALU.mult, ALU.add))
                settle()

            def bond_quad(q, s):
                for h in range(2):
                    t = q * 4 + 2 * h
                    done = STEPS * q + STEPS + 2 * h
                    v.wait_ge(bond_mm, q * 2 + h + 1)
                    v.tensor_tensor(prod[:, :, :].rearrange("p t (k i) -> p t k i", k=BOND),
                                    ps_u[h][:, :, :].rearrange("p t (k i) -> p t k i", k=BOND),
                                    bcast(rows[:, bass.ds(t, 2), 0:BOND], D), ALU.mult).then_inc(bond_step, 1)
                    v.wait_ge(bond_step, done + 1)
                    v.tensor_reduce(out=buf_c[:, bass.ds(t, 2), :],
                                    in_=prod[:, :, :].rearrange("p t (k i) -> p t i k", k=BOND),
                                    op=ALU.add, axis=AX.X).then_inc(bond_step, 1)
                    v.wait_ge(bond_step, done + 2)
                v.wait_ge(lin_mm, q + 3)
                v.tensor_tensor(quad(buf_c, q), quad(buf_c, q), ps_o[s][:, 0, :], ALU.add)\
                    .then_inc(bond_step, 1)
                v.wait_ge(bond_step, STEPS * q + 2 * STEPS)

            w, b = bond_in.rearrange("p (a f) -> p a f", a=1), bias_in.rearrange("p (a f) -> p a f", a=1)
            for n in range(PARTS):
                step(v.tensor_copy(bond_parts[:, n:n + 1, :], w))
                step(v.tensor_copy(bias_parts[:, n:n + 1, :], b))
                settle()
                if n + 1 < PARTS:
                    step(v.tensor_tensor(w, w, bond_parts[:, n:n + 1, :], ALU.subtract))
                    step(v.tensor_tensor(b, b, bias_parts[:, n:n + 1, :], ALU.subtract))
                    settle()
            v.wait_ge(zeros_stored, 16 * 8)

            def rest(n):
                a, b = CHUNKS[n]
                v.wait_ge(parts_first, n + 1)
                link(v.tensor_tensor(buf_c[:, a:b], buf_a[:, a:b], norm_parts[n % 2][:, :, 0], ALU.subtract))
                v.sem_inc(rest_made, 1)

            def third_parts(n):
                a, b = CHUNKS[n]
                v.wait_ge(parts_second, n + 1)
                link(v.tensor_tensor(norm_parts[n % 2][:, :, 2], buf_c[:, a:b], norm_parts[n % 2][:, :, 1],
                                     ALU.subtract))
                v.sem_inc(parts_made, 1)

            def scale_first(n):
                scale(NORM0, n)
                v.sem_inc(input_ready, 1)

            for n in range(NC + 1):
                if n < NC:
                    v.wait_ge(got_dst[n], 16 * CHUNK)
                    centre(NORM0, n)
                stages = (lambda n: spread(NORM0, n), scale_first, rest, third_parts, lambda n: None)
                for stage, quads in zip(stages, ((0, 1), (2,), (3,), (4,), (5, 6))):
                    for j in quads:
                        q = QUADS_C * (n - 1) + j
                        if n:
                            bond_quad(q, q % 2)
                    if n < NC:
                        stage(n)
            normed[0] += NC
            v.sem_inc(lin_used, QUADS)
            link(v.tensor_copy(dst_last[:, :], x_dst_rows[:, :, D]))
            step(v.tensor_scalar(live[:, :], dst_last[:, :], float(SLOTS), None, ALU.is_lt))
            step(v.tensor_scalar(var[:, :], src_index[:, :], float(NODES), None, ALU.is_lt))
            settle()
            link(v.tensor_tensor(live[:, :], live[:, :], var[:, :], ALU.mult))
            link(v.tensor_reduce(out=mean[:, 0:1], in_=live[:, :], op=ALU.add, axis=AX.X))
            link(v.tensor_copy(wide[:, :], mean[:, 0:1].to_broadcast([P, D])))
            pe_does()
            link(v.tensor_reduce(out=mean[0:D, 0:1], in_=ps_small[0:D, :], op=ALU.max, axis=AX.X))
            link(v.tensor_copy(count_i[:, :], mean[0:D, 0:1]))
            group_prefix(buf_c)
            v.wait_ge(h_stored, 16)
            link(v.tensor_tensor(buf_a, x_src, buf_c, ALU.add))
            v.sem_inc(state_made, 1)
            tails_back(buf_b, buf_a)
            v.sem_inc(state_spread, 1)
            v.sem_inc(count_known, 1)

            def to_live(payload, bits, vw):
                work = key_b[:, 0:TILES]
                link(v.tensor_tensor(work, payload, live[:, :], ALU.mult))
                link(v.scalar_tensor_tensor(work, var[:, :], float(1 << bits), work, ALU.mult, ALU.add))
                rounds = -(-vw // 8)
                for r in range(rounds):
                    top = key_a[:, 8 * r:8 * r + 8]
                    link(v.max(top, work))
                    if r + 1 < rounds:
                        link(v.match_replace(out=work, in_to_replace=top, in_values=work, imm_value=0.0))
                link(v.tensor_copy(key_i[:, 0:vw], key_a[:, 0:vw]))

            def list_live(vw):
                entries = slice(1, 1 + vw)
                keys, part = key_i[:, 0:vw], key_t[:, 0:vw]
                step(v.tensor_copy(mean[:, :], dst_last[:, :]))
                step(v.tensor_copy(row_base[:, :], slot_id[:, 0:1]))
                step(v.tensor_scalar(var[:, :], col_i[:, 0:TILES], -1.0, float(TILES), ALU.mult, ALU.add))
                settle()
                link(v.tensor_tensor(var[:, :], var[:, :], live[:, :], ALU.mult))
                to_live(mean[:, :], ID_BITS, vw)
                step(v.tensor_scalar(live_empty[:, entries], keys, 0.0, None, ALU.is_equal))
                step(v.tensor_scalar(part, keys, SORT_N - 1, None, ALU.bitwise_and))
                settle()
                link(v.scalar_tensor_tensor(live_last[:, entries], live_empty[:, entries], float(NOWHERE), part,
                                            ALU.mult, ALU.add))
                v.sem_inc(last_listed, 1)
                link(v.tensor_scalar(part, keys, ID_BITS, None, ALU.logical_shift_right))
                link(v.tensor_scalar(live_t[:, entries], part, -1.0, float(TILES), ALU.mult, ALU.add))
                link(v.tensor_scalar(live_t[:, entries], live_t[:, entries], row_base[:, :], None, ALU.add))
                link(v.scalar_tensor_tensor(live_slot[:, entries], live_empty[:, entries], float(NOWHERE),
                                            live_t[:, entries], ALU.mult, ALU.add))
                v.sem_inc(slot_listed, 1)
                bits = weight_s[:, :].bitcast(I32)
                link(v.tensor_scalar(key_t[:, 0:TILES], bits, 16, None, ALU.logical_shift_right))
                link(v.tensor_copy(mean[:, :], key_t[:, 0:TILES]))
                to_live(mean[:, :], 16, vw)
                link(v.tensor_scalar(live_w.bitcast(I32)[:, entries], keys, 16, None, ALU.logical_shift_left))
                link(v.tensor_scalar(key_t[:, 0:TILES], bits, (1 << 16) - 1, None, ALU.bitwise_and))
                link(v.tensor_copy(mean[:, :], key_t[:, 0:TILES]))
                to_live(mean[:, :], 16, vw)
                link(v.tensor_scalar(keys, keys, (1 << 16) - 1, None, ALU.bitwise_and))
                link(v.tensor_tensor(live_w.bitcast(I32)[:, entries], live_w.bitcast(I32)[:, entries], keys,
                                     ALU.bitwise_or))
                link(v.tensor_copy(mean[:, :], slot_id[:, :]))
                link(v.tensor_tensor(mean[:, :], mean[:, :], is_tail[:, :], ALU.mult))
                link(v.tensor_tensor_scan(own_tail[:, ::-1], not_tail[:, ::-1], mean[:, ::-1], 0.0,
                                          op0=ALU.mult, op1=ALU.add))
                link(v.tensor_copy(wide[:, :], own_tail[:, 0:1].to_broadcast([P, D])))
                carry_back()
                link(v.scalar_tensor_tensor(own_tail[:, :], from_next[:, :], carry[:, 0:1], own_tail[:, :],
                                            ALU.mult, ALU.add))
                to_live(own_tail[:, :], ID_BITS, vw)
                link(v.tensor_scalar(part, keys, SORT_N - 1, None, ALU.bitwise_and))
                link(v.tensor_tensor(live_ids[:, entries], part, live_empty[:, entries], ALU.subtract))
                link(v.tensor_scalar(live_ids[:, 0:1], own_tail[:, 0:1], 1.0, None, ALU.add))
                link(v.tensor_tensor(live_ids[:, 0:1], live_ids[:, 0:1], goes_on[:, 0:1], ALU.mult))
                link(v.tensor_scalar(live_ids[:, 0:1], live_ids[:, 0:1], -1.0, None, ALU.add))
                link(v.tensor_tensor_scan(live_ids[:, 0:1 + vw], live_ids[:, 0:1 + vw], live_ids[:, 0:1 + vw],
                                          -1.0, op0=ALU.max, op1=ALU.max))
                link(v.tensor_copy(live_ids[:, vw + 1:vw + 2], own_tail[:, TILES - 1:TILES]))
                ve = vw + 2
                step(v.memset(live_goes[:, 0:1], 1.0))
                step(v.tensor_tensor(live_goes[:, 1:ve], live_ids[:, 1:ve], live_ids[:, 0:ve - 1], ALU.is_equal))
                settle()
                step(v.tensor_copy(live_t[:, 0:ve - 1], live_goes[:, 1:ve]))
                step(v.tensor_copy(live_t[:, ve - 1:ve], not_tail[:, TILES - 1:TILES]))
                step(v.tensor_scalar(live_empty[:, 0:ve], live_ids[:, 0:ve], 0.0, None, ALU.is_lt))
                step(v.tensor_tensor_scan(live_from[:, 0:ve], live_goes[:, 0:ve], live_goes[:, 0:ve], 1.0,
                                          op0=ALU.mult, op1=ALU.mult))
                settle()
                link(v.tensor_tensor(live_t[:, 0:ve], live_t[:, 0:ve], live_empty[:, 0:ve], ALU.add))
                link(v.scalar_tensor_tensor(live_y[:, 0:ve], live_t[:, 0:ve], float(NOWHERE), live_ids[:, 0:ve],
                                            ALU.mult, ALU.add))
                v.sem_inc(y_listed, 1)
                link(v.tensor_copy(wide[:, :], live_from[:, ve - 1:ve].to_broadcast([P, D])))
                pe_does()
                link(v.tensor_copy(live_whole[:, :], ps_small[0:D, :]))

            def layers(vw):
                entries = slice(1, 1 + vw)
                passes = [0]

                def live_arrived():
                    passes[0] += 1
                    v.wait_ge(got_live, 16 * vw * passes[0])

                link(v.memset(x_live[:, 0:vw + 2], 0.0))
                list_live(vw)

                v.wait_ge(h_stored, 16)
                v.wait_ge(state_kept, 1)
                v.wait_ge(state_stored, 16)
                layer_norm(slots_norm(x_state, buf_a, buf_c))
                live_arrived()
                layer_norm(live_norm(vw))
                v.sem_inc(h_made, 1)
                v.wait_ge(h_back, 16)
                v.sem_inc(input_ready, 1)
                v.wait_ge(lin_used, 2 * QUADS + 2)
                batch_norm(0, buf_a)
                v.sem_inc(input_ready, 1)
                v.wait_ge(lin_used, 3 * QUADS + 2)
                batch_norm(1, buf_c)
                group_prefix(buf_c)
                link(v.tensor_tensor(x_state, x_state, buf_c, ALU.add))
                v.sem_inc(state_made, 1)

                live_arrived()
                layer_norm(live_norm(vw))
                v.sem_inc(h_made, 1)
                v.wait_ge(h_back, 32)
                link(v.tensor_tensor(buf_c, buf_a, bcast(weight_s[:, :], D), ALU.mult))
                group_prefix(buf_c)
                v.sem_inc(state_made, 1)
                for turn in range(2):
                    live_arrived()
                    step(v.tensor_tensor(wide_b[:, entries], wide_b[:, entries], bcast(live_w[:, entries], D),
                                         ALU.mult))
                    step(v.memset(wide_b[:, 0], 0.0))
                    step(v.memset(wide_b[:, vw + 1], 0.0))
                    settle()
                    group_prefix(wide_b[:, 0:vw + 2], live_sums=True)
                    v.sem_inc(y_made, 1)
                live_arrived()
                link(v.tensor_tensor(x_live[:, entries], x_live[:, entries], wide_b[:, entries], ALU.add))
                v.wait_ge(state_stored, 16 * 3)
                layer_norm(live_norm(vw))
                v.sem_inc(h_made, 1)
                v.wait_ge(y3_back, 16)
                link(v.tensor_tensor(x_state, x_state, buf_c, ALU.add))

                v.wait_ge(h_back, 48)
                link(v.tensor_scalar(buf_a, buf_a, 0.0, MSG_EPS, ALU.max, ALU.add))
                link(v.tensor_scalar(buf_b, buf_a, beta_c[:, :], None, ALU.mult))
                link(v.tensor_copy(buf_c, buf_b))
                group_prefix(buf_c, largest=True)
                tails_back(buf_d, buf_c)
                link(v.tensor_tensor(buf_b, buf_b, buf_d, ALU.subtract))
                v.sem_inc(exp_ready, 1)
                v.wait_ge(exp_done, 1)
                link(v.tensor_tensor(buf_a, buf_a, buf_b, ALU.mult))
                group_prefix(buf_a)
                group_prefix(buf_b)
                link(v.tensor_scalar(buf_b, buf_b, 1e-30, None, ALU.max))
                link(v.reciprocal(buf_b, buf_b))
                link(v.tensor_tensor(buf_a, buf_a, buf_b, ALU.mult))
                v.sem_inc(input_ready, 1)

                def add_quad(q, s):
                    v.wait_ge(lin_mm, 3 * QUADS + q + 3)
                    v.tensor_tensor(quad(x_state, q), quad(x_state, q), ps_o[s][:, 0, :], ALU.add)\
                        .then_inc(lin_used, 1)

                first_then_second(v, add_quad, lambda q, s: None)
                v.wait_ge(lin_used, 4 * QUADS + 2)
                small[0], steps[0], normed[0] = started

            started = (small[0], steps[0], normed[0])
            narrow_or_wide(v, layers)

        @block.tensor
        def _(pe):
            small = [0]

            def asked():
                small[0] += 1
                pe.wait_ge(to_pe, small[0])

            def turn_keys(keys):
                asked()
                pe.transpose(ps_t[0][:, 0, :], keys[:, 0:P], ident[:, :])
                pe.transpose(ps_t[0][:, 1, :], keys[:, P:2 * P], ident[:, :]).then_inc(from_pe, 1)

            def turn_wide(a):
                asked()
                pe.transpose(ps_small[0:D, :], a, ident[:, :]).then_inc(from_pe, 1)

            def turn_back(a):
                asked()
                pe.transpose(ps_small[:, 0:D], a, ident[0:D, 0:D]).then_inc(from_pe, 1)

            def group_carry(buf, last=TILES - 1):
                turn_wide(buf[:, last, :])
                turn_back(carry_t[:, 0:P])

            def tail_carry(buf):
                turn_wide(buf[:, 0, :])
                turn_back(carry_t[:, 1:P + 1])

            def over_edges():
                asked()
                pe.matmul(ps_small[:, 0:D], ones[:, :], sums[:, 0, :], start=True, stop=False)
                pe.matmul(ps_small[:, 0:D], ones_full[:, :], sums[:, 1, :], start=False, stop=True)\
                    .then_inc(from_pe, 1)

            def turn(stage, *bufs):
                def one(q, s):
                    pe.wait_ge(copied, stage * QUADS + q + 1)
                    for n, buf in enumerate(bufs):
                        last = pe.transpose(ps_t[s][:, n, :], quad(buf, q), ident[:, :])
                    last.then_inc(turned, 1)
                return one

            def ready(stage, q):
                pe.wait_ge(copied, stage * QUADS + q + 3)
                if stage:
                    pe.wait_ge(lin_used, stage * QUADS + q + 1)

            def turn_parts(q, s):
                if q % QUADS_C == 0:
                    pe.wait_ge(parts_made, q // QUADS_C + 1)
                pe.wait_ge(copied, q + 1)
                for t in range(4):
                    parts = norm_parts[q // QUADS_C % 2][:, 4 * q % CHUNK + t].rearrange("p n j -> p (n j)")
                    last = pe.transpose(ps_parts[s][:, t * P:(t + 1) * P], parts, ident_half[:, :])
                last.then_inc(turned, 1)

            def bond_products(q, s):
                ready(0, q)
                for h in range(2):
                    pe.wait_ge(bond_step, STEPS * q + 1 + 2 * h)
                    for t in range(2):
                        norm = parts_t[s][:, (2 * h + t) * P:(2 * h + t + 1) * P]
                        for n in range(PARTS):
                            last = pe.matmul(ps_u[h][:, t, :], norm, bond_parts[:, n, :],
                                             start=n == 0, stop=n == PARTS - 1)
                    last.then_inc(bond_mm, 1)
                pe.wait_ge(bond_step, STEPS * q)
                for t in range(4):
                    norm = parts_t[s][:, t * P:(t + 1) * P]
                    for n in range(PARTS):
                        last = pe.matmul(ps_o[s][:, 0, D * t:D * t + D], norm, bias_parts[:, n, :],
                                         start=n + t == 0, stop=n + t == PARTS + 2)
                last.then_inc(lin_mm, 1)

            def pair_products(q, s):
                ready(1, q)
                pe.matmul(ps_o[s][:, 0, :], ones[0:1, :], b1_row[:, :], start=True, stop=False)
                pe.matmul(ps_o[s][:, 0, :], w_t[s][:, 0, :], w1s_bd[:, :], start=False, stop=False)
                pe.matmul(ps_o[s][:, 0, :], w_t[s][:, 1, :], w1d_bd[:, :], start=False, stop=True)\
                    .then_inc(lin_mm, 1)

            def second_products(q, s):
                ready(2, q)
                pe.matmul(ps_o[s][:, 0, :], ones[0:1, :], b2_row[:, :], start=True, stop=False)
                pe.matmul(ps_o[s][:, 0, :], w_t[s][:, 0, :], w2_bd[:, :], start=False, stop=True)\
                    .then_inc(lin_mm, 1)

            def mlp_products(q, s):
                ready(3, q)
                pe.wait_ge(hid_done, q + 1)
                for u in range(2):
                    r = slice(64 * u, 64 * u + 64)
                    last = pe.matmul(ps_u[s][:, u, 0:P], w3a_bd[r, :], w_t[s][r, 0, :], start=True, stop=True)
                last.then_inc(hid_mm, 1)
                pe.wait_ge(hid_done, q + 3)
                pe.matmul(ps_o[s][:, 0, :], ones[0:1, :], b3b_row[:, :], start=True, stop=False)
                for u in range(2):
                    last = pe.matmul(ps_o[s][:, 0, H2 * u:H2 * u + H2], r_t[s][:, u, :], w3b_bd[:, :],
                                     start=False, stop=u == 1)
                last.then_inc(lin_mm, 1)

            pe.sem_inc(lin_mm, 2)
            pe.sem_inc(hot_used, HOT)
            pe.wait_ge(ident_made, 8)
            for n in range(2 * PART_TURNS):
                turn_keys(key_turned[n])
            turn_wide(wide[:, :])
            turn_wide(wide[:, :])
            def count(t, s, start=False, stop=False):
                pe.wait_ge(hot_made, 2 * t + 2)
                for h in range(2):
                    last = pe.matmul(ps_o[h][:, :, :].rearrange("p a b -> p (a b)")[:, 0:LO_H], hot_hi[s][:, :],
                                     hot_lo[s][:, h * LO_H:(h + 1) * LO_H], start=start, stop=stop)
                last.then_inc(hot_used, 1)

            for j in range(HOT_LOOP):
                count(j, j % HOT, start=j == 0)
            with pe.Fori(1, TILES // HOT_LOOP - 1) as i:
                for j in range(HOT_LOOP):
                    count(i * HOT_LOOP + j, j % HOT)
            for j in range(HOT_LOOP):
                count(TILES - HOT_LOOP + j, j % HOT, stop=j == HOT_LOOP - 1)
            pe.wait_ge(hot_used, TILES + HOT)
            pe.sem_inc(counted, 1)
            asked()
            for h in range(2):
                part = cnt[:, h * LO_H:(h + 1) * LO_H]
                pe.matmul(ps_u[0][:, h, 0:LO_H], upper[:, :], part, start=True, stop=True)
                last = pe.matmul(ps_u[1][:, h, 0:LO_H], ones[:, :], part, start=True, stop=True)
            last.then_inc(from_pe, 1)
            asked()
            for b in range(-(-LOS // P)):
                w = min(P, LOS - b * P)
                last = pe.transpose(ps_t[b // 4][0:w, b % 4, :], run[:, b * P:b * P + w], ident[:, :])
            last.then_inc(from_pe, 1)
            pe.wait_ge(weights_in, 16 * len(weight_loads))
            asked()
            pe.matmul(ps_small[:, 0:D], rb3a_w[:, :], w3b_bd[0:H2, 0:D], start=True, stop=False)
            pe.matmul(ps_small[:, 0:D], ones[0:1, :], b3b_row[:, 0:D], start=False, stop=True).then_inc(from_pe, 1)
            first_then_second(None, turn_parts, bond_products)
            turn_wide(wide[:, :])
            group_carry(buf_c)
            tail_carry(buf_b)
            pe.wait_ge(count_known, 1)

            def layers(vw):
                turn_wide(wide[:, :])
                turn_back(carry_t[:, 1:P + 1])
                turn_wide(wide[:, :])
                pe.wait_ge(input_ready, NC + 1)
                first_then_second(None, turn(1, buf_a, buf_b), pair_products)
                over_edges()
                over_edges()
                pe.wait_ge(input_ready, NC + 2)
                first_then_second(None, turn(2, buf_a), second_products)
                over_edges()
                over_edges()
                group_carry(buf_c)
                group_carry(buf_c)
                for _ in range(2):
                    group_carry(wide_b, vw + 1)
                group_carry(buf_c)
                tail_carry(buf_d)
                group_carry(buf_a)
                group_carry(buf_b)
                pe.wait_ge(input_ready, NC + 3)
                first_then_second(None, turn(3, buf_a), mlp_products)
                small[0] = started

            started = small[0]
            narrow_or_wide(pe, layers)


def kernel(**inputs):
    import numpy as np
    import concourse.bacc as bacc
    from concourse import mybir as mb
    from concourse.bass_utils import run_bass_kernel_spmd as run

    a = {k: np.ascontiguousarray(v) for k, v in inputs.items()}
    a["L0_gnn_kernel"] = np.ascontiguousarray(a["L0_gnn_kernel"].reshape(16, 32, 32).transpose(2, 0, 1)
                                              .reshape(32, 512))
    a["L0_gnn_bias"] = np.ascontiguousarray(a["L0_gnn_bias"].reshape(32, 32).T)
    names = ["x", "src", "dst", "edge_attr_16", "edge_weight", "L0_gnn_kernel", "L0_gnn_bias",
             "L1_gnn_W1", "L1_gnn_b1", "L1_gnn_gamma1", "L1_gnn_beta1", "L1_gnn_W2", "L1_gnn_b2",
             "L1_gnn_gamma2", "L1_gnn_beta2", "L3_gnn_beta", "L3_gnn_W1", "L3_gnn_b1", "L3_gnn_W2", "L3_gnn_b2"]
    nc = bacc.Bacc("TRN2", target_bir_lowering=False, num_devices=1)
    arrays, args = {}, []
    for name in names:
        arrays[f"in_{name}"] = a[name]
        args.append(nc.dram_tensor(f"in_{name}", a[name].shape, mb.dt.from_np(a[name].dtype),
                                   kind="ExternalInput").ap())
    args.append(nc.dram_tensor("out_x", a["x"].shape, mb.dt.float32, kind="ExternalOutput").ap())
    gnn(nc, *args)
    return run(nc, [arrays], core_ids=[0]).results[0]["out_x"]
```

```python
import concourse.bass as bass
from concourse import mybir
from contextlib import ExitStack

FP32 = mybir.dt.float32
I32 = mybir.dt.int32
F16 = mybir.dt.float16
BF16 = mybir.dt.bfloat16
ALU = mybir.AluOpType
ACT = mybir.ActivationFunctionType
AX = mybir.AxisListType

P = 128
D = 32
BOND = 16
H2 = 2 * D
LN_EPS = 1e-05
BN_EPS = 1e-05
MSG_EPS = 1e-07
BIG = 1e38
NOWHERE = 1 << 20


def gnn(nc, x, src, dst, attr, weight, bond_k, bond_b, w1a, b1a, g1a, be1a, w1b, b1b, g1b, be1b,
        beta3, w3a, b3a, w3b, b3b, out):
    NODES = x.shape[0]
    EDGES = src.shape[0]
    TILES = -(-EDGES // (P * 4)) * 4
    SLOTS = P * TILES
    QUADS = TILES // 4
    FULL_P = EDGES // TILES
    REST = EDGES - FULL_P * TILES
    assert FULL_P == P - 1 and 0 < REST < TILES
    SORT_C = 256
    SORT_N = P * SORT_C
    ID_BITS = SORT_N.bit_length() - 1
    HALF = NODES // 2
    LIFT = 1 << (23 - ID_BITS)
    NARROW = 45
    RUN = 16
    W_AT, DST_AT, X_AT = BOND, BOND + 1, BOND + 2
    ROW = X_AT + D
    XROW = D + 1
    LOS = -(-NODES // P)
    LO_H = LOS // 2
    LAST_N = LOS * P
    XROWS = 71
    XCH = (NODES // P) // XROWS
    assert XCH * XROWS == NODES // P
    XLEFT = NODES - P * XCH * XROWS
    HOT = 4
    HOT_LOOP = 28
    LOOP = 16
    CHUNK = 28
    NC = TILES // CHUNK
    QUADS_C = CHUNK // 4
    assert NC * CHUNK == TILES
    PARTS = 3
    KP = PARTS * D
    LOOPS = QUADS // LOOP
    ZEROS = TILES * D // 4
    assert LOOPS * LOOP == QUADS - 1

    ctx = ExitStack()
    with ctx:
        def sb(name, shape, dt=FP32):
            return ctx.enter_context(nc.sbuf_tensor(name, shape, dt))

        def pb(name, shape, dt=FP32):
            return ctx.enter_context(nc.psum_tensor(name, shape, dt))

        def sem(name):
            return ctx.enter_context(nc.semaphore(name))

        def dram(name, shape, dt=FP32):
            return nc.dram_tensor(name, shape, dt, kind="Internal").ap()

        sorted_keys = dram("sorted_keys", (SORT_N + 2,))
        edge_rows = dram("edge_rows", (SLOTS, ROW))
        node_last = dram("node_last", (LAST_N,))
        nodes_x = dram("nodes_x", (NODES, XROW))
        x1_table, x2_table, y1_table = (dram(n, (SLOTS, D)) for n in ("x1_table", "x2_table", "y1_table"))
        y2_table, y3_table = (dram(n, (SLOTS, D)) for n in ("y2_table", "y3_table"))
        live_table = dram("live_table", (SLOTS + 2, 4), I32)
        h_table = dram("h_table", (SLOTS, D))

        rows = sb("rows", [P, TILES, ROW])
        x_src = rows[:, :, X_AT:ROW]
        x_dst_rows = sb("x_dst_rows", [P, TILES, XROW])
        x_dst = x_dst_rows[:, :, 0:D]
        buf_ab = sb("buf_ab", [P, 2, TILES + 2, D])
        wide_a, wide_b, wide_c = buf_ab[:, 0], buf_ab[:, 1], sb("wide_c", [P, TILES + 2, D])
        buf_a, buf_b, buf_c = (w[:, 0:TILES, :] for w in (wide_a, wide_b, wide_c))
        x_state = rows[:, :, :].rearrange("p t r -> p (t r)")[:, 0:TILES * D].rearrange("p (t d) -> p t d", d=D)
        spare = x_dst_rows[:, :, :].rearrange("p t k -> p (t k)")
        buf_d = spare[:, 0:TILES * D].rearrange("p (t d) -> p t d", d=D)
        x_live = spare[:, 0:TILES * D].rearrange("p (t d) -> p t d", d=D)
        packed = buf_ab[:, :, :, :].rearrange("p a t d -> p (a t d)")[:, 0:TILES * ROW].rearrange(
            "p (t r) -> p t r", r=ROW)
        early = wide_c[:, :, :].rearrange("p t d -> p (t d)")
        PAD = XROWS * XROW
        x_pad = [early[:, n * PAD:(n + 1) * PAD].rearrange("p (r k) -> p r k", k=XROW) for n in range(2)]
        early2 = x_dst_rows[:, :, :].rearrange("p t k -> p (t k)")
        cnt, tot, run, turned_last = (early2[:, n * 896:n * 896 + w] for n, w in
                                      enumerate((LOS, LOS, LOS, 7 * P)))
        ones_wide = early2[:, 4 * 896:4 * 896 + LOS]
        attr_in = rows[:, :, :].rearrange("p t r -> p (t r)")[:, 0:TILES * BOND].rearrange(
            "p (t k) -> p t k", k=BOND)

        key_a = sb("key_a", [P, SORT_C])
        key_b = sb("key_b", [P, SORT_C])
        key_i = sb("key_i", [P, SORT_C], I32)
        key_t = sb("key_t", [P, SORT_C], I32)
        edge_id = sb("edge_id", [P, SORT_C], I32)
        col_i = sb("col_i", [P, SORT_C], I32)
        part_i = sb("part_i", [P, 1], I32)
        part_t = sb("part_t", [P, 1], I32)
        COL_LEVELS = SORT_C.bit_length() - 2
        PART_LEVELS = ID_BITS - COL_LEVELS - 1
        PART_TURNS = P.bit_length() - 1
        sign_col = sb("sign_col", [P, COL_LEVELS, SORT_C], F16)
        sign_part = sb("sign_part", [P, PART_LEVELS])
        whole_next_neg = sb("whole_next_neg", [D, P])
        zero1 = sb("zero1", [1, 1])

        key_here = sb("key_here", [P, TILES])
        key_prev = sb("key_prev", [P, TILES])
        key_next = sb("key_next", [P, TILES])
        row_index = sb("row_index", [P, TILES], I32)
        src_index = sb("src_index", [P, TILES], I32)
        dst_index = sb("dst_index", [P, TILES], I32)
        tail_index = sb("tail_index", [P, TILES], I32)
        src_raw = sb("src_raw", [P, TILES], I32)
        live_index = sb("live_index", [P, TILES], I32)
        last_sb = sb("last_sb", [P, NODES // P])
        last_left = sb("last_left", [XLEFT, 1])
        not_tail_neg, from_next_neg = key_here, key_next
        src_hi = sb("src_hi", [P, TILES])
        src_lo = sb("src_lo", [P, TILES])
        lo_iota = sb("lo_iota", [P, LOS], F16)
        hot = sb("hot", [P, HOT * (LOS + P)], F16)
        hot_lo = [hot[:, n * (LOS + P):n * (LOS + P) + LOS] for n in range(HOT)]
        hot_hi = [hot[:, n * (LOS + P) + LOS:(n + 1) * (LOS + P)] for n in range(HOT)]
        weights_early = sb("weights_early", [KP, (BOND + 1) * D])
        live_words = hot[:, :].bitcast(I32)
        live_rows = live_words[:, 0:TILES * 4].rearrange("p (t k) -> p t k", k=4)
        live_in = live_words[:, TILES * 4:TILES * 8 + 8].rearrange("p (t k) -> p t k", k=4)
        LAST_AT, SLOT_AT, WEIGHT_AT, TAIL_AT = range(4)
        live_goes, live_from, live_y = key_a, key_b, key_i
        slot_id = sb("slot_id", [P, TILES], I32)
        own_tail = sb("own_tail", [P, TILES])
        live = sb("live", [P, TILES])
        counts = sb("counts", [P, 2])
        wide_i = sb("wide_i", [1, 1], I32)
        live_whole = sb("live_whole", [D, P])
        upper = sb("upper", [P, P])
        weight_s = sb("weight_s", [P, TILES])
        goes_on = sb("goes_on", [P, TILES])
        goes_on_neg = sb("goes_on_neg", [P, TILES])
        not_tail = sb("not_tail", [P, TILES])
        is_tail = sb("is_tail", [P, TILES])
        from_prev = sb("from_prev", [P, TILES])
        from_prev_neg = sb("from_prev_neg", [P, TILES])
        from_next = sb("from_next", [P, TILES])
        whole = sb("whole", [D, P])
        whole_neg = sb("whole_neg", [D, P])
        whole_next = sb("whole_next", [D, P])
        wide = sb("wide", [P, D])
        carry_t = sb("carry_t", [D, P + 1])
        carry = sb("carry", [P, D])
        mean = sb("mean", [P, TILES])
        var = sb("var", [P, TILES])
        assert LN_EPS == BN_EPS
        eps_c = sb("eps_c", [P, 1])

        ident = sb("ident", [P, P])
        ones = sb("ones", [P, P])
        ones_full = sb("ones_full", [P, P])
        ident_half = sb("ident_half", [P, P], BF16)
        bond_parts = sb("bond_parts", [KP, PARTS, BOND * D], BF16)
        bias_parts = sb("bias_parts", [KP, PARTS, D], BF16)
        w1s_bd = sb("w1s_bd", [P, P])
        w1d_bd = sb("w1d_bd", [P, P])
        w2_bd = sb("w2_bd", [P, P])
        bias_par = sb("bias_par", [P, 2, D])
        bn_par = sb("bn_par", [P, 4, D])
        beta_c = sb("beta_c", [P, 1])
        w3a_bd = sb("w3a_bd", [P, P])
        w3b_bd = sb("w3b_bd", [P, H2])
        b3a_c = sb("b3a_c", [P, 1])
        b3b_row = sb("b3b_row", [1, P])
        rb3a = sb("rb3a", [H2, 1])
        rb3a_w = sb("rb3a_w", [H2, P])
        idle_row = sb("idle_row", [P, D])
        sums = sb("sums", [P, 2, 2 * D])
        stats = sb("stats", [P, 2, D])
        apply_par = sb("apply_par", [P, 2, D])
        bias_off = sb("bias_off", [P, D])
        bn_mean = sb("bn_mean", [P, D])
        bn_scale = sb("bn_scale", [P, D])
        w_t = [sb(f"w_t{n}", [P, 2, P]) for n in range(2)]
        r_t = [sb(f"r_t{n}", [P, 2, P]) for n in range(2)]
        x_ring = [sb("x_ring0", [P, XROWS * D]),
                  buf_ab[:, :, :, :].rearrange("p a t d -> p (a t d)")[:, TILES * ROW:TILES * ROW + XROWS * D]]

        ps_t = [pb(f"ps_t{n}", [P, 4, P]) for n in range(2)]
        ps_u = [pb(f"ps_u{n}", [P, 2, BOND * D]) for n in range(2)]
        ps_o = [pb(f"ps_o{n}", [P, 4, P]) for n in range(2)]
        prod = x_ring[0][:, 0:2 * BOND * D].rearrange("p (t f) -> p t f", t=2)
        PART_W = CHUNK * KP // 2
        norm_parts = [wide_b.rearrange("p t d -> p (t d)")[:, n * PART_W:(n + 1) * PART_W].bitcast(BF16)
                      .rearrange("p (t n j) -> p t n j", n=PARTS, j=D) for n in range(2)]
        parts_t = [w_t[n][:, :, :].rearrange("p a b -> p (a b)").bitcast(BF16)[0:KP, :] for n in range(2)]
        ps_parts = [ps_t[n][:, 0:2, :].rearrange("p a b -> p (a b)").bitcast(BF16)[0:KP, :] for n in range(2)]
        ps_key = ps_t[0][:, 0:2, :].rearrange("p a b -> p (a b)")
        ps_small = ps_t[1][:, 0, :]
        ps_first = ps_u[0][:, 0, 0:D]
        LISTED_IN = NC - 3
        LISTED_AT = QUADS_C * (LISTED_IN - 1) + 1
        ps_rank = ps_o[LISTED_AT % 2][:, 3, 0:3]

        key_pair = (key_a, key_b)
        moves, key_turned = 0, []
        for level in range(1, ID_BITS + 1):
            moves += level < ID_BITS
            crossing = max(0, level - (SORT_C.bit_length() - 1))
            if crossing:
                key_turned += [key_pair[moves % 2], key_pair[(moves + 1 + crossing) % 2]]
                moves += 2
            moves += level + (level < ID_BITS)
        key_sorted = key_pair[moves % 2]

        bond_in = weights_early[0:KP, 0:BOND * D]
        bias_in = weights_early[0:KP, BOND * D:BOND * D + D]
        weight_loads = [(bn_par[:, n, :], p.partition_broadcast(P)) for n, p in enumerate((g1a, be1a, g1b, be1b))]
        weight_loads.append((beta_c[:, :], beta3.partition_broadcast(P)))
        for t in range(4):
            r = slice(32 * t, 32 * t + 32)
            weight_loads += [
                (w1s_bd[r, r], w1a[0:D, :]),
                (w1d_bd[r, r], w1a[D:2 * D, :]), (w2_bd[r, r], w1b), 
                (b3b_row[0:1, r], b3b.unsqueeze(0)),
                (w3a_bd[r, H2 * (t % 2):H2 * (t % 2) + H2], w3a)]
        weight_loads += [(bias_par[:, n, :], p.partition_broadcast(P)) for n, p in enumerate((b1a, b1b))]
        for n in range(PARTS):
            r = slice(D * n, D * n + D)
            weight_loads += [(bond_in[r, :], bond_k), (bias_in[r, :], bond_b)]
        for t in range(2):
            r = slice(H2 * t, H2 * t + H2)
            weight_loads += [(w3b_bd[r, D * t:D * t + D], w3b), (b3a_c[r, :], b3a.unsqueeze(1))]

        iotas = sem("iotas")
        ident_made = sem("ident_made")
        keys_blank = sem("keys_blank")
        src_in = sem("src_in")
        edges_blank = sem("edges_blank")
        edges_in = sem("edges_in")
        packed_done = sem("packed_done")
        rows_stored = sem("rows_stored")
        weights_in = sem("weights_in")
        blocks_blank = sem("blocks_blank")
        dve_step = sem("dve_step")
        bond_step = sem("bond_step")
        to_pe = sem("to_pe")
        from_pe = sem("from_pe")
        sorted_done = sem("sorted_done")
        sorted_stored = sem("sorted_stored")
        keys_back = sem("keys_back")
        src_known = sem("src_known")
        hot_made = sem("hot_made")
        hot_used = sem("hot_used")
        counted = sem("counted")
        last_made = sem("last_made")
        last_stored = sem("last_stored")
        last_back = sem("last_back")
        x_padded = sem("x_padded")
        padded_stored = [sem(f"padded_stored{n}") for n in range(2)]
        got_rows = sem("got_rows")
        dst_known = sem("dst_known")
        got_dst = [sem(f"got_dst{c}") for c in range(NC)]
        got_src = [sem(f"got_src{c}") for c in range(NC)]
        state_made = sem("state_made")
        state_stored = sem("state_stored")
        state_spread = sem("state_spread")
        state_kept = sem("state_kept")
        zeros_made = sem("zeros_made")
        zeros_stored = sem("zeros_stored")
        h_stored = sem("h_stored")
        count_known = sem("count_known")
        rows_listed = sem("rows_listed")
        blanks_made = sem("blanks_made")
        blanks_stored = sem("blanks_stored")
        live_put = sem("live_put")
        live_back = sem("live_back")
        blanked = sem("blanked")
        y_listed = sem("y_listed")
        got_live = [sem(f"got_live{n}") for n in range(2)]
        h_made = sem("h_made")
        h_put = sem("h_put")
        h_back = [sem(f"h_back{n}") for n in range(2)]
        y_made = sem("y_made")
        y_put = sem("y_put")
        y3_back = sem("y3_back")
        centred = sem("centred")
        squared = sem("squared")
        root_ready = sem("root_ready")
        rooted = sem("rooted")
        input_ready = sem("input_ready")
        turned = sem("turned")
        copied = sem("copied")
        bond_mm = sem("bond_mm")
        parts_first = sem("parts_first")
        rest_made = sem("rest_made")
        parts_second = sem("parts_second")
        parts_made = sem("parts_made")
        lin_mm = sem("lin_mm")
        lin_used = sem("lin_used")
        hid_mm = sem("hid_mm")
        hid_done = sem("hid_done")
        scaled = sem("scaled")
        relu_done = sem("relu_done")
        exp_ready = sem("exp_ready")
        exp_done = sem("exp_done")
        x_loaded = [sem(f"x_loaded{n}") for n in range(2)]
        x_added = sem("x_added")
        x_stored = [sem(f"x_stored{n}") for n in range(2)]
        out_rows = sem("out_rows")

        block = ctx.enter_context(nc.Block())

        CHUNKS = [(t, t + CHUNK) for t in range(0, TILES, CHUNK)]
        STEPS = 5

        def first_then_second(eng, first, second):
            if eng is None:
                for q in range(QUADS + 1):
                    if q < QUADS:
                        first(q, q % 2)
                    if q:
                        second(q - 1, (q - 1) % 2)
                return
            with eng.Fori(0, LOOPS) as i:
                for j in range(LOOP + 1):
                    if j < LOOP:
                        first(i * LOOP + j, j % 2)
                    if j:
                        second(i * LOOP + j - 1, (j - 1) % 2)
            first(QUADS - 1, (QUADS - 1) % 2)
            second(QUADS - 1, (QUADS - 1) % 2)

        def ready_parts(vw):
            run = RUN if vw == NARROW else TILES
            return [slice(run, TILES), slice(0, run)] if run < TILES else [slice(0, TILES)]

        def narrow_or_wide(eng, layers):
            too_wide = eng.value_load(wide_i[0:1, 0:1], min_val=0, max_val=2)
            with eng.If(too_wide < 1):
                layers(NARROW)
            with eng.Else():
                layers(TILES)

        LAST_CHUNKS = [(0, 2), (2, QUADS_C)] + [(QUADS_C * n, QUADS_C * (n + 1)) for n in range(1, NC)]

        def quad(buf, q):
            return buf[:, bass.ds(q * 4, 4), :].rearrange("p t d -> p (t d)")

        def slots_norm(of, to, sq):
            return [(of[:, a:b], to[:, a:b], sq[:, a:b], mean[:, a:b], var[:, a:b]) for a, b in CHUNKS]

        def halves(vw):
            return slice(0, vw // 2), slice(vw // 2, vw)

        def live_norm(vw):
            return [tuple(a[:, half] for a in (x_live, wide_b, wide_c, mean, var)) for half in halves(vw)]

        NORM0 = slots_norm(x_dst, buf_a, buf_c)

        def bcast(a, n):
            return a.unsqueeze(len(a.shape)).to_broadcast(list(a.shape) + [n])

        @block.sync
        def _(sp):
            def by_edge(to, of):
                full = FULL_P * TILES
                yield sp.dma_start(to[0:FULL_P, 0:TILES], of[0:full].rearrange("(p t) k -> p t k", t=TILES))
                yield sp.dma_start(to[FULL_P:P, 0:REST], of[full:EDGES].unsqueeze(0))

            sp.wait_ge(keys_blank, 1)
            for to in (src_raw, key_i):
                for load in by_edge(to[:, :].unsqueeze(2), src.unsqueeze(1)):
                    load.then_inc(src_in, 16)
            sp.wait_ge(edges_blank, 1)
            for to, of in ((attr_in, attr), (key_prev[:, :].unsqueeze(2), weight.unsqueeze(1)),
                           (dst_index[:, :].unsqueeze(2), dst.unsqueeze(1))):
                for load in by_edge(to, of):
                    load.then_inc(edges_in, 16)

            def store_rows(chunks):
                for n in chunks:
                    a, b = CHUNKS[n]
                    sp.wait_ge(got_src[n], 16 * CHUNK)
                    sp.dma_start(edge_rows.rearrange("(p t) r -> p t r", p=P)[:, a:b], packed[:, a:b])\
                        .then_inc(rows_stored, 16)

            sp.wait_ge(packed_done, 1)
            store_rows(range(3))
            sp.wait_ge(sorted_done, 1)
            sp.dma_start(sorted_keys[0:1].unsqueeze(0), zero1[:, :]).then_inc(sorted_stored, 16)
            sp.dma_start(sorted_keys[1:1 + SORT_N].rearrange("(p t) -> p t", p=P), key_sorted[:, :])\
                .then_inc(sorted_stored, 16)
            sp.wait_ge(sorted_stored, 32)
            for to, off in ((key_here, 1), (key_prev, 0), (key_next, 2)):
                sp.dma_start(to[:, :], sorted_keys[off:off + SLOTS].rearrange("(p t) -> p t", p=P))\
                    .then_inc(keys_back, 16)
            store_rows(range(3, NC))
            sp.wait_ge(last_made, 1)
            by_lo = node_last.rearrange("(l h) -> l h", h=P)
            whole_blocks = LOS // P
            tl = turned_last.rearrange("p (b h) -> p b h", h=P)
            sp.dma_start(by_lo[0:whole_blocks * P].rearrange("(b l) h -> l b h", l=P), tl[:, 0:whole_blocks])\
                .then_inc(last_stored, 16)
            sp.dma_start(by_lo[whole_blocks * P:LOS], tl[0:LOS - whole_blocks * P, whole_blocks])\
                .then_inc(last_stored, 16)
            sp.wait_ge(last_stored, 32)
            full = P * XCH * XROWS
            sp.dma_start(last_sb[:, :], node_last[0:full].rearrange("(p r) -> p r", p=P)).then_inc(last_back, 16)
            sp.dma_start(last_left[:, :], node_last[full:NODES].unsqueeze(1)).then_inc(last_back, 16)
            def by_slot(table):
                return table.rearrange("(p t) d -> p t d", p=P)

            sp.wait_ge(blanks_made, 1)
            sp.dma_start(live_table[0:SLOTS].rearrange("(p t) k -> p t k", p=P), live_in[:, 0:TILES])\
                .then_inc(blanks_stored, 16)
            sp.dma_start(live_table[SLOTS:SLOTS + 2].unsqueeze(0), live_in[0:1, 0:2]).then_inc(blanks_stored, 16)
            sp.wait_ge(zeros_made, 1)
            for table in (y2_table, y3_table):
                for n in range(4):
                    sp.dma_start(table.rearrange("(p t) d -> p (t d)", p=P)[:, n * ZEROS:(n + 1) * ZEROS],
                                 x_ring[0][:, 0:ZEROS]).then_inc(zeros_stored, 16)
            sp.wait_ge(input_ready, NC)
            sp.dma_start(by_slot(h_table), buf_a).then_inc(h_stored, 16)
            sp.wait_ge(count_known, 1)

            def layers(vw):
                sp.wait_ge(live_put, 16 * TILES)
                first, last = 1, P * vw
                before, here = (live_table[n:n + P * vw].rearrange("(p t) k -> p t k", p=P) for n in (0, first))
                after = live_table[first + vw:first + last].rearrange("(p t) k -> p t k", p=P - 1)
                for to, of in ((live_in[:, 0:1], before[:, 0:1]), (live_in[:, 1:1 + vw], here),
                               (live_in[0:P - 1, vw + 1:vw + 2], after[:, 0:1]),
                               (live_in[P - 1:P, vw + 1:vw + 2], live_table[last + 1:last + 2].unsqueeze(0))):
                    sp.dma_start(to, of).then_inc(live_back, 16)
                parts = ready_parts(vw)

                def store(count, table, of):
                    for n, cols in enumerate(parts):
                        sp.wait_ge(state_made, (count - 1) * len(parts) + n + 1)
                        sp.dma_start(by_slot(table)[:, cols], of[:, cols]).then_inc(state_stored, 16)

                def load_h(count, to):
                    sp.wait_ge(h_put, 16 * vw * count)
                    for half, back in zip(halves(TILES), h_back):
                        sp.dma_start(to[:, half], by_slot(h_table)[:, half]).then_inc(back, 16)

                store(1, x1_table, buf_a)
                load_h(1, buf_b)
                store(2, x2_table, x_state)
                load_h(2, buf_a)
                store(3, y1_table, buf_c)
                sp.wait_ge(y_put, 16 * vw * 2)
                sp.wait_ge(h_made, 6)
                sp.wait_ge(state_stored, 16 * 3 * len(parts))
                sp.dma_start(buf_c, by_slot(y3_table)).then_inc(y3_back, 16)
                load_h(3, buf_a)
                sp.wait_ge(y3_back, 16)

            narrow_or_wide(sp, layers)

        @block.scalar
        def _(act):
            act.wait_ge(blocks_blank, 1)
            for to, of in weight_loads:
                act.dma_start(to, of).then_inc(weights_in, 16)

            def x_rows(t, c):
                return t[0:P * XCH * XROWS, :].rearrange("(p c r) d -> c p (r d)", c=XCH, r=XROWS)[c]

            def load(c):
                if c >= 2:
                    act.wait_ge(x_stored[c % 2], 16 * (c // 2))
                act.dma_start(x_ring[c % 2][:, :], x_rows(x, c)).then_inc(x_loaded[c % 2], 16)

            def pad(c, ring, tail, padded, to):
                act.wait_ge(x_loaded[c % 2], 16 * (c // 2 + 1))
                if c >= 2:
                    act.wait_ge(padded_stored[c % 2], 16 * (c // 2))
                act.activation(padded[:, :, D], tail, ACT.Copy).then_inc(x_padded, 1)
                act.activation(padded[:, :, 0:D], ring, ACT.Copy).then_inc(x_padded, 1)
                act.wait_ge(x_padded, 2 * c + 2)
                act.dma_start(to, padded).then_inc(padded_stored[c % 2], 16)

            full = P * XCH * XROWS
            padded_rows = nodes_x[0:full].rearrange("(p c r) k -> c p r k", c=XCH, r=XROWS)
            left = x_ring[XCH % 2][0:XLEFT, 0:D]
            load(0)
            act.wait_ge(last_back, 32)
            for c in range(XCH):
                if c + 1 < XCH:
                    load(c + 1)
                pad(c, x_ring[c % 2][:, :].rearrange("p (r d) -> p r d", d=D),
                    last_sb[:, c * XROWS:(c + 1) * XROWS], x_pad[c % 2], padded_rows[c])
                act.wait_ge(x_added, c + 1)
                act.dma_start(x_rows(out, c), x_ring[c % 2][:, :]).then_inc(x_stored[c % 2], 16)
            act.wait_ge(x_stored[XCH % 2], 16 * (XCH // 2))
            act.dma_start(left, x[full:NODES, :]).then_inc(x_loaded[XCH % 2], 16)
            pad(XCH, left.unsqueeze(1), last_left[:, :], x_pad[XCH % 2][0:XLEFT, 0:1],
                nodes_x[full:NODES].unsqueeze(1))
            act.wait_ge(x_added, XCH + 1)
            act.dma_start(out[full:NODES, :], left).then_inc(x_stored[XCH % 2], 16)

            normed = [0]

            def square(part):
                act.wait_ge(centred, normed[0] + part + 1)
                of = act_parts[part]
                act.activation(of[2], of[1], ACT.Square).then_inc(squared, 1)

            def root(part):
                act.wait_ge(root_ready, normed[0] + part + 1)
                v = act_parts[part][4]
                act.activation(v, v, ACT.Sqrt, bias=eps_c[:, :], scale=1.0 / D).then_inc(rooted, 1)

            def norm(parts):
                act_parts[:] = parts
                for n in range(len(parts) + 1):
                    if n < len(parts):
                        square(n)
                    if n:
                        root(n - 1)
                normed[0] += len(parts)

            def norm_halves(vw):
                act_parts[:] = live_norm(vw)
                for n in range(2):
                    square(n)
                    root(n)
                normed[0] += 2

            act_parts = []

            def batch_layer(copy, relu_first=None):
                if relu_first:
                    relu_first(0)
                for n in range(NC + 1):
                    if relu_first and n + 1 < NC:
                        relu_first(n + 1)
                    for j in range(QUADS_C):
                        if j == QUADS_C // 2 and n:
                            a, b = CHUNKS[n - 1]
                            act.wait_ge(centred, normed[0] + n)
                            act.activation(buf_b[:, a:b], buf_c[:, a:b], ACT.Square).then_inc(squared, 1)
                        if n < NC:
                            q = QUADS_C * n + j
                            copy(q, q % 2)
                act.wait_ge(root_ready, normed[0] + NC)
                act.activation(bn_scale[:, :], bn_scale[:, :], ACT.Sqrt, bias=eps_c[:, :]).then_inc(rooted, NC)
                normed[0] += NC

            def copy_turned(stage, blocks):
                def copy(q, s):
                    act.wait_ge(turned, stage * QUADS + q + 1)
                    act.wait_ge(lin_mm, stage * QUADS + q + 1)
                    act.activation(w_t[s][:, 0:blocks, :], ps_t[s][:, 0:blocks, :], ACT.Copy)\
                        .then_inc(copied, 1)
                return copy

            def hidden(q, s):
                act.wait_ge(hid_mm, q + 1)
                act.wait_ge(lin_mm, 3 * QUADS + q + 1)
                act.activation(r_t[s][:, :, :], ps_u[s][:, :, 0:P], ACT.Relu, bias=b3a_c[:, :])\
                    .then_inc(hid_done, 1)

            for n in range(2):
                act.wait_ge(x_stored[n], 16 * ((XCH + 2 - n) // 2))
            act.sem_inc(copied, 2)
            act.sem_inc(hid_done, 2)
            act_parts[:] = NORM0

            def first_parts(n):
                a, b = CHUNKS[n]
                act.wait_ge(input_ready, n + 1)
                if n >= 2:
                    act.wait_ge(turned, QUADS_C * (n - 1))
                act.activation(norm_parts[n % 2][:, :, 0], buf_a[:, a:b], ACT.Copy).then_inc(parts_first, 1)

            def second_parts(n):
                a, b = CHUNKS[n]
                act.wait_ge(rest_made, n + 1)
                act.activation(norm_parts[n % 2][:, :, 1], buf_c[:, a:b], ACT.Copy).then_inc(parts_second, 1)

            def copy_parts(q, s):
                act.wait_ge(turned, q + 1)
                act.wait_ge(lin_mm, q + 1)
                act.activation(parts_t[s], ps_parts[s], ACT.Copy).then_inc(copied, 1)

            for n in range(NC + 1):
                stages = [square, root, first_parts, second_parts] if n < NC else [None] * 4
                for stage, ahead in zip(stages + [None], ((), (1, 2), (3,), (4,), (5, 6, 7))):
                    for j in ahead:
                        q = QUADS_C * (n - 1) + j
                        if 0 <= q < QUADS and (n or j == QUADS_C):
                            copy_parts(q, q % 2)
                    if stage:
                        stage(n)
            normed[0] += NC
            act.wait_ge(count_known, 1)

            def relu_chunk(n, to):
                a, b = CHUNKS[n]
                relus[0] += 1
                act.wait_ge(scaled, relus[0])
                act.activation(to[:, a:b], buf_c[:, a:b], ACT.Relu).then_inc(relu_done, 1)

            relus = [0]

            def layers(vw):
                act.wait_ge(state_spread, 1)
                act.activation(x_state, buf_b, ACT.Copy).then_inc(state_kept, 1)
                norm(slots_norm(x_state, buf_a, buf_c))
                norm_halves(vw)
                batch_layer(copy_turned(1, 2))
                batch_layer(copy_turned(2, 1), relu_first=lambda n: relu_chunk(n, buf_a))
                act.wait_ge(scaled, NC + 1)
                for d in range(D // 2, D):
                    act.activation(buf_c[:, :, d], buf_c[:, :, d], ACT.Relu, bias=apply_par[:, 1, d:d + 1],
                                   scale=apply_par[:, 0, d:d + 1]).then_inc(relu_done, 1)
                norm_halves(vw)
                norm_halves(vw)
                for n, (a, b) in enumerate(CHUNKS):
                    act.wait_ge(exp_ready, n + 1)
                    act.activation(buf_b[:, a:b], buf_b[:, a:b], ACT.Exp).then_inc(exp_done, 1)
                first_then_second(act, copy_turned(3, 1), hidden)
                normed[0], relus[0] = NC, 0

            narrow_or_wide(act, layers)

        @block.gpsimd
        def _(gp):
            gp.iota(edge_id[:, 0:TILES], pattern=[[1, TILES]], base=0, channel_multiplier=TILES)\
                .then_inc(iotas, 1)
            gp.iota(edge_id[:, TILES:SORT_C], pattern=[[1, SORT_C - TILES]], base=SLOTS,
                    channel_multiplier=SORT_C - TILES).then_inc(iotas, 1)
            gp.iota(slot_id[:, :], pattern=[[1, TILES]], base=0, channel_multiplier=TILES).then_inc(iotas, 1)
            gp.iota(lo_iota[:, :], pattern=[[1, LOS]], base=0, channel_multiplier=0,
                    allow_small_or_imprecise_dtypes=True).then_inc(iotas, 1)
            gp.iota(col_i[:, :], pattern=[[1, SORT_C]], base=0, channel_multiplier=0).then_inc(iotas, 1)
            gp.iota(part_i[:, :], pattern=[[1, 1]], base=0, channel_multiplier=1).then_inc(iotas, 1)
            gp.memset(ident[:, :], 0.0).then_inc(ident_made, 1)
            gp.memset(ones_full[:, :], 1.0).then_inc(ident_made, 1)
            gp.memset(upper[:, :], 1.0).then_inc(ident_made, 1)
            gp.memset(ident_half[:, :], 0.0).then_inc(ident_made, 1)
            gp.wait_ge(ident_made, 4)
            gp.affine_select(out=ident_half[:, :], in_=ident_half[:, :], compare_op=ALU.not_equal, fill=1.0,
                             base=0, pattern=[[-1, P]], channel_multiplier=1).then_inc(ident_made, 1)
            gp.affine_select(out=upper[:, :], in_=upper[:, :], compare_op=ALU.is_ge, fill=0.0, base=0,
                             pattern=[[1, P]], channel_multiplier=-1).then_inc(ident_made, 1)
            gp.affine_select(out=ident[:, :], in_=ident[:, :], compare_op=ALU.not_equal, fill=1.0, base=0,
                             pattern=[[-1, P]], channel_multiplier=1).then_inc(ident_made, 1)
            gp.affine_select(out=ones_full[:, :], in_=ones_full[:, :], compare_op=ALU.is_gt, fill=0.0,
                             base=FULL_P, pattern=[[0, P]], channel_multiplier=-1).then_inc(ident_made, 1)

            def gather(to, table, rows_at, signal):
                gp.indirect_dma_start(out=to, out_offset=None, in_=table,
                                      in_offset=bass.IndirectOffsetOnAxis(ap=rows_at, axis=0),
                                      bounds_check=table.shape[0] - 1,
                                      oob_is_err=False).then_inc(signal, 16)

            def scatter(table, rows_at, of, signal):
                gp.indirect_dma_start(out=table, in_=of, in_offset=None,
                                      out_offset=bass.IndirectOffsetOnAxis(ap=rows_at, axis=0),
                                      bounds_check=table.shape[0] - 1, oob_is_err=False).then_inc(signal, 16)

            gp.wait_ge(edges_blank, 1)
            gp.wait_ge(src_in, 16 * 4)
            for t in range(TILES):
                gather(packed[:, t, X_AT:ROW], x, src_raw[:, t:t + 1], got_src[t // CHUNK])
            gp.wait_ge(rows_stored, 16 * NC)
            gp.wait_ge(src_known, 1)
            for t in range(TILES):
                gather(rows[:, t, :], edge_rows, row_index[:, t:t + 1], got_rows)
            gp.wait_ge(dst_known, 1)
            for n in range(2):
                gp.wait_ge(padded_stored[n], 16 * ((XCH + 2 - n) // 2))
            for t in range(TILES):
                gather(x_dst_rows[:, t, :], nodes_x, dst_index[:, t:t + 1], got_dst[t // CHUNK])
            gp.wait_ge(blanks_stored, 32)
            gp.wait_ge(rows_listed, 1)
            for t in range(TILES):
                scatter(live_table, live_index[:, t:t + 1], live_rows[:, t, :], live_put)
            gp.wait_ge(h_stored, 16)
            gp.wait_ge(zeros_stored, 16 * 8)
            gp.wait_ge(count_known, 1)

            def layers(vw):
                puts_h, puts_y = [0], [0]

                def live_word(j, at):
                    return live_in[:, 1 + j, at:at + 1]

                def at_live(buf, table):
                    for j in range(vw):
                        gather(buf[:, j, :], table, live_word(j, LAST_AT), got_live[j >= vw // 2])

                def put_h():
                    puts_h[0] += 1
                    for n, half in enumerate(halves(vw)):
                        gp.wait_ge(h_made, 2 * puts_h[0] + n - 1)
                        for j in range(half.start, half.stop):
                            scatter(h_table, live_word(j, SLOT_AT), wide_b[:, j, :], h_put)
                    gp.wait_ge(h_put, 16 * vw * puts_h[0])

                def put_y(table):
                    puts_y[0] += 1
                    for n, half in enumerate(halves(vw)):
                        gp.wait_ge(y_made, 2 * puts_y[0] + n - 1)
                        for j in range(half.start, half.stop):
                            scatter(table, live_y[:, j:j + 1], wide_b[:, j, :], y_put)
                    gp.wait_ge(y_put, 16 * vw * puts_y[0])

                gp.wait_ge(live_back, 16 * 4)
                parts = len(ready_parts(vw))
                gp.wait_ge(state_stored, 16 * parts)
                gp.wait_ge(blanked, 1)
                at_live(x_live, x1_table)
                put_h()
                gp.wait_ge(state_stored, 16 * 2 * parts)
                at_live(x_live, x2_table)
                put_h()
                gp.wait_ge(state_stored, 16 * 3 * parts)
                at_live(wide_b, y1_table)
                gp.wait_ge(y_listed, 1)
                put_y(y2_table)
                at_live(wide_b, y2_table)
                put_y(y3_table)
                at_live(wide_b, y3_table)
                put_h()
                for n in range(2):
                    gp.wait_ge(x_stored[n], 16 * ((XCH + 2 - n) // 2))
                for t in range(TILES):
                    if t % 4 == 0:
                        gp.wait_ge(lin_used, 3 * QUADS + t // 4 + 3)
                    scatter(out, tail_index[:, t:t + 1], x_state[:, t, :], out_rows)
                gp.wait_ge(out_rows, 16 * TILES)

            narrow_or_wide(gp, layers)

        @block.vector
        def _(v):
            steps = [0]

            def step(ins):
                steps[0] += 1
                ins.then_inc(dve_step, 1)

            def settle():
                v.wait_ge(dve_step, steps[0])

            def link(ins):
                step(ins)
                settle()

            small = [0]

            def pe_does(meanwhile=None):
                small[0] += 1
                v.sem_inc(to_pe, 1)
                if meanwhile:
                    meanwhile()
                v.wait_ge(from_pe, small[0])

            def over_t(a, n):
                return a.unsqueeze(1).to_broadcast([P, n, D])

            step(v.memset(key_i[:, :], NODES))
            step(v.memset(src_raw[:, :], NODES))
            settle()
            v.sem_inc(keys_blank, 1)
            step(v.memset(packed[P - 32:P, REST:TILES, X_AT:ROW], 0.0))
            step(v.memset(attr_in[P - 32:P, REST:TILES, :], 0.0))
            step(v.memset(key_prev[P - 32:P, REST:TILES], 0.0))
            step(v.memset(dst_index[P - 32:P, REST:TILES], 0))
            settle()
            v.sem_inc(edges_blank, 1)
            step(v.memset(zero1[:, :], 0.0))
            step(v.memset(ones[:, :], 1.0))
            step(v.memset(eps_c[:, :], LN_EPS))
            step(v.memset(ones_wide, 1.0))
            for t in (w1s_bd, w1d_bd, w2_bd, w3a_bd, w3b_bd):
                step(v.memset(t[:, :], 0.0))
            settle()
            v.sem_inc(blocks_blank, 1)
            v.sem_inc(bond_step, STEPS)
            v.sem_inc(lin_used, 2)

            v.wait_ge(iotas, 6)
            v.wait_ge(src_in, 16 * 4)
            link(v.tensor_copy(key_a[:, :], key_i[:, :]))
            step(v.tensor_scalar(key_b[:, :], key_a[:, :], -1.0, float(HALF - 1), ALU.mult, ALU.add))
            step(v.tensor_scalar(key_t[:, :], key_a[:, :], float(HALF), None, ALU.is_lt))
            step(v.tensor_scalar(tail_index[:, :], key_i[:, 0:TILES], P - 1, None, ALU.bitwise_and))
            step(v.tensor_scalar(row_index[:, :], key_i[:, 0:TILES], P.bit_length() - 1, None,
                                 ALU.logical_shift_right))
            settle()
            step(v.tensor_copy(src_hi[:, :], tail_index[:, :]))
            step(v.tensor_copy(src_lo[:, :], row_index[:, :]))
            link(v.scalar_tensor_tensor(key_a[:, :], key_a[:, :], -float(HALF), key_b[:, :], ALU.add, ALU.max))
            link(v.tensor_scalar(key_i[:, :], key_a[:, :], float(LIFT), None, ALU.add))
            link(v.tensor_scalar(key_i[:, :], key_i[:, :], ID_BITS, None, ALU.logical_shift_left))
            link(v.tensor_scalar(key_t[:, :], key_t[:, :], 31, None, ALU.logical_shift_left))
            link(v.tensor_tensor(key_i[:, :], key_i[:, :], edge_id[:, :], ALU.bitwise_or))
            link(v.tensor_tensor(key_a[:, :].bitcast(I32), key_i[:, :], key_t[:, :], ALU.bitwise_or))
            for n in range(COL_LEVELS):
                link(v.tensor_scalar(key_t[:, :], col_i[:, :], 2 << n, None, ALU.bitwise_and))
                link(v.tensor_scalar(sign_col[:, n, :], key_t[:, :], -1.0 / (1 << n), 1.0, ALU.mult, ALU.add))
            for n in range(PART_LEVELS):
                link(v.tensor_scalar(part_t[:, :], part_i[:, :], 1 << n, None, ALU.bitwise_and))
                link(v.tensor_scalar(sign_part[:, n:n + 1], part_t[:, :], -2.0 / (1 << n), 1.0,
                                     ALU.mult, ALU.add))

            v.wait_ge(edges_in, 16 * 6)
            step(v.tensor_copy(packed[:, :, 0:BOND], attr_in))
            step(v.tensor_copy(packed[:, :, W_AT], key_prev[:, :]))
            step(v.tensor_copy(packed[:, :, DST_AT], dst_index[:, :]))
            settle()
            v.sem_inc(packed_done, 1)

            pair = [key_a, key_b]

            def flip(level):
                a, b = pair
                if level <= COL_LEVELS:
                    link(v.tensor_tensor(b[:, :], a[:, :], sign_col[:, level - 1, :], ALU.mult))
                else:
                    n = level - COL_LEVELS - 1
                    link(v.tensor_scalar(b[:, :], a[:, :], sign_part[:, n:n + 1], None, ALU.mult))
                pair.reverse()

            def exchange(distance):
                a, b = (k[:, :].rearrange("p (b h d) -> p b h d", h=2, d=distance) for k in pair)
                step(v.tensor_tensor(b[:, :, 0], a[:, :, 0], a[:, :, 1], ALU.min))
                link(v.tensor_tensor(b[:, :, 1], a[:, :, 0], a[:, :, 1], ALU.max))
                pair.reverse()

            def turn_keys():
                pe_does()
                link(v.tensor_copy(pair[1][:, :], ps_key))
                pair.reverse()

            for level in range(1, ID_BITS + 1):
                if level < ID_BITS:
                    flip(level)
                distance = 1 << (level - 1)
                if distance >= SORT_C:
                    turn_keys()
                    while distance >= SORT_C:
                        exchange(distance // SORT_C)
                        distance //= 2
                    turn_keys()
                while distance:
                    exchange(distance)
                    distance //= 2
                if level < ID_BITS:
                    flip(level)
            assert pair[0] is key_sorted
            v.sem_inc(sorted_done, 1)

            v.wait_ge(keys_back, 16 * 3)
            here, prev, nxt = (k[:, :].bitcast(I32) for k in (key_here, key_prev, key_next))
            link(v.tensor_scalar(row_index[:, :], here, SORT_N - 1, None, ALU.bitwise_and))
            for k in (here, prev, nxt):
                step(v.tensor_scalar(k, k, ID_BITS, None, ALU.logical_shift_right))
            settle()
            step(v.tensor_tensor(goes_on[:, :], here, prev, ALU.is_equal))
            step(v.tensor_tensor(not_tail[:, :], here, nxt, ALU.is_equal))
            settle()
            half_bit = 31 - ID_BITS
            step(v.tensor_scalar(prev, here, half_bit, None, ALU.logical_shift_right))
            step(v.tensor_scalar(nxt, here, (1 << half_bit) - 1, None, ALU.bitwise_and))
            settle()
            link(v.tensor_scalar(mean[:, :], prev, -2.0, 1.0, ALU.mult, ALU.add))
            link(v.scalar_tensor_tensor(mean[:, :], nxt, -float(LIFT), mean[:, :], ALU.add, ALU.mult))
            link(v.scalar_tensor_tensor(mean[:, :], prev, -1.0, mean[:, :], ALU.mult, ALU.add))
            link(v.tensor_scalar(src_index[:, :], mean[:, :], float(HALF), None, ALU.add))
            v.sem_inc(src_known, 1)
            step(v.scalar_tensor_tensor(tail_index[:, :], not_tail[:, :], float(NOWHERE), src_index[:, :],
                                        ALU.mult, ALU.add))
            step(v.tensor_scalar(is_tail[:, :], not_tail[:, :], -1.0, 1.0, ALU.mult, ALU.add))
            step(v.tensor_scalar(goes_on_neg[:, :], goes_on[:, :], 1.0, BIG, ALU.subtract, ALU.mult))
            step(v.tensor_tensor_scan(from_prev[:, :], goes_on[:, :], goes_on[:, :], 1.0,
                                      op0=ALU.mult, op1=ALU.mult))
            step(v.tensor_tensor_scan(from_next[:, ::-1], not_tail[:, ::-1], not_tail[:, ::-1], 1.0,
                                      op0=ALU.mult, op1=ALU.mult))
            settle()
            link(v.tensor_scalar(from_prev_neg[:, :], from_prev[:, :], 1.0, BIG, ALU.subtract, ALU.mult))
            link(v.tensor_copy(wide[:, :], from_prev[:, TILES - 1:TILES].to_broadcast([P, D])))
            pe_does()
            link(v.tensor_copy(whole[:, :], ps_small[0:D, :]))
            link(v.tensor_scalar(whole_neg[:, :], whole[:, :], 1.0, BIG, ALU.subtract, ALU.mult))
            link(v.tensor_copy(wide[:, :], from_next[:, 0:1].to_broadcast([P, D])))
            pe_does()
            link(v.tensor_copy(whole_next[:, :], ps_small[0:D, :]))

            def hot(t, s):
                v.wait_ge(hot_used, t + 1)
                v.tensor_scalar(hot_lo[s][:, :], lo_iota[:, :], src_lo[:, bass.ds(t, 1)], None, ALU.is_equal)\
                    .then_inc(hot_made, 1)
                v.tensor_scalar(hot_hi[s][:, :], lo_iota[:, 0:P], src_hi[:, bass.ds(t, 1)], None, ALU.is_equal)\
                    .then_inc(hot_made, 1)

            with v.Fori(0, TILES // HOT_LOOP) as i:
                for j in range(HOT_LOOP):
                    hot(i * HOT_LOOP + j, j % HOT)
            v.wait_ge(counted, 1)
            for h in range(2):
                step(v.tensor_copy(cnt[:, h * LO_H:(h + 1) * LO_H], ps_o[h][:, :, :].rearrange(
                    "p a b -> p (a b)")[:, 0:LO_H]))
            settle()
            pe_does()
            for h in range(2):
                part = slice(h * LO_H, (h + 1) * LO_H)
                step(v.tensor_copy(tot[:, part], ps_u[1][:, h, 0:LO_H]))
            settle()
            link(v.tensor_tensor_scan(run, ones_wide, tot, -1.0, op0=ALU.mult, op1=ALU.add))
            link(v.tensor_tensor(run, run, tot, ALU.subtract))
            for h in range(2):
                part = slice(h * LO_H, (h + 1) * LO_H)
                step(v.tensor_tensor(run[:, part], run[:, part], ps_u[0][:, h, 0:LO_H], ALU.add))
            step(v.tensor_scalar(cnt, cnt, 0.0, float(NOWHERE), ALU.is_equal, ALU.mult))
            settle()
            link(v.tensor_tensor(run, run, cnt, ALU.add))
            pe_does()
            for b in range(-(-LOS // P)):
                w = min(P, LOS - b * P)
                step(v.tensor_copy(turned_last[0:w, b * P:(b + 1) * P], ps_t[b // 4][0:w, b % 4, :]))
            settle()
            v.sem_inc(last_made, 1)

            v.wait_ge(weights_in, 16 * len(weight_loads))
            link(v.tensor_scalar(rb3a[:, :], b3a_c[0:H2, :], 0.0, None, ALU.max))
            link(v.tensor_copy(rb3a_w[:, :], rb3a[:, :].to_broadcast([H2, P])))
            pe_does()
            link(v.tensor_copy(idle_row[:, :], ps_small[:, 0:D]))
            for c in range(XCH):
                v.wait_ge(x_padded, 2 * c + 2)
                ring = x_ring[c % 2][:, :].rearrange("p (r d) -> p r d", d=D)
                link(v.tensor_tensor(ring, ring, over_t(idle_row[:, :], XROWS), ALU.add))
                v.sem_inc(x_added, 1)
            v.wait_ge(x_padded, 2 * XCH + 2)
            left = x_ring[XCH % 2][0:XLEFT, 0:D]
            link(v.tensor_tensor(left, left, idle_row[0:XLEFT, :], ALU.add))
            v.sem_inc(x_added, 1)

            for n in range(2):
                v.wait_ge(x_stored[n], 16 * ((XCH + 2 - n) // 2))
            link(v.memset(x_ring[0][:, 0:ZEROS], 0.0))
            v.sem_inc(zeros_made, 1)

            def carry_back():
                link(v.memset(carry_t[:, P:P + 1], 0.0))
                pe_does()
                link(v.tensor_tensor_scan(carry_t[:, 0:P][:, ::-1], whole_next[:, ::-1],
                                          ps_small[0:D, ::-1], 0.0, op0=ALU.mult, op1=ALU.add))
                pe_does()
                link(v.tensor_copy(carry[:, :], ps_small[:, 0:D]))

            step(v.memset(live_in, NOWHERE))
            step(v.tensor_copy(mean[:, :], slot_id[:, :]))
            settle()
            step(v.memset(live_in[:, :, WEIGHT_AT], 0))
            step(v.tensor_copy(live_rows[:, :, SLOT_AT], slot_id[:, :]))
            step(v.tensor_tensor(mean[:, :], mean[:, :], is_tail[:, :], ALU.mult))
            settle()
            v.sem_inc(blanks_made, 1)
            link(v.tensor_tensor_scan(own_tail[:, ::-1], not_tail[:, ::-1], mean[:, ::-1], 0.0,
                                      op0=ALU.mult, op1=ALU.add))
            link(v.tensor_copy(wide[:, :], own_tail[:, 0:1].to_broadcast([P, D])))
            carry_back()
            link(v.scalar_tensor_tensor(live_rows[:, :, TAIL_AT], from_next[:, :], carry[:, 0:1], own_tail[:, :],
                                        ALU.mult, ALU.add))
            step(v.tensor_scalar(not_tail_neg[:, :], not_tail[:, :], 1.0, BIG, ALU.subtract, ALU.mult))
            step(v.tensor_scalar(from_next_neg[:, :], from_next[:, :], 1.0, BIG, ALU.subtract, ALU.mult))
            step(v.tensor_scalar(whole_next_neg[:, :], whole_next[:, :], 1.0, BIG, ALU.subtract, ALU.mult))
            step(v.tensor_scalar(live[:, :], src_index[:, :], float(NODES), None, ALU.is_lt))
            step(v.tensor_reduce(out=bn_mean[:, 0:1], in_=from_prev[:, :], op=ALU.add, axis=AX.X))
            settle()
            link(v.tensor_tensor(own_tail[:, :], from_next[:, :], live[:, :], ALU.mult))
            step(v.tensor_reduce(out=bn_mean[:, 1:2], in_=own_tail[:, :], op=ALU.add, axis=AX.X))
            settle()
            link(v.tensor_tensor(bn_mean[:, 0:1], bn_mean[:, 0:1], bn_mean[:, 1:2], ALU.max))
            link(v.tensor_scalar(counts[:, 1:2], bn_mean[:, 0:1], float(RUN), None, ALU.is_gt))

            v.wait_ge(got_rows, 16 * TILES)
            step(v.tensor_copy(dst_index[:, :], rows[:, :, DST_AT]))
            step(v.tensor_copy(weight_s[:, :], rows[:, :, W_AT]))
            step(v.tensor_copy(live_rows.bitcast(FP32)[:, :, WEIGHT_AT], rows[:, :, W_AT]))
            settle()
            v.sem_inc(dst_known, 1)

            normed = [0]

            def centre(parts, n):
                of, to, _, m, _ = parts[n]
                link(v.tensor_reduce(out=m, in_=of, op=ALU.add, axis=AX.X))
                link(v.tensor_scalar(m, m, 1.0 / D, None, ALU.mult))
                link(v.tensor_tensor(to, of, bcast(m, D), ALU.subtract))
                v.sem_inc(centred, 1)

            def spread(parts, n):
                v.wait_ge(squared, normed[0] + n + 1)
                link(v.tensor_reduce(out=parts[n][4], in_=parts[n][2], op=ALU.add, axis=AX.X))
                v.sem_inc(root_ready, 1)

            def scale(parts, n):
                _, to, _, _, var_n = parts[n]
                v.wait_ge(rooted, normed[0] + n + 1)
                link(v.reciprocal(var_n, var_n))
                link(v.scalar_tensor_tensor(to, to, 0.0, bcast(var_n, D), ALU.max, ALU.mult))

            def layer_norm(parts):
                for n in range(len(parts) + 2):
                    if n < len(parts):
                        centre(parts, n)
                    if 1 <= n <= len(parts):
                        spread(parts, n - 1)
                    if n >= 2:
                        scale(parts, n - 2)
                normed[0] += len(parts)

            edges = sorted({a for a, _ in CHUNKS} | {REST, TILES})
            PIECES = list(zip(edges, edges[1:]))
            HEAD = edges.index(REST)
            piece_sums = x_ring[0][:, 0:2 * D * len(PIECES)].rearrange("p (k d n) -> p k d n", k=2, d=D)
            assert CHUNK <= REST

            def sum_chunk(kind, buf, chunk):
                for n, (a, b) in enumerate(PIECES):
                    if CHUNKS[chunk][0] <= a < CHUNKS[chunk][1]:
                        step(v.tensor_reduce(out=piece_sums[:, kind, :, n], in_=buf[:, a:b, :].rearrange(
                            "p t d -> p d t"), op=ALU.add, axis=AX.X))

            def batch_layer(stage, among=lambda n: ()):
                def take(q, s, bias):
                    v.wait_ge(lin_mm, stage * QUADS + q + 3)
                    v.tensor_tensor(buf_c[:, 4 * q:4 * q + 4, :], ps_o[s][:, 0, :].rearrange(
                        "p (t d) -> p t d", d=D), over_t(bias, 4), ALU.add).then_inc(lin_used, 1)

                for n in range(NC + 1):
                    work = list(among(n)) if n < NC else []
                    if n:
                        work += [lambda: sum_chunk(0, buf_c, n - 1),
                                 lambda: (v.wait_ge(squared, normed[0] + n), sum_chunk(1, buf_b, n - 1))]
                    for j in range(QUADS_C):
                        if n < NC:
                            q = QUADS_C * n + j
                            take(q, q % 2, bias_off[:, :] if n else bias_par[:, stage - 1, :])
                        if j and work:
                            work.pop(0)()
                    if n < NC:
                        v.wait_ge(lin_used, stage * QUADS + QUADS_C * (n + 1) + 2)
                    if n == 0:
                        a, b = CHUNKS[0]
                        link(v.tensor_reduce(out=sums[:, 0, 0:D], in_=buf_c[:, a:b, :].rearrange("p t d -> p d t"),
                                             op=ALU.add, axis=AX.X))
                        pe_does()
                        link(v.tensor_scalar(bn_mean[:, :], ps_first, 1.0 / (P * CHUNK), None, ALU.mult))
                        step(v.tensor_tensor(bias_off[:, :], bias_par[:, stage - 1, :], bn_mean[:, :],
                                             ALU.subtract))
                        step(v.tensor_tensor(buf_c[:, a:b], buf_c[:, a:b], over_t(bn_mean[:, :], b - a),
                                             ALU.subtract))
                        settle()
                    if n < NC:
                        v.sem_inc(centred, 1)
                normed[0] += NC
                settle()
                flat = piece_sums.rearrange("p k d n -> p (k d) n")
                step(v.tensor_reduce(out=sums[:, 0, :], in_=flat[:, :, 0:HEAD], op=ALU.add, axis=AX.X))
                step(v.tensor_reduce(out=sums[:, 1, :], in_=flat[:, :, HEAD:], op=ALU.add, axis=AX.X))
                settle()
                pe_does()
                link(v.tensor_scalar(stats[:, :, :], ps_small[:, 0:2 * D].rearrange("p (k d) -> p k d", k=2),
                                     1.0 / EDGES, None, ALU.mult))
                link(v.tensor_tensor(bn_mean[:, :], stats[:, 0, :], stats[:, 0, :], ALU.mult))
                link(v.tensor_tensor(bn_scale[:, :], stats[:, 1, :], bn_mean[:, :], ALU.subtract))
                v.sem_inc(root_ready, NC)
                v.wait_ge(rooted, normed[0])
                link(v.reciprocal(bn_scale[:, :], bn_scale[:, :]))
                link(v.tensor_tensor(bn_scale[:, :], bn_scale[:, :], bn_par[:, 2 * stage - 2, :], ALU.mult))
                link(v.tensor_tensor(bn_mean[:, :], stats[:, 0, :], bn_scale[:, :], ALU.mult))
                link(v.tensor_tensor(bn_mean[:, :], bn_par[:, 2 * stage - 1, :], bn_mean[:, :], ALU.subtract))

            def apply_norm(n):
                a, b = CHUNKS[n]

                def scaled_by():
                    link(v.tensor_tensor(buf_c[:, a:b], buf_c[:, a:b], over_t(scale_now, b - a), ALU.mult))

                def shifted():
                    link(v.tensor_tensor(buf_c[:, a:b], buf_c[:, a:b], over_t(shift_now, b - a), ALU.add))
                    v.sem_inc(scaled, 1)

                return scaled_by, shifted

            scale_now, shift_now = apply_par[:, 0, :], apply_par[:, 1, :]

            def keep_norm():
                step(v.tensor_copy(scale_now, bn_scale[:, :]))
                step(v.tensor_copy(shift_now, bn_mean[:, :]))
                settle()

            def add_carry(buf, came, ops, cols):
                if cols.stop - cols.start > RUN:
                    for d in range(D):
                        step(v.scalar_tensor_tensor(buf[:, cols, d], came[:, cols], carry[:, d:d + 1],
                                                    buf[:, cols, d], ops[0], ops[1]))
                    settle()
                else:
                    part = x_ring[0][:, 0:RUN * D].rearrange("p (t d) -> p t d", d=D)
                    link(v.tensor_tensor(part, over_t(carry[:, :], RUN), bcast(came[:, cols], D), ops[0]))
                    link(v.tensor_tensor(buf[:, cols], buf[:, cols], part, ops[1]))

            def scan_groups(buf, of, on, start, ops):
                for d in range(D):
                    step(v.tensor_tensor_scan(buf[:, :, d], on, of[:, :, d], start, op0=ops[0], op1=ops[1]))
                settle()

            def group_prefix(buf, run, of=None, largest=False, live_sums=False, then=None,
                             scanned=False, meanwhile=None):
                on, inside, came, start, ops = (
                    (goes_on_neg, whole_neg, from_prev_neg, -BIG, (ALU.add, ALU.max)) if largest else
                    (goes_on, whole, from_prev, 0.0, (ALU.mult, ALU.add)))
                if live_sums:
                    on, inside, came = live_goes, live_whole, live_from
                on = on[:, 0:buf.shape[1]]
                of = buf if of is None else of
                if not scanned:
                    scan_groups(buf, of, on, start, ops)
                link(v.memset(carry_t[:, 0:1], start))
                pe_does((lambda: then(slice(run, TILES))) if then and not live_sums and run < TILES
                        else meanwhile)
                link(v.tensor_tensor_scan(carry_t[:, 1:P + 1], inside[:, :], ps_small[0:D, :], start,
                                          op0=ops[0], op1=ops[1]))
                pe_does()
                link(v.tensor_copy(carry[:, :], ps_small[:, 0:D]))
                if live_sums:
                    for half in halves(run):
                        part = wide_c[:, half]
                        link(v.tensor_tensor(part, over_t(carry[:, :], half.stop - half.start),
                                             bcast(came[:, half], D), ALU.mult))
                        link(v.tensor_tensor(buf[:, half], buf[:, half], part, ALU.add))
                        then(half)
                    return
                add_carry(buf, came, ops, slice(0, run))
                if then:
                    then(slice(0, run))

            def tails_back(to, of, run):
                link(v.tensor_tensor(to[:, :, :], of[:, :, :], bcast(is_tail[:, :], D), ALU.mult))
                for d in range(D):
                    step(v.tensor_tensor_scan(to[:, ::-1, d], not_tail[:, ::-1], to[:, ::-1, d], 0.0,
                                              op0=ALU.mult, op1=ALU.add))
                settle()
                carry_back()
                add_carry(to, from_next, (ALU.mult, ALU.add), slice(TILES - run, TILES))

            def largest_back(to, of, run):
                for d in range(D):
                    step(v.tensor_tensor_scan(to[:, ::-1, d], not_tail_neg[:, ::-1], of[:, ::-1, d], -BIG,
                                              op0=ALU.add, op1=ALU.max))
                settle()
                link(v.memset(carry_t[:, P:P + 1], -BIG))
                pe_does()
                link(v.tensor_tensor_scan(carry_t[:, 0:P][:, ::-1], whole_next_neg[:, ::-1],
                                          ps_small[0:D, ::-1], -BIG, op0=ALU.add, op1=ALU.max))
                pe_does()
                link(v.tensor_copy(carry[:, :], ps_small[:, 0:D]))
                add_carry(to, from_next_neg, (ALU.add, ALU.max), slice(TILES - run, TILES))

            def bond_quad(q, s):
                for h in range(2):
                    t = q * 4 + 2 * h
                    done = STEPS * q + STEPS + 2 * h
                    v.wait_ge(bond_mm, q * 2 + h + 1)
                    v.tensor_tensor(prod[:, :, :].rearrange("p t (k i) -> p t k i", k=BOND),
                                    ps_u[h][:, :, :].rearrange("p t (k i) -> p t k i", k=BOND),
                                    bcast(rows[:, bass.ds(t, 2), 0:BOND], D), ALU.mult).then_inc(bond_step, 1)
                    v.wait_ge(bond_step, done + 1)
                    v.tensor_reduce(out=buf_c[:, bass.ds(t, 2), :],
                                    in_=prod[:, :, :].rearrange("p t (k i) -> p t i k", k=BOND),
                                    op=ALU.add, axis=AX.X).then_inc(bond_step, 1)
                    v.wait_ge(bond_step, done + 2)
                v.wait_ge(lin_mm, q + 3)
                v.tensor_tensor(quad(buf_c, q), quad(buf_c, q), ps_o[s][:, 0, :], ALU.add)\
                    .then_inc(bond_step, 1)
                v.wait_ge(bond_step, STEPS * q + 2 * STEPS)

            w, b = bond_in.rearrange("p (a f) -> p a f", a=1), bias_in.rearrange("p (a f) -> p a f", a=1)
            for n in range(PARTS):
                step(v.tensor_copy(bond_parts[:, n:n + 1, :], w))
                step(v.tensor_copy(bias_parts[:, n:n + 1, :], b))
                settle()
                if n + 1 < PARTS:
                    step(v.tensor_tensor(w, w, bond_parts[:, n:n + 1, :], ALU.subtract))
                    step(v.tensor_tensor(b, b, bias_parts[:, n:n + 1, :], ALU.subtract))
                    settle()
            v.wait_ge(zeros_stored, 16 * 8)

            def rest(n):
                a, b = CHUNKS[n]
                v.wait_ge(parts_first, n + 1)
                link(v.tensor_tensor(buf_c[:, a:b], buf_a[:, a:b], norm_parts[n % 2][:, :, 0], ALU.subtract))
                v.sem_inc(rest_made, 1)

            def third_parts(n):
                a, b = CHUNKS[n]
                v.wait_ge(parts_second, n + 1)
                link(v.tensor_tensor(norm_parts[n % 2][:, :, 2], buf_c[:, a:b], norm_parts[n % 2][:, :, 1],
                                     ALU.subtract))
                v.sem_inc(parts_made, 1)

            def scale_first(n):
                scale(NORM0, n)
                v.sem_inc(input_ready, 1)

            def list_live():
                step(v.tensor_copy(live_rows[:, :, LAST_AT], x_dst_rows[:, :, D]))
                step(v.tensor_scalar(own_tail[:, :], x_dst_rows[:, :, D], float(SLOTS), None, ALU.is_lt))
                settle()
                link(v.tensor_tensor(live[:, :], live[:, :], own_tail[:, :], ALU.mult))
                link(v.tensor_tensor_scan(own_tail[:, :], live[:, :], live[:, :], 0.0, op0=ALU.add, op1=ALU.max))
                link(v.tensor_copy(counts[:, 0:1], own_tail[:, TILES - 1:TILES]))
                pe_does()
                link(v.tensor_tensor(bn_mean[:, 0:1], ps_rank[:, 0:1], counts[:, 0:1], ALU.subtract))
                link(v.tensor_scalar(own_tail[:, :], own_tail[:, :], bn_mean[:, 0:1], float(NOWHERE),
                                     ALU.add, ALU.add))
                link(v.scalar_tensor_tensor(live_index[:, :], live[:, :], -float(NOWHERE), own_tail[:, :],
                                            ALU.mult, ALU.add))
                v.sem_inc(rows_listed, 1)
                link(v.tensor_scalar(bn_mean[:, 0:1], ps_rank[:, 1:2], float(P * NARROW), None, ALU.is_gt))
                link(v.tensor_scalar(bn_mean[:, 1:2], ps_rank[:, 2:3], 0.0, None, ALU.is_gt))
                link(v.tensor_tensor(wide_i[0:1, :], bn_mean[0:1, 0:1], bn_mean[0:1, 1:2], ALU.add))
                v.sem_inc(count_known, 1)

            for n in range(NC + 1):
                if n < NC:
                    v.wait_ge(got_dst[n], 16 * CHUNK)
                    centre(NORM0, n)
                if n == LISTED_IN:
                    v.wait_ge(got_dst[NC - 1], 16 * CHUNK)
                    list_live()
                stages = (lambda n: spread(NORM0, n), scale_first, rest, third_parts, lambda n: None)
                for stage, quads in zip(stages, ((0, 1), (2,), (3,), (4,), (5, 6))):
                    for j in quads:
                        q = QUADS_C * (n - 1) + j
                        if n:
                            bond_quad(q, q % 2)
                    if n < NC:
                        stage(n)
            normed[0] += NC
            v.sem_inc(lin_used, QUADS)
            v.wait_ge(h_stored, 16)

            def layers(vw):
                run, parts = ready_parts(vw)[-1].stop, len(ready_parts(vw))
                passes = [0]

                def as_live_arrive(take_half):
                    passes[0] += 1
                    for n, half in enumerate(halves(vw)):
                        v.wait_ge(got_live[n], 16 * (half.stop - half.start) * passes[0])
                        take_half(n, half)

                def norm_live(n, half):
                    parts = live_norm(vw)
                    centre(parts, n)
                    spread(parts, n)
                    scale(parts, n)
                    normed[0] += n * len(parts)
                    v.sem_inc(h_made, 1)

                def weigh_live(n, half):
                    link(v.tensor_tensor(wide_b[:, half], wide_b[:, half],
                                         bcast(live_weight[:, half], D), ALU.mult))

                def add_and_norm_live(n, half):
                    link(v.tensor_tensor(x_live[:, half], x_live[:, half], wide_b[:, half], ALU.add))
                    norm_live(n, half)

                live_weight = live_in.bitcast(FP32)[:, 1:1 + vw, WEIGHT_AT]

                def add_sums(cols):
                    link(v.tensor_tensor(buf_a[:, cols], x_src[:, cols], buf_c[:, cols], ALU.add))
                    v.sem_inc(state_made, 1)

                group_prefix(buf_c, run, then=add_sums)
                link(v.memset(x_live[:, 0:vw], 0.0))
                v.sem_inc(blanked, 1)
                tails_back(buf_b, buf_a, run)
                v.sem_inc(state_spread, 1)
                v.wait_ge(live_back, 16 * 4)
                before, here, after = (live_in[:, n:n + vw, TAIL_AT] for n in range(3))
                step(v.tensor_tensor(live_goes[:, 0:vw], here, before, ALU.is_equal))
                step(v.tensor_tensor(live[:, 0:vw], here, after, ALU.is_equal))
                settle()
                step(v.tensor_tensor_scan(live_from[:, 0:vw], live_goes[:, 0:vw], live_goes[:, 0:vw], 1.0,
                                          op0=ALU.mult, op1=ALU.mult))
                step(v.scalar_tensor_tensor(live_y[:, 0:vw], live[:, 0:vw], float(NOWHERE), here,
                                            ALU.mult, ALU.add))
                settle()
                v.sem_inc(y_listed, 1)
                link(v.tensor_copy(wide[:, :], live_from[:, vw - 1:vw].to_broadcast([P, D])))
                pe_does()
                link(v.tensor_copy(live_whole[:, :], ps_small[0:D, :]))

                v.wait_ge(state_kept, 1)
                v.wait_ge(state_stored, 16 * parts)
                layer_norm(slots_norm(x_state, buf_a, buf_c))
                as_live_arrive(norm_live)
                v.sem_inc(input_ready, 1)
                batch_layer(1)
                keep_norm()
                for n in range(2):
                    for part in apply_norm(n):
                        part()
                batch_layer(2, among=lambda n: apply_norm(n + 2) if n + 2 < NC else ())
                keep_norm()
                v.sem_inc(scaled, 1)
                lower = buf_c[:, :, 0:D // 2]
                link(v.tensor_tensor(lower, lower, scale_now[:, 0:D // 2].unsqueeze(1).to_broadcast(
                    [P, TILES, D // 2]), ALU.mult))
                link(v.tensor_tensor(lower, lower, shift_now[:, 0:D // 2].unsqueeze(1).to_broadcast(
                    [P, TILES, D // 2]), ALU.add))
                link(v.tensor_scalar(lower, lower, 0.0, None, ALU.max))
                v.wait_ge(relu_done, NC + D // 2)

                def add_state(cols):
                    link(v.tensor_tensor(x_state[:, cols], x_state[:, cols], buf_c[:, cols], ALU.add))
                    v.sem_inc(state_made, 1)

                group_prefix(buf_c, run, then=add_state)

                as_live_arrive(norm_live)
                for n, half in enumerate(halves(TILES)):
                    v.wait_ge(h_back[n], 32)
                    step(v.tensor_tensor(buf_c[:, half], buf_a[:, half], bcast(weight_s[:, half], D), ALU.mult))
                settle()
                group_prefix(buf_c, run, then=lambda cols: v.sem_inc(state_made, 1))
                for turn in range(2):
                    as_live_arrive(weigh_live)
                    group_prefix(wide_b[:, 0:vw], vw, live_sums=True, then=lambda half: v.sem_inc(y_made, 1))
                v.wait_ge(state_stored, 16 * 3 * parts)
                as_live_arrive(add_and_norm_live)
                v.wait_ge(y3_back, 16)
                link(v.tensor_tensor(x_state, x_state, buf_c, ALU.add))

                for n, half in enumerate(halves(TILES)):
                    v.wait_ge(h_back[n], 48)
                    link(v.tensor_scalar(buf_a[:, half], buf_a[:, half], 0.0, MSG_EPS, ALU.max, ALU.add))
                    link(v.tensor_scalar(buf_b[:, half], buf_a[:, half], beta_c[:, :], None, ALU.mult))
                group_prefix(buf_c, run, of=buf_b, largest=True)
                largest_back(buf_d, buf_c, run)
                for a, b in CHUNKS:
                    link(v.tensor_tensor(buf_b[:, a:b], buf_b[:, a:b], buf_d[:, a:b], ALU.subtract))
                    v.sem_inc(exp_ready, 1)
                for n, (a, b) in enumerate(CHUNKS):
                    v.wait_ge(exp_done, n + 1)
                    step(v.tensor_tensor(buf_a[:, a:b], buf_a[:, a:b], buf_b[:, a:b], ALU.mult))
                settle()
                group_prefix(buf_a, run, meanwhile=lambda: scan_groups(buf_b, buf_b, goes_on[:, :], 0.0,
                                                                       (ALU.mult, ALU.add)))
                group_prefix(buf_b, run, scanned=True)

                def divide(n):
                    a, b = (4 * q for q in LAST_CHUNKS[n])
                    link(v.tensor_scalar(buf_b[:, a:b], buf_b[:, a:b], 1e-30, None, ALU.max))
                    link(v.reciprocal(buf_b[:, a:b], buf_b[:, a:b]))
                    link(v.tensor_tensor(buf_a[:, a:b], buf_a[:, a:b], buf_b[:, a:b], ALU.mult))
                    v.sem_inc(input_ready, 1)

                def add_quad(q, s):
                    v.wait_ge(lin_mm, 3 * QUADS + q + 3)
                    v.tensor_tensor(quad(x_state, q), quad(x_state, q), ps_o[s][:, 0, :], ALU.add)\
                        .then_inc(lin_used, 1)

                divide(0)
                for n, quads in enumerate(LAST_CHUNKS):
                    if n + 1 < len(LAST_CHUNKS):
                        divide(n + 1)
                    for q in range(*quads):
                        add_quad(q, q % 2)
                small[0], steps[0], normed[0] = started

            started = (small[0], steps[0], normed[0])
            narrow_or_wide(v, layers)

        @block.tensor
        def _(pe):
            small = [0]

            def asked():
                small[0] += 1
                pe.wait_ge(to_pe, small[0])

            def turn_keys(keys):
                asked()
                pe.transpose(ps_t[0][:, 0, :], keys[:, 0:P], ident[:, :])
                pe.transpose(ps_t[0][:, 1, :], keys[:, P:2 * P], ident[:, :]).then_inc(from_pe, 1)

            def turn_wide(a):
                asked()
                pe.transpose(ps_small[0:D, :], a, ident[:, :]).then_inc(from_pe, 1)

            def turn_back(a):
                asked()
                pe.transpose(ps_small[:, 0:D], a, ident[0:D, 0:D]).then_inc(from_pe, 1)

            def group_carry(buf, last=TILES - 1):
                turn_wide(buf[:, last, :])
                turn_back(carry_t[:, 0:P])

            def tail_carry(buf):
                turn_wide(buf[:, 0, :])
                turn_back(carry_t[:, 1:P + 1])

            def over_edges():
                asked()
                pe.matmul(ps_small[:, 0:2 * D], ones[:, :], sums[:, 0, :], start=True, stop=False)
                pe.matmul(ps_small[:, 0:2 * D], ones_full[:, :], sums[:, 1, :], start=False, stop=True)\
                    .then_inc(from_pe, 1)

            def first_over_edges(turn_quad):
                def one(q, s):
                    if q == QUADS_C + 1:
                        asked()
                        pe.matmul(ps_first, ones[:, :], sums[:, 0, 0:D], start=True, stop=True).then_inc(from_pe, 1)
                    turn_quad(q, s)
                return one

            def turn(stage, *bufs):
                def one(q, s):
                    pe.wait_ge(copied, stage * QUADS + q + 1)
                    for n, buf in enumerate(bufs):
                        last = pe.transpose(ps_t[s][:, n, :], quad(buf, q), ident[:, :])
                    last.then_inc(turned, 1)
                return one

            def turn_chunks(stage, signal, before, starts):
                def one(q, s):
                    if q in starts:
                        pe.wait_ge(signal, before + starts.index(q) + 1)
                    turn(stage, buf_a)(q, s)
                return one

            def ready(stage, q):
                pe.wait_ge(copied, stage * QUADS + q + 3)
                if stage:
                    pe.wait_ge(lin_used, stage * QUADS + q + 1)

            def turn_parts(q, s):
                if q % QUADS_C == 0:
                    pe.wait_ge(parts_made, q // QUADS_C + 1)
                pe.wait_ge(copied, q + 1)
                for t in range(4):
                    parts = norm_parts[q // QUADS_C % 2][:, 4 * q % CHUNK + t].rearrange("p n j -> p (n j)")
                    last = pe.transpose(ps_parts[s][:, t * P:(t + 1) * P], parts, ident_half[:, :])
                last.then_inc(turned, 1)

            def bond_products(q, s):
                ready(0, q)
                for h in range(2):
                    pe.wait_ge(bond_step, STEPS * q + 1 + 2 * h)
                    for t in range(2):
                        norm = parts_t[s][:, (2 * h + t) * P:(2 * h + t + 1) * P]
                        for n in range(PARTS):
                            last = pe.matmul(ps_u[h][:, t, :], norm, bond_parts[:, n, :],
                                             start=n == 0, stop=n == PARTS - 1)
                    last.then_inc(bond_mm, 1)
                pe.wait_ge(bond_step, STEPS * q)
                for t in range(4):
                    norm = parts_t[s][:, t * P:(t + 1) * P]
                    for n in range(PARTS):
                        last = pe.matmul(ps_o[s][:, 0, D * t:D * t + D], norm, bias_parts[:, n, :],
                                         start=n + t == 0, stop=n + t == PARTS + 2)
                last.then_inc(lin_mm, 1)

            def pair_products(q, s):
                ready(1, q)
                pe.matmul(ps_o[s][:, 0, :], w_t[s][:, 0, :], w1s_bd[:, :], start=True, stop=False)
                pe.matmul(ps_o[s][:, 0, :], w_t[s][:, 1, :], w1d_bd[:, :], start=False, stop=True)\
                    .then_inc(lin_mm, 1)

            def second_products(q, s):
                ready(2, q)
                pe.matmul(ps_o[s][:, 0, :], w_t[s][:, 0, :], w2_bd[:, :], start=True, stop=True)\
                    .then_inc(lin_mm, 1)

            def mlp_products(q, s):
                ready(3, q)
                pe.wait_ge(hid_done, q + 1)
                for u in range(2):
                    r = slice(64 * u, 64 * u + 64)
                    last = pe.matmul(ps_u[s][:, u, 0:P], w3a_bd[r, :], w_t[s][r, 0, :], start=True, stop=True)
                last.then_inc(hid_mm, 1)
                pe.wait_ge(hid_done, q + 3)
                pe.matmul(ps_o[s][:, 0, :], ones[0:1, :], b3b_row[:, :], start=True, stop=False)
                for u in range(2):
                    last = pe.matmul(ps_o[s][:, 0, H2 * u:H2 * u + H2], r_t[s][:, u, :], w3b_bd[:, :],
                                     start=False, stop=u == 1)
                last.then_inc(lin_mm, 1)

            pe.sem_inc(lin_mm, 2)
            pe.sem_inc(hot_used, HOT)
            pe.wait_ge(ident_made, 8)
            for n in range(2 * PART_TURNS):
                turn_keys(key_turned[n])
            turn_wide(wide[:, :])
            turn_wide(wide[:, :])
            def count(t, s, start=False, stop=False):
                pe.wait_ge(hot_made, 2 * t + 2)
                for h in range(2):
                    last = pe.matmul(ps_o[h][:, :, :].rearrange("p a b -> p (a b)")[:, 0:LO_H], hot_hi[s][:, :],
                                     hot_lo[s][:, h * LO_H:(h + 1) * LO_H], start=start, stop=stop)
                last.then_inc(hot_used, 1)

            for j in range(HOT_LOOP):
                count(j, j % HOT, start=j == 0)
            with pe.Fori(1, TILES // HOT_LOOP - 1) as i:
                for j in range(HOT_LOOP):
                    count(i * HOT_LOOP + j, j % HOT)
            for j in range(HOT_LOOP):
                count(TILES - HOT_LOOP + j, j % HOT, stop=j == HOT_LOOP - 1)
            pe.wait_ge(hot_used, TILES + HOT)
            pe.sem_inc(counted, 1)
            asked()
            for h in range(2):
                part = cnt[:, h * LO_H:(h + 1) * LO_H]
                pe.matmul(ps_u[0][:, h, 0:LO_H], upper[:, :], part, start=True, stop=True)
                last = pe.matmul(ps_u[1][:, h, 0:LO_H], ones[:, :], part, start=True, stop=True)
            last.then_inc(from_pe, 1)
            asked()
            for b in range(-(-LOS // P)):
                w = min(P, LOS - b * P)
                last = pe.transpose(ps_t[b // 4][0:w, b % 4, :], run[:, b * P:b * P + w], ident[:, :])
            last.then_inc(from_pe, 1)
            pe.wait_ge(weights_in, 16 * len(weight_loads))
            asked()
            pe.matmul(ps_small[:, 0:D], rb3a_w[:, :], w3b_bd[0:H2, 0:D], start=True, stop=False)
            pe.matmul(ps_small[:, 0:D], ones[0:1, :], b3b_row[:, 0:D], start=False, stop=True).then_inc(from_pe, 1)
            turn_wide(wide[:, :])
            turn_back(carry_t[:, 1:P + 1])

            def count_then_turn(q, s):
                if q == LISTED_AT:
                    asked()
                    pe.matmul(ps_rank[:, 0:1], upper[:, :], counts[:, 0:1], start=True, stop=True)
                    pe.matmul(ps_rank[:, 1:3], ones[:, :], counts[:, :], start=True, stop=True)\
                        .then_inc(from_pe, 1)
                turn_parts(q, s)

            first_then_second(None, count_then_turn, bond_products)
            pe.wait_ge(count_known, 1)

            def layers(vw):
                group_carry(buf_c)
                tail_carry(buf_b)
                turn_wide(wide[:, :])
                pe.wait_ge(input_ready, NC + 1)

                def turn_as_loaded(q, s):
                    for half, back in zip(halves(TILES), h_back):
                        if q == half.start // 4:
                            pe.wait_ge(back, 16)
                    turn(1, buf_a, buf_b)(q, s)

                first_then_second(None, first_over_edges(turn_as_loaded), pair_products)
                over_edges()
                by_chunk = turn_chunks(2, relu_done, 0, [a // 4 for a, _ in CHUNKS])
                first_then_second(None, first_over_edges(by_chunk), second_products)
                over_edges()
                group_carry(buf_c)
                group_carry(buf_c)
                for _ in range(2):
                    group_carry(wide_b, vw - 1)
                group_carry(buf_c)
                tail_carry(buf_d)
                group_carry(buf_a)
                group_carry(buf_b)
                first_then_second(None, turn_chunks(3, input_ready, NC + 1,
                                                    [q for q, _ in LAST_CHUNKS]), mlp_products)
                small[0] = started

            started = small[0]
            narrow_or_wide(pe, layers)


def kernel(**inputs):
    import numpy as np
    import concourse.bacc as bacc
    from concourse import mybir as mb
    from concourse.bass_utils import run_bass_kernel_spmd as run

    a = {k: np.ascontiguousarray(v) for k, v in inputs.items()}
    a["L0_gnn_kernel"] = np.ascontiguousarray(a["L0_gnn_kernel"].reshape(16, 32, 32).transpose(2, 0, 1)
                                              .reshape(32, 512))
    a["L0_gnn_bias"] = np.ascontiguousarray(a["L0_gnn_bias"].reshape(32, 32).T)
    names = ["x", "src", "dst", "edge_attr_16", "edge_weight", "L0_gnn_kernel", "L0_gnn_bias",
             "L1_gnn_W1", "L1_gnn_b1", "L1_gnn_gamma1", "L1_gnn_beta1", "L1_gnn_W2", "L1_gnn_b2",
             "L1_gnn_gamma2", "L1_gnn_beta2", "L3_gnn_beta", "L3_gnn_W1", "L3_gnn_b1", "L3_gnn_W2", "L3_gnn_b2"]
    nc = bacc.Bacc("TRN2", target_bir_lowering=False, num_devices=1)
    arrays, args = {}, []
    for name in names:
        arrays[f"in_{name}"] = a[name]
        args.append(nc.dram_tensor(f"in_{name}", a[name].shape, mb.dt.from_np(a[name].dtype),
                                   kind="ExternalInput").ap())
    args.append(nc.dram_tensor("out_x", a["x"].shape, mb.dt.float32, kind="ExternalOutput").ap())
    gnn(nc, *args)
    return run(nc, [arrays], core_ids=[0]).results[0]["out_x"]
```
